# Optimizing a Trainium2 kernel written in Bass

```python
import numpy as np
import jax
import jax.numpy as jnp

def _softmax(x, axis=-1):
    return jax.nn.softmax(x, axis=axis)

def _gelu(x):
    return jax.nn.gelu(x, approximate=True)

def _silu(x):
    return jax.nn.silu(x)

def _sigmoid(x):
    return jax.nn.sigmoid(x)

def _layernorm(x, axis=-1, eps=1e-05):
    m = jnp.mean(x, axis=axis, keepdims=True)
    v = jnp.var(x, axis=axis, keepdims=True)
    return (x - m) / jnp.sqrt(v + eps)

def _scatter_add(tgt, idx, src, axis=0):
    return tgt.at[idx].add(src)

def _segment_sum(src, seg, n):
    return jax.ops.segment_sum(src, seg, n)
kernel_name = 'mk_flamingo_gated_d1_seqx_r4_a2100c'

def setup_inputs(seed: int=0):
    np.random.seed(seed)
    _w = jnp.asarray

    def _rec_inputs():
        import jax
        import jax.numpy as jnp
        _rk = jax.random.key(seed)
        x = 7.22e-05 + 1 * jax.random.normal(jax.random.fold_in(_rk, 1), (32, 128, 512), jnp.float32)
        _lenS = 128 - jax.random.randint(jax.random.fold_in(_rk, 7), (32,), 0, max(1, 128 // 4) + 1, jnp.int32)
        _lenS2 = 128 - jax.random.randint(jax.random.fold_in(_rk, 8), (32,), 0, max(1, 128 // 4) + 1, jnp.int32)
        _ctx_512P = jax.random.normal(jax.random.fold_in(_rk, 11), (32, 16, 128), jnp.float32)
        _ctx_512c = jax.random.dirichlet(jax.random.fold_in(_rk, 511), 0.3 * jnp.ones((16,), jnp.float32), (32, 128))
        _ctx_512t = jnp.einsum('bsk,bkd->bsd', _ctx_512c, _ctx_512P)
        _ctx_512t = _ctx_512t * jax.lax.rsqrt(jnp.mean(jnp.square(_ctx_512t)) + 1e-12) * 0.953939
        ctx_512 = -0.000514642 + 1.00011 * (_ctx_512t + 0.3 * jax.random.normal(jax.random.fold_in(_rk, 611), (32, 128, 128), jnp.float32))
        _g = jax.random.normal(jax.random.fold_in(_rk, 9001), (2, 1), jnp.float32)
        _g = jnp.sign(_g) * jnp.maximum(jnp.abs(_g), 1.0) + (_g == 0) * 1.0
        g_xattn = _g[0]
        g_ffn = _g[1]
        return (x, ctx_512, g_xattn, g_ffn)
    x, ctx_512, g_xattn, g_ffn = _rec_inputs()

    def _L0_xattn_setup():
        import jax, jax.numpy as jnp
        import numpy as np
        import math
        NUM_Q_HEADS = 32
        NUM_KV_HEADS = 8
        key = jax.random.key(seed)
        k1, k2, k3 = jax.random.split(key, 3)
        B, S, E = (2, 512, 512)
        kv_E = NUM_KV_HEADS * (E // NUM_Q_HEADS)
        q = jax.random.normal(k1, (B, S, E), dtype=jnp.float32)
        k = jax.random.normal(k2, (B, S, kv_E), dtype=jnp.float32)
        v = jax.random.normal(k3, (B, S, kv_E), dtype=jnp.float32)
        return {'q': q, 'k': k, 'v': v}
    _L0_xattn_all = _L0_xattn_setup()
    _L0_xattn_in = {k: v for k, v in _L0_xattn_all.items() if k in ()}
    del _L0_xattn_all

    def _L0_ffn_setup():
        import jax, jax.numpy as jnp
        import numpy as np
        H = 512
        I = 512
        E_ROUTED = 7
        NS = 1
        TOPK = 2
        TEMP = 1.0

        def _moe_forward(x, Wr, br, gate_bias, Wup, bup, Wgate, bgate, Wdown, bdown, Wsu, bsu, Wsg, bsg, Wsd, bsd):
            B, S, _ = x.shape
            xt = x.reshape(-1, H)
            N = xt.shape[0]
            gate = (xt @ Wr + br) / TEMP
            bias_gate = gate + gate_bias
            _, ids = jax.lax.top_k(bias_gate, TOPK)
            sel_logits = jnp.take_along_axis(gate, ids, axis=-1)
            masked = jnp.full_like(gate, -jnp.inf)
            masked = masked.at[jnp.arange(N)[:, None], ids].set(sel_logits)
            probs = jax.nn.softmax(masked, axis=-1)
            u = jnp.einsum('nh,ehi->eni', xt, Wup) + bup[:, None, :]
            g = jax.nn.silu(jnp.einsum('eni,eij->enj', u, Wgate) + bgate[:, None, :]) * u
            eo = jnp.einsum('enj,ejh->enh', g, Wdown) + bdown[:, None, :]
            out = jnp.einsum('ne,enh->nh', probs, eo)
            su = (xt @ Wsu + bsu).reshape(N, NS, I)
            sg = jax.nn.silu(su @ Wsg + bsg) * su
            so = (sg @ Wsd + bsd).sum(axis=1)
            out = out + so
            return out.reshape(B, S, H)
        key = jax.random.key(seed)
        ks = jax.random.split(key, 20)
        s = lambda fan_in: 1.0 / np.sqrt(fan_in)
        inp = {'x': jax.random.normal(ks[0], (4, 256, H), dtype=jnp.float32), 'Wr': jax.random.normal(ks[1], (H, E_ROUTED), jnp.float32) * s(H), 'br': jax.random.normal(ks[2], (E_ROUTED,), jnp.float32) * s(H), 'gate_bias': jnp.zeros((E_ROUTED,), jnp.float32), 'Wup': jax.random.normal(ks[3], (E_ROUTED, H, I), jnp.float32) * s(H), 'bup': jax.random.normal(ks[4], (E_ROUTED, I), jnp.float32) * s(H), 'Wgate': jax.random.normal(ks[5], (E_ROUTED, I, I), jnp.float32) * s(I), 'bgate': jax.random.normal(ks[6], (E_ROUTED, I), jnp.float32) * s(I), 'Wdown': jax.random.normal(ks[7], (E_ROUTED, I, H), jnp.float32) * s(I), 'bdown': jax.random.normal(ks[8], (E_ROUTED, H), jnp.float32) * s(I), 'Wsu': jax.random.normal(ks[9], (H, NS * I), jnp.float32) * s(H), 'bsu': jax.random.normal(ks[10], (NS * I,), jnp.float32) * s(H), 'Wsg': jax.random.normal(ks[11], (I, I), jnp.float32) * s(I), 'bsg': jax.random.normal(ks[12], (I,), jnp.float32) * s(I), 'Wsd': jax.random.normal(ks[13], (I, H), jnp.float32) * s(I), 'bsd': jax.random.normal(ks[14], (H,), jnp.float32) * s(I)}
        return inp
    _L0_ffn_all = _L0_ffn_setup()
    _L0_ffn_in = {k: v for k, v in _L0_ffn_all.items() if k in ('Wr', 'br', 'gate_bias', 'Wup', 'bup', 'Wgate', 'bgate', 'Wdown', 'bdown', 'Wsu', 'bsu', 'Wsg', 'bsg', 'Wsd', 'bsd')}
    del _L0_ffn_all
    return {'x': x, 'ctx_512': ctx_512, 'g_xattn': g_xattn, 'g_ffn': g_ffn, 'L0_ffn_Wr': _L0_ffn_in['Wr'], 'L0_ffn_br': _L0_ffn_in['br'], 'L0_ffn_gate_bias': _L0_ffn_in['gate_bias'], 'L0_ffn_Wup': _L0_ffn_in['Wup'], 'L0_ffn_bup': _L0_ffn_in['bup'], 'L0_ffn_Wgate': _L0_ffn_in['Wgate'], 'L0_ffn_bgate': _L0_ffn_in['bgate'], 'L0_ffn_Wdown': _L0_ffn_in['Wdown'], 'L0_ffn_bdown': _L0_ffn_in['bdown'], 'L0_ffn_Wsu': _L0_ffn_in['Wsu'], 'L0_ffn_bsu': _L0_ffn_in['bsu'], 'L0_ffn_Wsg': _L0_ffn_in['Wsg'], 'L0_ffn_bsg': _L0_ffn_in['bsg'], 'L0_ffn_Wsd': _L0_ffn_in['Wsd'], 'L0_ffn_bsd': _L0_ffn_in['bsd']}

def reference(x, ctx_512, g_xattn, g_ffn, L0_ffn_Wr, L0_ffn_br, L0_ffn_gate_bias, L0_ffn_Wup, L0_ffn_bup, L0_ffn_Wgate, L0_ffn_bgate, L0_ffn_Wdown, L0_ffn_bdown, L0_ffn_Wsu, L0_ffn_bsu, L0_ffn_Wsg, L0_ffn_bsg, L0_ffn_Wsd, L0_ffn_bsd):
    import jax
    import jax.numpy as jnp

    def _L0_xattn_ref(q, k, v):
        import jax, jax.numpy as jnp
        import numpy as np
        import math
        NUM_Q_HEADS = 32
        NUM_KV_HEADS = 8
        B, S, E = q.shape
        H, KV = (NUM_Q_HEADS, NUM_KV_HEADS)
        D = E // H
        G = H // KV
        scale = math.sqrt(D)
        qh = q.reshape(B, S, KV, G, D).transpose(0, 2, 3, 1, 4)
        kh = k.reshape(B, S, KV, D).transpose(0, 2, 1, 3)
        vh = v.reshape(B, S, KV, D).transpose(0, 2, 1, 3)
        scores = jnp.einsum('bkgsd,bktd->bkgst', qh, kh) / scale
        weights = jax.nn.softmax(scores, axis=-1)
        out = jnp.einsum('bkgst,bktd->bkgsd', weights, vh)
        return out.transpose(0, 3, 1, 2, 4).reshape(B, S, E)

    def _L0_ffn_ref(x, Wr, br, gate_bias, Wup, bup, Wgate, bgate, Wdown, bdown, Wsu, bsu, Wsg, bsg, Wsd, bsd):
        import jax, jax.numpy as jnp
        import numpy as np
        H = 512
        I = 512
        E_ROUTED = 7
        NS = 1
        TOPK = 2
        TEMP = 1.0

        def _moe_forward(x, Wr, br, gate_bias, Wup, bup, Wgate, bgate, Wdown, bdown, Wsu, bsu, Wsg, bsg, Wsd, bsd):
            B, S, _ = x.shape
            xt = x.reshape(-1, H)
            N = xt.shape[0]
            gate = (xt @ Wr + br) / TEMP
            bias_gate = gate + gate_bias
            _, ids = jax.lax.top_k(bias_gate, TOPK)
            sel_logits = jnp.take_along_axis(gate, ids, axis=-1)
            masked = jnp.full_like(gate, -jnp.inf)
            masked = masked.at[jnp.arange(N)[:, None], ids].set(sel_logits)
            probs = jax.nn.softmax(masked, axis=-1)
            u = jnp.einsum('nh,ehi->eni', xt, Wup) + bup[:, None, :]
            g = jax.nn.silu(jnp.einsum('eni,eij->enj', u, Wgate) + bgate[:, None, :]) * u
            eo = jnp.einsum('enj,ejh->enh', g, Wdown) + bdown[:, None, :]
            out = jnp.einsum('ne,enh->nh', probs, eo)
            su = (xt @ Wsu + bsu).reshape(N, NS, I)
            sg = jax.nn.silu(su @ Wsg + bsg) * su
            so = (sg @ Wsd + bsd).sum(axis=1)
            out = out + so
            return out.reshape(B, S, H)
        return _moe_forward(x, Wr, br, gate_bias, Wup, bup, Wgate, bgate, Wdown, bdown, Wsu, bsu, Wsg, bsg, Wsd, bsd)
    x = x + jnp.tanh(g_xattn[0]) * _L0_xattn_ref(_layernorm(x, axis=-1), ctx_512, ctx_512)
    x = x + jnp.tanh(g_ffn[0]) * _L0_ffn_ref(_layernorm(x, axis=-1), L0_ffn_Wr, L0_ffn_br, L0_ffn_gate_bias, L0_ffn_Wup, L0_ffn_bup, L0_ffn_Wgate, L0_ffn_bgate, L0_ffn_Wdown, L0_ffn_bdown, L0_ffn_Wsu, L0_ffn_bsu, L0_ffn_Wsg, L0_ffn_bsg, L0_ffn_Wsd, L0_ffn_bsd)
    return x

_drawn_inputs = setup_inputs


def setup_inputs(seed=0):
    import zlib

    import numpy as np

    out = dict(_drawn_inputs(seed))
    spreads = {'L0_ffn_gate_bias': (0.0, 0.1)}
    factors = {'L0_ffn_bup': 2.927, 'L0_ffn_bgate': 4.176, 'L0_ffn_bsg': 3.142}
    for name, (base, spread) in spreads.items():
        noise = np.random.default_rng([zlib.crc32(name.encode()), seed]).standard_normal(out[name].shape)
        drawn = base * np.exp(spread * noise) if base else spread * noise
        out[name] = jnp.asarray(drawn.astype(out[name].dtype))
    for name, factor in factors.items():
        out[name] = (out[name] * factor).astype(out[name].dtype)
    return out
```

```python
import concourse.bass as bass
from concourse import mybir
from contextlib import ExitStack
import numpy as np

F32 = mybir.dt.float32
F16 = mybir.dt.float16
I32 = mybir.dt.int32
ALU = mybir.AluOpType
ACT = mybir.ActivationFunctionType
AX = mybir.AxisListType

P = 128
NB = 32
HID = 512
KT = HID // P
CTX = 128
NH = 32
NKV = 8
D = HID // NH
UNITS = 4
HPU = NH // UNITS
BLK = NH // 2
E_R = 7
E_ALL = 8
TT = 256
EPS = 1e-5
WS = 64.0
BIG = 3.0e38

SLOT_TILES = NB * P * 2 // TT + E_R - 1
SH_TILES = NB * P // TT
SH_A = SH_TILES // 2
N_TILES = SLOT_TILES + SH_TILES
SH_B0 = SH_A + SLOT_TILES
R_COLS = SLOT_TILES * TT // P
COLS = N_TILES * TT // P
XC = 8


def need(eng, sem, value):
    if isinstance(value, int) and value <= 0:
        return
    eng.wait_ge(sem, value)


def program(nc, a, out):
    ctx = ExitStack()
    phase = ExitStack()
    with ctx:
        def sb(name, shape, dt, where=ctx):
            return where.enter_context(nc.sbuf_tensor(name, shape, dt))

        def sem(name):
            return ctx.enter_context(nc.semaphore(name))

        wsc = nc.dram_tensor("wsc", (E_ALL, 3, P, KT * 2 * HID), F16, kind="Internal").ap()
        xnd = nc.dram_tensor("xnd", (NB * P, 2 * HID), F16, kind="Internal").ap()
        idd = nc.dram_tensor("idd", (R_COLS * P, 1), F32, kind="Internal").ap()
        ysl = nc.dram_tensor("ysl", (COLS * P, HID), F32, kind="Internal").ap()

        X = sb("X", [P, NB, HID], F32)
        id16 = sb("id16", [P, P], F16)
        id32 = sb("id32", [P, P], F32)
        tri = sb("tri", [P, P], F16)
        one16 = sb("one16", [P, P], F16)
        gts = sb("gts", [P, 2], F32)
        tg = sb("tg", [P, 2], F32)
        st1 = sb("st1", [P, NB, 6], F32)
        mv1 = sb("mv1", [P, NB, 2], F32)
        ln = sb("ln", [P, 6, NB], F32)
        ln2 = sb("ln2", [P, 6, NB], F32)
        st2 = sb("st2", [P, NB, 6], F32)
        mv2 = sb("mv2", [P, NB, 2], F32)
        eps = sb("eps", [P, 1], F32)
        wr32 = sb("wr32", [P, KT, E_R], F32)
        wrs = sb("wrs", [P, 2, KT, E_R], F16)
        brb = sb("brb", [P, E_R], F32)
        gbb = sb("gbb", [P, E_R], F32)
        idx = sb("idx", [P, COLS], I32)
        pos = sb("pos", [P, 2, NB], I32)
        prb = sb("prb", [P, 2, NB], F32)
        etab = sb("etab", [P, N_TILES], I32)

        def sa(name, shape, dt):
            return sb(name, shape, dt, phase)

        C = sa("C", [P, NB, NKV * D], F32)
        xn32 = sa("xn32", [P, 2, HID], F32)
        qcat = sa("qcat", [P, 2, NH, 4, D], F16)
        kcat = sa("kcat", [P, 2, NKV, 2, 4, D], F16)
        vaug = sa("vaug", [P, 2, NKV, D + 1], F32)
        qT = sa("qT", [P, 2, BLK, P], F16)
        kT = sa("kT", [P, 2, NKV, P], F16)
        negm = sa("negm", [P, 2, UNITS, HPU], F16)
        Pt = sa("Pt", [P, 2, HPU, P], F32)
        rec = sa("rec", [P, 2, NH // 2], F32)
        att = sa("att", [P, 2, HID], F32)
        wst = sa("wst", [P, 2, 3, HID], F32)
        whl = sa("whl", [P, 2, 3, 2, HID], F16)
        xhl = sa("xhl", [P, 2, 2, HID], F16)
        xhT = sa("xhT", [P, 2, 2 * KT, P], F16)
        gate = sa("gate", [P, NB, 8], F32)
        bia = sa("bia", [P, NB, 8], F32)
        oh = sa("oh", [P, 2, NB, 8], F32)
        r1 = sa("r1", [P, NB, 8], F32)
        r2 = sa("r2", [P, NB, 8], F32)
        r3 = sa("r3", [P, NB, 8], F32)
        msum = sa("msum", [P, NB, 8], F16)
        mx = sa("mx", [P, NB], F32)
        rev8 = sa("rev8", [P, 8], F32)
        sel = sa("sel", [P, 2, NB], F32)
        ex = sa("ex", [P, 2, NB], F32)
        e8 = sa("e8", [P, 6, 8], F32)
        i8 = sa("i8", [P, 2, 8], I32)
        it = sa("it", [P, SLOT_TILES], F32)
        ef = sa("ef", [P, 2, SLOT_TILES], F32)
        tok = sa("tok", [P, NB], F32)
        idr = sa("idr", [R_COLS, P], F32)
        ex_i = sa("ex_i", [P, 2, NB], I32)
        phase.close()
        wb = sb("wb", [P, 2, 3, KT, 2, HID], F16)
        bb = sb("bb", [P, 2, 2, KT], F32)
        bd = sb("bd", [P, 2, HID], F32)
        xs = sb("xs", [P, 2, 2, 2 * HID], F16)
        xT = sb("xT", [P, 2, 2, KT, TT], F16)
        u32 = sb("u32", [P, 2, KT, TT], F32)
        uhl = sb("uhl", [P, 2, KT, TT], F16)
        sl = sb("sl", [P, KT, TT], F32)
        g32 = sb("g32", [P, KT, TT], F32)
        ghl = sb("ghl", [P, 2, KT, TT], F16)
        ixr = sb("ixr", [P, 2, 2], I32)
        yb = sb("yb", [P, 2, 2, HID], F32)
        yg = sb("yg", [P, 2, 3, HID], F32)
        ob = sb("ob", [P, 2, HID], F32)

        PS = [ctx.enter_context(nc.psum_tensor(f"PS{i}", [P, 2, 512], F32)) for i in range(4)]

        S = {}
        for n in ("ctx_in const_in wr_in id0 id_ready ones_ready vone tanh_done tg_free var1 std1 ln1_ready chain chainp "
                  "xn_ready kh_ready qh_ready k_split v_ready q_split tk_done tq0_done tq1_done kT_ready qT0_ready qT1_ready "
                  "m_done max_done t_done exp_done pv_done att_ready x1_ready rec_done st2_ready "
                  "w64_ready whi_ready wlo_ready "
                  "var2 std2 ln2_ready x2n_ready x2h_ready x2l_ready t2_done x2T_ready gate_done wrs_ready wrh_ready "
                  "rt_mask rt_cnt rt_sel rt_exp rt_pos rt_etab idz id_scat id_load idT idx_ready phaseC "
                  "xt_done xTa_ready xTv_ready l1_done l2_done l3_done u_ready uh_ready ul_ready s_ready g_ready gh_ready gl_ready y_ready "
                  "ix_ready cmb_done").split():
            S[n] = sem(n)
        x_in = [sem(f"x_in{c}") for c in range(XC)]
        w_in = [sem(f"w_in{j}") for j in range(2)]
        w_out = [sem(f"w_out{j}") for j in range(2)]
        x2_out = [sem(f"x2_out{j}") for j in range(2)]
        wl_in = [[sem(f"wl_in{l}{j}") for j in range(2)] for l in range(3)]
        bi_in = [sem(f"bi_in{j}") for j in range(2)]
        xs_in = [sem(f"xs_in{j}") for j in range(2)]
        y_out = [sem(f"y_out{j}") for j in range(2)]
        yg_in = [sem(f"yg_in{j}") for j in range(2)]
        ysh_in = [sem(f"ysh_in{j}") for j in range(2)]
        o_out = [sem(f"o_out{j}") for j in range(2)]
        block = ctx.enter_context(nc.Block())

        Mb, Tb = PS[0], PS[1]
        Rb = PS[2]
        Ob = PS[3]
        Rb16 = [Rb[:, j, :].bitcast(F16).rearrange("p (n c) -> p n c", c=P) for j in range(2)]
        Obv = [Ob[:, j, 0:(NH // 2) * (D + 1)].rearrange("p (h c) -> p h c", c=D + 1) for j in range(2)]
        LG = PS[0][:, 0, 0:NB * 8].rearrange("p (b e) -> p b e", e=8)

        def over_batches(eng, body):
            body(0, 0, True, False)
            body(0, 1, False, False)
            body(1, 0, False, False)
            with eng.Fori(1, NB // 2 - 1) as i:
                body(i, 1, False, False)
                body(i + 1, 0, False, False)
            body(NB // 2 - 1, 1, False, True)

        @block.sync
        def _(sp):
            xv = a["x"].rearrange("b p d -> p b d")
            n = NB // XC
            for c in range(XC):
                sp.dma_start(X[:, c * n:(c + 1) * n, :], xv[:, c * n:(c + 1) * n, :]).then_inc(x_in[c], 16)
                if c == 0:
                    sp.dma_start(C[:, :, :], a["ctx"].rearrange("b t d -> t b d")).then_inc(S["ctx_in"], 16)
                    sp.dma_start(gts[:, 0:1], a["g_xattn"].unsqueeze(0).to_broadcast([P, 1])).then_inc(S["const_in"], 16)
                    sp.dma_start(gts[:, 1:2], a["g_ffn"].unsqueeze(0).to_broadcast([P, 1])).then_inc(S["const_in"], 16)
                    sp.dma_start(brb[:, :], a["br"].unsqueeze(0).to_broadcast([P, E_R])).then_inc(S["const_in"], 16)
                    sp.dma_start(gbb[:, :], a["gbias"].unsqueeze(0).to_broadcast([P, E_R])).then_inc(S["const_in"], 16)
                    sp.dma_start(wr32[:, :, :], a["wr"].rearrange("(k p) e -> p k e", p=P)).then_inc(S["wr_in"], 16)

            def load_w(b, par):
                sp.dma_start(wst[:, par, :, :], a["wall"][b]).then_inc(w_in[par], 16)

            def store_w(half, par, last):
                b = 2 * half + par
                sp.wait_ge(S["wlo_ready"], b + 1)
                e, kt = (b // KT, b % KT)
                sp.dma_start(wsc[e].rearrange("l p (k r) -> p l k r", k=KT)[:, :, kt, :],
                             whl[:, par, :, :, :].rearrange("p l h c -> p l (h c)")).then_inc(w_out[par], 16)
                if not last:
                    load_w(b + 2, par)

            load_w(0, 0)
            load_w(1, 1)
            with sp.Fori(0, NB // KT - 1) as e:
                for j in range(KT):
                    sp.wait_ge(S["wlo_ready"], KT * e + j + 1)
                    sp.dma_start(wsc[e].rearrange("l p (k r) -> p l k r", k=KT)[:, :, j, :],
                                 whl[:, j % 2, :, :, :].rearrange("p l h c -> p l (h c)")).then_inc(w_out[j % 2], 16)
                    load_w(KT * e + j + 2, j % 2)
            for b in range(NB - KT, NB):
                store_w(b // 2, b % 2, b + 2 >= NB)

            def store_x2(i):
                for par in range(2):
                    b = 2 * i + par
                    sp.wait_ge(S["x2l_ready"], b + 1)
                    sp.wait_ge(S["x2h_ready"], b + 1)
                    sp.dma_start(xnd[bass.ds(b * P, P), :], xhl[:, par, :, :].rearrange("p h c -> p (h c)")).then_inc(x2_out[par], 16)
            with sp.Fori(0, NB // 2) as i:
                store_x2(i)
            sp.wait_ge(S["phaseC"], 1)
            for par in range(2):
                sp.wait_ge(w_out[par], 16 * (NB // 2))
            def expert(i):
                return sp.value_load(etab[0:1, bass.ds(i, 1)], min_val=0, max_val=E_ALL - 1)

            def load_layer(l, e, par):
                sp.dma_start(wb[:, par, l, :, :, :].rearrange("p k h c -> p (k h c)"),
                             wsc[bass.ds(e, 1), l].rearrange("o p r -> (o p) r")).then_inc(wl_in[l][par], 16)

            def load_bias(e, par):
                sp.dma_start(bb[:, par, :, :].rearrange("p l k -> p (l k)"),
                             a["bcol"][bass.ds(e, 1)].rearrange("o p r -> (o p) r")).then_inc(bi_in[par], 16)
                sp.dma_start(bd[:, par, :], a["bdown"][bass.ds(e, 1), :].to_broadcast([P, HID])).then_inc(bi_in[par], 16)

            def store_y(i, par):
                sp.wait_ge(S["y_ready"], 2 * i + 2)
                sp.dma_start(ysl[bass.ds(i * TT, TT), :].rearrange("(t p) c -> p t c", p=P), yb[:, par, :, :]).then_inc(y_out[par], 16)

            for i in range(2):
                e = expert(i)
                load_bias(e, i)
                for l in range(3):
                    load_layer(l, e, i)
            e = expert(2)
            sp.wait_ge(S["l1_done"], 2)
            load_layer(0, e, 0)

            def tile(i, par, more2, more3):
                if more2:
                    e2 = expert(i + 2)
                if more3:
                    e3 = expert(i + 3)
                if more2:
                    sp.wait_ge(S["l2_done"], 2 * i + 2)
                    load_layer(1, e2, par)
                if more3:
                    sp.wait_ge(S["l1_done"], 2 * i + 4)
                    load_layer(0, e3, 1 - par)
                if more2:
                    sp.wait_ge(S["l3_done"], 2 * i + 2)
                    load_layer(2, e2, par)
                store_y(i, par)
                if more2:
                    load_bias(e2, par)
            with sp.Fori(0, N_TILES // 2 - 2) as h:
                tile(2 * h, 0, True, True)
                tile(2 * h + 1, 1, True, True)
            for i in range(N_TILES - 4, N_TILES):
                tile(i, i % 2, i + 2 < N_TILES, i + 3 < N_TILES)
            for par in range(2):
                sp.wait_ge(y_out[par], 16 * (N_TILES // 2))

            def load_sh(b, base, par):
                sp.dma_start(yg[:, par, 2, :], ysl[bass.ds(base + b * P, P), :]).then_inc(ysh_in[par], 16)

            def put(b, par):
                sp.wait_ge(S["cmb_done"], b + 1)
                sp.dma_start(out[b].rearrange("p c -> p c") if isinstance(b, int) else out[bass.ds(b, 1)].rearrange("o p c -> (o p) c"),
                             ob[:, par, :]).then_inc(o_out[par], 16)
            load_sh(0, 0, 0)
            load_sh(1, 0, 1)
            half = NB // 2
            with sp.Fori(0, half // 2 - 1) as h:
                for par in range(2):
                    put(2 * h + par, par)
                    load_sh(2 * h + par + 2, 0, par)
            off = SH_B0 * TT - half * P
            for par in range(2):
                put(half - 2 + par, par)
                load_sh(half + par, off, par)
            with sp.Fori(half // 2, half - 1) as h:
                for par in range(2):
                    put(2 * h + par, par)
                    load_sh(2 * h + par + 2, off, par)
            for par in range(2):
                put(NB - 2 + par, par)
            for par in range(2):
                sp.wait_ge(o_out[par], 16 * (NB // 2))

        @block.gpsimd
        def _(g):
            cp = [0]

            def link(ins):
                cp[0] += 1
                ins.then_inc(S["chainp"], 1)
                g.wait_ge(S["chainp"], cp[0])
            g.memset(eps[:, :], EPS).then_inc(S["id_ready"], 1)
            link(g.memset(id32[:, :], 0.0))
            link(g.memset(one16[:, :], 1.0))
            g.affine_select(out=id32[:, :], in_=id32[:, :], compare_op=ALU.not_equal, fill=1.0, base=0,
                            pattern=[[-1, P]], channel_multiplier=1).then_inc(S["id_ready"], 1)
            g.wait_ge(S["id_ready"], 2)
            g.tensor_copy(id16[:, :], id32[:, :]).then_inc(S["id_ready"], 1)
            g.affine_select(out=tri[:, :], in_=one16[:, :], compare_op=ALU.is_gt, fill=0.0, base=0,
                            pattern=[[1, P]], channel_multiplier=-1).then_inc(S["id_ready"], 1)
            for par in range(2):
                g.memset(vaug[:, par, :, D:D + 1], 1.0).then_inc(S["vone"], 1)
                g.memset(qcat[:, par, :, 3, :], 0.0).then_inc(S["vone"], 1)
                g.memset(kcat[:, par, :, :, 3, :], 0.0).then_inc(S["vone"], 1)
            g.iota(tok[:, :], pattern=[[P, NB]], base=0, channel_multiplier=1, allow_small_or_imprecise_dtypes=True).then_inc(S["id_ready"], 1)
            g.iota(rev8[:, :], pattern=[[-1, 8]], base=8, channel_multiplier=0, allow_small_or_imprecise_dtypes=True).then_inc(S["id_ready"], 1)
            g.iota(it[:, :], pattern=[[1, SLOT_TILES]], base=0, channel_multiplier=0, allow_small_or_imprecise_dtypes=True).then_inc(S["id_ready"], 1)
            ca = SH_A * TT // P
            g.iota(idx[:, 0:ca], pattern=[[P, ca]], base=0, channel_multiplier=1).then_inc(S["idx_ready"], 1)
            g.iota(idx[:, COLS - ca:COLS], pattern=[[P, ca]], base=ca * P, channel_multiplier=1).then_inc(S["idx_ready"], 1)
            g.memset(etab[:, 0:SH_A], E_R).then_inc(S["idx_ready"], 1)
            g.memset(etab[:, SH_B0:N_TILES], E_R).then_inc(S["idx_ready"], 1)
            link(g.memset(idr[:, :], 0.0))
            g.dma_start(idd.rearrange("(c p) o -> c (p o)", p=P), idr[:, :]).then_inc(S["idz"], 16)

            def split_kq(half, par):
                b = 2 * half + par
                g.wait_ge(S["kh_ready"], b + 1)
                cv = C[:, bass.ds(b, 1), :].rearrange("p o (h d) -> p (o h) d", d=D)
                g.tensor_tensor(kcat[:, par, :, :, 1, :], cv.unsqueeze(2).to_broadcast([P, NKV, 2, D]),
                                kcat[:, par, :, :, 0, :], ALU.subtract).then_inc(S["k_split"], 1)
                need(g, S["pv_done"], UNITS * (b - 1))
                g.nop(nofuse=True)
                g.tensor_copy(vaug[:, par, :, 0:D], cv).then_inc(S["v_ready"], 1)
                g.wait_ge(S["qh_ready"], b + 1)
                g.wait_ge(S["xn_ready"], b + 1)
                g.tensor_tensor(qcat[:, par, :, 2, :], xn32[:, par, :].rearrange("p (h d) -> p h d", d=D),
                                qcat[:, par, :, 0, :], ALU.subtract).then_inc(S["q_split"], 1)

            def residual(half, par):
                b = 2 * half + par
                g.wait_ge(S["att_ready"], 2 * b + 2)
                xv = X[:, bass.ds(b, 1), :].rearrange("p o c -> p (o c)")
                g.tensor_tensor(xv, xv, att[:, par, :], ALU.add).then_inc(S["x1_ready"], 1)

            def weights_lo(half, par):
                b = 2 * half + par
                g.wait_ge(S["whi_ready"], b + 1)
                g.tensor_tensor(whl[:, par, :, 1, :], wst[:, par, :, :], whl[:, par, :, 0, :], ALU.subtract).then_inc(S["wlo_ready"], 1)

            g.wait_ge(S["ctx_in"], 16)
            g.wait_ge(S["ln1_ready"], 1)
            split_kq(0, 0)

            def body(half, par, first, last):
                if not last:
                    split_kq(*((half, 1) if par == 0 else (half + 1, 0)))
                weights_lo(half, par)
                if not first:
                    residual(*((half - 1, 1) if par == 0 else (half, 0)))
            over_batches(g, body)
            residual(NB // 2 - 1, 1)

            def low2(i, first):
                for par in range(2):
                    b = 2 * i + par
                    g.wait_ge(S["x2n_ready"], b + 1)
                    g.wait_ge(S["x2h_ready"], b + 1)
                    g.tensor_tensor(xhl[:, par, 1, :], xn32[:, par, :], xhl[:, par, 0, :], ALU.subtract).then_inc(S["x2l_ready"], 1)
            low2(0, True)
            with g.Fori(1, NB // 2) as i:
                low2(i, False)

            g.wait_ge(S["idz"], 16)
            g.wait_ge(S["rt_pos"], 1)
            g.wait_ge(S["id_ready"], 7)
            for b in range(NB):
                for k in range(2):
                    g.indirect_dma_start(out=idd, out_offset=bass.IndirectOffsetOnAxis(ap=ex_i[:, k, b:b + 1], axis=0),
                                         in_=tok[:, b:b + 1], in_offset=None).then_inc(S["id_scat"], 16)
            for par in range(2):
                g.wait_ge(x2_out[par], 16 * (NB // 2))
            g.wait_ge(S["id_scat"], 16 * 2 * NB)
            g.dma_start(idr[:, :], idd.rearrange("(c p) o -> c (p o)", p=P)).then_inc(S["id_load"], 16)
            g.wait_ge(S["idx_ready"], 5)
            g.wait_ge(S["phaseC"], 1)

            def gather(i, par):
                need(g, S["xt_done"], 2 * i - 2)
                g.nop(nofuse=True)
                g.tensor_copy(ixr[:, par, :], idx[:, bass.ds(2 * i, 2)]).then_inc(S["ix_ready"], 1)
                g.wait_ge(S["ix_ready"], i + 1)
                g.nop(nofuse=True)
                for t in range(2):
                    g.indirect_dma_start(out=xs[:, par, t, :], out_offset=None, in_=xnd,
                                         in_offset=bass.IndirectOffsetOnAxis(ap=ixr[:, par, t:t + 1], axis=0)).then_inc(xs_in[par], 16)

            def g_lo(i):
                for hf in range(2):
                    g.wait_ge(S["gh_ready"], 2 * i + hf + 1)
                    g.tensor_tensor(ghl[:, 1, 2 * hf:2 * hf + 2, :], g32[:, 2 * hf:2 * hf + 2, :],
                                    ghl[:, 0, 2 * hf:2 * hf + 2, :], ALU.subtract).then_inc(S["gl_ready"], 1)
            gather(0, 0)
            gather(1, 1)
            g_lo(0)
            gather(2, 0)
            with g.Fori(0, N_TILES // 2 - 2) as h:
                g_lo(2 * h + 1)
                gather(2 * h + 3, 1)
                g_lo(2 * h + 2)
                gather(2 * h + 4, 0)
            g_lo(N_TILES - 3)
            gather(N_TILES - 1, 1)
            g_lo(N_TILES - 2)
            g_lo(N_TILES - 1)

            for par in range(2):
                g.wait_ge(y_out[par], 16 * (N_TILES // 2))

            def fetch(b, par):
                g.nop(nofuse=True)
                g.tensor_copy(ixr[:, par, :].unsqueeze(2), pos[:, :, bass.ds(b, 1)]).then_inc(S["ix_ready"], 1)
                g.wait_ge(S["ix_ready"], N_TILES + b + 1)
                g.nop(nofuse=True)
                for k in range(2):
                    g.indirect_dma_start(out=yg[:, par, k, :], out_offset=None, in_=ysl,
                                         in_offset=bass.IndirectOffsetOnAxis(ap=ixr[:, par, k:k + 1], axis=0)).then_inc(yg_in[par], 16)
            fetch(0, 0)
            fetch(1, 1)
            with g.Fori(1, NB // 2) as h:
                for par in range(2):
                    g.wait_ge(S["cmb_done"], 2 * h + par - 1)
                    fetch(2 * h + par, par)




        @block.scalar
        def _(act):
            act.wait_ge(S["const_in"], 64)
            act.activation(tg[:, :], gts[:, :], ACT.Tanh).then_inc(S["tanh_done"], 1)
            act.wait_ge(S["id_ready"], 1)
            act.wait_ge(S["var1"], 1)
            act.activation(ln[:, 2, :], mv1[:, :, 1], ACT.Sqrt, bias=eps[:, 0:1]).then_inc(S["std1"], 1)
            act.wait_ge(S["ctx_in"], 16)
            act.wait_ge(S["ln1_ready"], 1)
            act.wait_ge(S["wrs_ready"], 1)
            act.activation(wrs[:, 0, :, :], wr32[:, :, :], ACT.Copy).then_inc(S["wrh_ready"], 1)

            def high(half, par):
                b = 2 * half + par
                need(act, S["tk_done"], b - 1)
                cv = C[:, bass.ds(b, 1), :].rearrange("p o (h d) -> p (o h) d", d=D)
                for dup in range(2):
                    ins = act.activation(kcat[:, par, :, dup, 0:3:2, :], cv.unsqueeze(2).to_broadcast([P, NKV, 2, D]), ACT.Copy)
                ins.then_inc(S["kh_ready"], 1)
                need(act, S["tq1_done"], b - 1)
                act.activation(qcat[:, par, :, 0:2, :], X[:, bass.ds(b, 1), :].rearrange("p o (h d) -> p (o h) d", d=D).unsqueeze(2).to_broadcast([P, NH, 2, D]),
                               ACT.Identity, bias=ln[:, 1, bass.ds(b, 1)], scale=ln[:, 0, bass.ds(b, 1)]).then_inc(S["qh_ready"], 1)

            def evac_q0(half, par):
                b = 2 * half + par
                act.wait_ge(S["tq0_done"], b + 1)
                act.activation(qT[:, par, 0:8, :], Rb16[1], ACT.Copy).then_inc(S["qT0_ready"], 1)

            def exps(half, par, u):
                n = UNITS * (2 * half + par) + u
                act.wait_ge(S["t_done"], n + 1)
                need(act, S["pv_done"], n - 1)
                act.activation(Pt[:, u % 2, :, :].rearrange("p (o h) s -> p o (h s)", o=2), Tb[:, :, :], ACT.Exp, scale=float(D) ** -0.5).then_inc(S["exp_done"], 1)

            def weights_hi(half, par):
                b = 2 * half + par
                act.wait_ge(S["w64_ready"], b + 1)
                if not (isinstance(b, int) and b < 2):
                    act.wait_ge(w_out[par], 16 * half)
                act.activation(whl[:, par, :, 0, :], wst[:, par, :, :], ACT.Copy).then_inc(S["whi_ready"], 1)

            high(0, 0)
            evac_q0(0, 0)

            def body(half, par, first, last):
                nx = (half, 1) if par == 0 else (half + 1, 0)
                if not last:
                    high(*nx)
                exps(half, par, 0)
                weights_hi(half, par)
                exps(half, par, 1)
                exps(half, par, 2)
                if not last:
                    evac_q0(*nx)
                exps(half, par, 3)
            over_batches(act, body)

            act.wait_ge(S["var2"], 1)
            act.activation(ln2[:, 2, :], mv2[:, :, 1], ACT.Sqrt, bias=eps[:, 0:1]).then_inc(S["std2"], 1)
            act.wait_ge(S["ln2_ready"], 1)

            def norm2(i, first):
                for par in range(2):
                    b = 2 * i + par
                    if not first:
                        act.wait_ge(S["t2_done"], b - 1)
                        act.wait_ge(x2_out[par], 16 * i)
                    act.activation(xhl[:, par, 0, :], X[:, bass.ds(b, 1), :].rearrange("p o c -> p (o c)"),
                                   ACT.Identity, bias=ln2[:, 1, bass.ds(b, 1)], scale=ln2[:, 0, bass.ds(b, 1)]).then_inc(S["x2h_ready"], 1)
            norm2(0, True)
            with act.Fori(1, NB // 2) as i:
                norm2(i, False)
            act.wait_ge(S["rt_sel"], 1)
            act.activation(ex[:, :, :], sel[:, :, :], ACT.Exp).then_inc(S["rt_exp"], 1)
            act.wait_ge(S["phaseC"], 1)

            def evac_x(i, par):
                act.wait_ge(S["xt_done"], 2 * i + 1)
                need(act, S["l1_done"], 2 * i - 2)
                act.activation(xT[:, par, :, :, 0:P], PS[3][:, 0, :].bitcast(F16).rearrange("p (h k c) -> p h k c", h=2, k=KT),
                               ACT.Copy).then_inc(S["xTa_ready"], 1)

            def up_out(i, par):
                for hf in range(2):
                    act.wait_ge(S["l1_done"], 2 * i + hf + 1)
                    if hf == 0:
                        act.wait_ge(bi_in[par], 32 * (i // 2 + 1) if isinstance(i, int) else i_half[0] * 32 + 32)
                        need(act, S["g_ready"], 2 * i - 2)
                    for m in range(2 * hf, 2 * hf + 2):
                        ins = act.activation(u32[:, par, m, :], PS[0][:, hf, bass.ds((m % 2) * TT, TT)], ACT.Identity,
                                             bias=bb[:, par, 0, m:m + 1], scale=1.0 / WS)
                    ins.then_inc(S["u_ready"], 2 // 2)

            def gate_out(i, par):
                for hf in range(2):
                    act.wait_ge(S["l2_done"], 2 * i + hf + 1)
                    need(act, S["g_ready"], 2 * i - 1 + hf)
                    for m in range(2 * hf, 2 * hf + 2):
                        ins = act.activation(sl[:, m, :], PS[1][:, hf, bass.ds((m % 2) * TT, TT)], ACT.Silu,
                                             bias=bb[:, par, 1, m:m + 1], scale=1.0 / WS)
                    ins.then_inc(S["s_ready"], 1)
            i_half = [0]
            evac_x(0, 0)
            up_out(0, 0)

            def tile(half, par, last):
                i = 2 * half + par
                if not last:
                    evac_x(i + 1, 1 - par)
                gate_out(i, par)
                if not last:
                    i_half[0] = half + par
                    up_out(i + 1, 1 - par)
            tile(0, 0, False)
            tile(0, 1, False)
            with act.Fori(1, N_TILES // 2 - 1) as h:
                tile(h, 0, False)
                tile(h, 1, False)
            tile(N_TILES // 2 - 1, 0, False)
            tile(N_TILES // 2 - 1, 1, True)

        @block.vector
        def _(v):
            cv = [0]

            def link(ins):
                cv[0] += 1
                ins.then_inc(S["chain"], 1)
                v.wait_ge(S["chain"], cv[0])

            n = NB // XC
            v.wait_ge(S["wr_in"], 16)
            v.tensor_scalar(wr32[:, :, :], wr32[:, :, :], WS, None, ALU.mult).then_inc(S["wrs_ready"], 1)
            for c in range(XC):
                v.wait_ge(x_in[c], 16)
                for b in range(c * n, (c + 1) * n):
                    ins = v.bn_stats(st1[:, b, :], X[:, b, :])
            link(ins)
            for b in range(NB):
                ins = v.bn_aggr(mv1[:, b, :], st1[:, b, :])
            ins.then_inc(S["var1"], 1)

            def rstd(mv, t):
                link(v.reciprocal(t[:, 3, :], t[:, 2, :]))
                link(v.tensor_scalar(t[:, 4, :], mv[:, :, 1], EPS, None, ALU.add))
                link(v.tensor_tensor(t[:, 4, :], t[:, 4, :], t[:, 3, :], ALU.mult))
                link(v.tensor_tensor(t[:, 4, :], t[:, 4, :], t[:, 3, :], ALU.mult))
                link(v.tensor_scalar(t[:, 4, :], t[:, 4, :], -0.5, 1.5, ALU.mult, ALU.add))
                link(v.tensor_tensor(t[:, 0, :], t[:, 4, :], t[:, 3, :], ALU.mult))
                return v.scalar_tensor_tensor(out=t[:, 1, :], in0=mv[:, :, 0], scalar=-1.0, in1=t[:, 0, :], op0=ALU.mult, op1=ALU.mult)
            v.wait_ge(S["std1"], 1)
            rstd(mv1, ln).then_inc(S["ln1_ready"], 1)
            v.wait_ge(S["ln1_ready"], 1)
            v.wait_ge(S["tanh_done"], 1)
            v.wait_ge(S["wrh_ready"], 1)
            v.tensor_tensor(wrs[:, 1, :, :], wr32[:, :, :], wrs[:, 0, :, :], ALU.subtract).then_inc(S["wrs_ready"], 1)

            def norm1(half, par):
                b = 2 * half + par
                need(v, S["q_split"], b - 1)
                v.tensor_scalar(xn32[:, par, :], X[:, bass.ds(b, 1), :].rearrange("p o c -> p (o c)"), ln[:, 0, bass.ds(b, 1)],
                                ln[:, 1, bass.ds(b, 1)], ALU.mult, ALU.add).then_inc(S["xn_ready"], 1)

            def evac_k(half, par):
                b = 2 * half + par
                v.wait_ge(S["tk_done"], b + 1)
                v.tensor_copy(kT[:, par, :, :], Rb16[0]).then_inc(S["kT_ready"], 1)

            def evac_q1(half, par):
                b = 2 * half + par
                v.wait_ge(S["tq1_done"], b + 1)
                v.tensor_copy(qT[:, par, 8:16, :], Rb16[0]).then_inc(S["qT1_ready"], 1)

            def maxes(half, par, u):
                k = UNITS * (2 * half + par) + u
                v.wait_ge(S["m_done"], k + 1)
                v.tensor_reduce(negm[:, par, u, :].rearrange("p (o j) -> p o j", o=2), Mb[:, :, :].rearrange("p o (j t) -> p o j t", t=CTX),
                                AX.X, ALU.max, negate=True).then_inc(S["max_done"], 1)

            def normalise(half, par, hf):
                b = 2 * half + par
                v.wait_ge(S["pv_done"], UNITS * b + 2 * hf + 2)
                v.reciprocal(rec[:, hf, :], Obv[hf][:, :, D]).then_inc(S["rec_done"], 1)
                v.wait_ge(S["rec_done"], 4 * b + 2 * hf + 1)
                v.tensor_scalar(rec[:, hf, :], rec[:, hf, :], tg[:, 0:1], None, ALU.mult).then_inc(S["rec_done"], 1)
                v.wait_ge(S["rec_done"], 4 * b + 2 * hf + 2)
                need(v, S["x1_ready"], b - 1)
                v.tensor_tensor(att[:, par, hf * 256:(hf + 1) * 256].rearrange("p (h d) -> p h d", d=D), Obv[hf][:, :, 0:D],
                                rec[:, hf, :].unsqueeze(2).to_broadcast([P, NH // 2, D]), ALU.mult).then_inc(S["att_ready"], 1)

            def stats2(half, par):
                b = 2 * half + par
                v.wait_ge(S["x1_ready"], b + 1)
                v.bn_stats(st2[:, bass.ds(b, 1), :].rearrange("p o c -> p (o c)"),
                           X[:, bass.ds(b, 1), :].rearrange("p o c -> p (o c)")).then_inc(S["st2_ready"], 1)

            def weights64(half, par):
                b = 2 * half + par
                v.wait_ge(w_in[par], 16 * (half + 1))
                v.tensor_scalar(wst[:, par, :, :], wst[:, par, :, :], WS, None, ALU.mult).then_inc(S["w64_ready"], 1)

            norm1(0, 0)
            evac_k(0, 0)
            evac_q1(0, 0)
            maxes(0, 0, 0)

            def body(half, par, first, last):
                nx = (half, 1) if par == 0 else (half + 1, 0)
                pv = (half - 1, 1) if par == 0 else (half, 0)
                if not last:
                    norm1(*nx)
                weights64(half, par)
                maxes(half, par, 1)
                if not first:
                    normalise(*pv, 1)
                maxes(half, par, 2)
                if not last:
                    evac_k(*nx)
                if not first:
                    stats2(*pv)
                maxes(half, par, 3)
                normalise(half, par, 0)
                if not last:
                    evac_q1(*nx)
                    maxes(*nx, 0)
            over_batches(v, body)
            normalise(NB // 2 - 1, 1, 1)
            stats2(NB // 2 - 1, 1)
            v.wait_ge(S["st2_ready"], NB)
            for b in range(NB):
                ins = v.bn_aggr(mv2[:, b, :], st2[:, b, :])
            ins.then_inc(S["var2"], 1)
            v.wait_ge(S["std2"], 1)
            v.wait_ge(S["var2"], 1)
            rstd(mv2, ln2).then_inc(S["ln2_ready"], 1)
            v.wait_ge(S["ln2_ready"], 1)

            def norm2(i, first):
                for par in range(2):
                    b = 2 * i + par
                    if not first:
                        v.wait_ge(S["x2l_ready"], b - 1)
                    v.tensor_scalar(xn32[:, par, :], X[:, bass.ds(b, 1), :].rearrange("p o c -> p (o c)"), ln2[:, 0, bass.ds(b, 1)],
                                    ln2[:, 1, bass.ds(b, 1)], ALU.mult, ALU.add).then_inc(S["x2n_ready"], 1)
                for par in range(2):
                    b = 2 * i + par
                    v.wait_ge(S["t2_done"], b + 1)
                    if not first:
                        v.wait_ge(S["gate_done"], b - 1)
                    v.tensor_copy(xhT[:, par, :, :], Rb16[par]).then_inc(S["x2T_ready"], 1)
            norm2(0, True)
            with v.Fori(1, NB // 2) as i:
                norm2(i, False)

            def over_b(ap):
                return ap.unsqueeze(1).to_broadcast([P, NB, ap.shape[-1]])

            def over_e(ap):
                return ap.unsqueeze(2).to_broadcast([P, NB, 8])

            v.wait_ge(S["gate_done"], NB)
            link(v.memset(gate[:, :, :], 0.0))
            link(v.memset(bia[:, :, :], -BIG))
            link(v.scalar_tensor_tensor(out=gate[:, :, 0:E_R], in0=LG[:, :, 0:E_R], scalar=1.0 / WS, in1=over_b(brb[:, :]),
                                        op0=ALU.mult, op1=ALU.add))
            link(v.tensor_tensor(bia[:, :, 0:E_R], gate[:, :, 0:E_R], over_b(gbb[:, :]), ALU.add))
            v.wait_ge(S["id_ready"], 7)
            for k in range(2):
                link(v.tensor_reduce(mx[:, :], bia[:, :, :], AX.X, ALU.max))
                link(v.tensor_tensor(r1[:, :, :], bia[:, :, :], over_e(mx[:, :]), ALU.is_equal))
                link(v.tensor_tensor(r1[:, :, :], r1[:, :, :], over_b(rev8[:, :]), ALU.mult))
                link(v.tensor_reduce(mx[:, :], r1[:, :, :], AX.X, ALU.max))
                link(v.tensor_tensor(oh[:, k, :, :], over_b(rev8[:, :]), over_e(mx[:, :]), ALU.is_equal))
                if k == 0:
                    link(v.scalar_tensor_tensor(out=bia[:, :, :], in0=oh[:, 0, :, :], scalar=-BIG, in1=bia[:, :, :], op0=ALU.mult, op1=ALU.add))
                link(v.tensor_tensor(r2[:, :, :], oh[:, k, :, :], gate[:, :, :], ALU.mult))
                link(v.tensor_reduce(sel[:, k, :], r2[:, :, :], AX.X, ALU.add))
            v.tensor_tensor(msum[:, :, :], oh[:, 0, :, :], oh[:, 1, :, :], ALU.add).then_inc(S["rt_mask"], 1)
            link(v.tensor_tensor(mx[:, :], sel[:, 0, :], sel[:, 1, :], ALU.max))
            v.tensor_tensor(sel[:, :, :], sel[:, :, :], mx[:, :].unsqueeze(1).to_broadcast([P, 2, NB]), ALU.subtract).then_inc(S["rt_sel"], 1)
            v.wait_ge(S["rt_exp"], 1)
            link(v.tensor_tensor(mx[:, :], ex[:, 0, :], ex[:, 1, :], ALU.add))
            link(v.reciprocal(mx[:, :], mx[:, :]))
            link(v.tensor_scalar(mx[:, :], mx[:, :], tg[:, 1:2], None, ALU.mult))
            link(v.tensor_tensor(prb[:, :, :], ex[:, :, :], mx[:, :].unsqueeze(1).to_broadcast([P, 2, NB]), ALU.mult))
            v.wait_ge(S["rt_cnt"], 2)
            CNT = PS[1][:, 1, 0:NB * 8].rearrange("p (b e) -> p b e", e=8)
            RNK = PS[1][:, 0, 0:NB * 8].rearrange("p (b e) -> p b e", e=8)
            link(v.tensor_copy(r1[:, :, :], CNT))
            src, dst, s = r1, r2, 1
            while s < NB:
                link(v.tensor_copy(dst[:, 0:s, :], src[:, 0:s, :]))
                link(v.tensor_tensor(dst[:, s:NB, :], src[:, s:NB, :], src[:, 0:NB - s, :], ALU.add))
                src, dst, s = dst, (r3 if dst is r2 else r2), 2 * s
            link(v.tensor_scalar(e8[:, 0, :], src[:, NB - 1, :], float(TT - 1), None, ALU.add))
            link(v.tensor_copy(i8[:, 0, :], e8[:, 0, :]))
            link(v.tensor_scalar(i8[:, 1, :], i8[:, 0, :], TT.bit_length() - 1, None, ALU.logical_shift_right))
            link(v.tensor_copy(e8[:, 1, :], i8[:, 1, :]))
            ends, nxt, s = 1, 2, 1
            while s < 8:
                link(v.tensor_copy(e8[:, nxt, 0:s], e8[:, ends, 0:s]))
                link(v.tensor_tensor(e8[:, nxt, s:8], e8[:, ends, s:8], e8[:, ends, 0:8 - s], ALU.add))
                ends, nxt, s = nxt, nxt + 1, 2 * s
            link(v.tensor_tensor(e8[:, 5, :], e8[:, ends, :], e8[:, 1, :], ALU.subtract))
            link(v.tensor_scalar(e8[:, 5, :], e8[:, 5, :], float(TT), None, ALU.mult))
            tot = dst
            link(v.tensor_tensor(tot[:, :, :], src[:, :, :], r1[:, :, :], ALU.subtract))
            link(v.tensor_tensor(tot[:, :, :], tot[:, :, :], over_b(e8[:, 5, :]), ALU.add))
            link(v.tensor_tensor(tot[:, :, :], tot[:, :, :], RNK, ALU.add))
            for k in range(2):
                link(v.tensor_tensor(r1[:, :, :], tot[:, :, :], oh[:, k, :, :], ALU.mult))
                link(v.tensor_reduce(sel[:, k, :], r1[:, :, :], AX.X, ALU.add))
            v.tensor_copy(ex_i[:, :, :], sel[:, :, :]).then_inc(S["rt_pos"], 1)
            link(v.tensor_scalar(sel[:, :, :], sel[:, :, :], float(SH_A * TT), None, ALU.add))
            link(v.tensor_copy(pos[:, :, :], sel[:, :, :]))
            link(v.memset(ef[:, 0, :], 0.0))
            for e in range(E_R):
                link(v.scalar_tensor_tensor(out=ef[:, (e + 1) % 2, :], in0=it[:, :], scalar=e8[:, ends, e:e + 1],
                                            in1=ef[:, e % 2, :], op0=ALU.is_ge, op1=ALU.add))
            link(v.tensor_scalar(ef[:, 0, :], ef[:, E_R % 2, :], float(E_R - 1), None, ALU.min))
            link(v.tensor_copy(etab[:, SH_A:SH_B0], ef[:, 0, :]))
            v.wait_ge(S["idT"], 1)
            v.tensor_copy(idx[:, SH_A * TT // P:COLS - (SH_TILES - SH_A) * TT // P], PS[0][:, 1, 0:R_COLS]).then_inc(S["idx_ready"], 1)
            v.wait_ge(S["idx_ready"], 5)
            v.memset(mx[:, :], 0.0).then_inc(S["phaseC"], 1)

            def evac_x(i, par):
                v.wait_ge(S["xt_done"], 2 * i + 2)
                need(v, S["l1_done"], 2 * i - 2)
                v.tensor_copy(xT[:, par, :, :, P:TT], PS[3][:, 1, :].bitcast(F16).rearrange("p (h k c) -> p h k c", h=2, k=KT)).then_inc(S["xTv_ready"], 1)

            def split_u(i, par):
                for hf in range(2):
                    ms = slice(2 * hf, 2 * hf + 2)
                    v.wait_ge(S["u_ready"], 2 * i + hf + 1)
                    need(v, S["l2_done"], 2 * i)
                    v.tensor_copy(uhl[:, 0, ms, :], u32[:, par, ms, :]).then_inc(S["uh_ready"], 1)
                    v.wait_ge(S["uh_ready"], 2 * i + hf + 1)
                    v.tensor_tensor(uhl[:, 1, ms, :], u32[:, par, ms, :], uhl[:, 0, ms, :], ALU.subtract).then_inc(S["ul_ready"], 1)

            def gating(i, par):
                for hf in range(2):
                    ms = slice(2 * hf, 2 * hf + 2)
                    v.wait_ge(S["s_ready"], 2 * i + hf + 1)
                    need(v, S["gl_ready"], 2 * i)
                    v.tensor_tensor(g32[:, ms, :], sl[:, ms, :], u32[:, par, ms, :], ALU.mult).then_inc(S["g_ready"], 1)
                    v.wait_ge(S["g_ready"], 2 * i + hf + 1)
                    need(v, S["l3_done"], 2 * i)
                    v.tensor_copy(ghl[:, 0, ms, :], g32[:, ms, :]).then_inc(S["gh_ready"], 1)

            def down_out(i, par, half):
                for t in range(2):
                    v.wait_ge(S["l3_done"], 2 * i + t + 1)
                    if t == 0 and not (isinstance(i, int) and i < 2):
                        v.wait_ge(y_out[par], 16 * half)
                    v.scalar_tensor_tensor(out=yb[:, par, t, :], in0=PS[2][:, t, :], scalar=1.0 / WS, in1=bd[:, par, :],
                                           op0=ALU.mult, op1=ALU.add).then_inc(S["y_ready"], 1)
            evac_x(0, 0)
            split_u(0, 0)

            def tile(half, par, last):
                i = 2 * half + par
                if not last:
                    evac_x(i + 1, 1 - par)
                gating(i, par)
                if not last:
                    split_u(i + 1, 1 - par)
                down_out(i, par, half)
            tile(0, 0, False)
            tile(0, 1, False)
            with v.Fori(1, N_TILES // 2 - 1) as h:
                tile(h, 0, False)
                tile(h, 1, False)
            tile(N_TILES // 2 - 1, 0, False)
            tile(N_TILES // 2 - 1, 1, True)

            def combine(h, first):
                for par in range(2):
                    b = 2 * h + par
                    xv = X[:, bass.ds(b, 1), :].rearrange("p o c -> p (o c)")
                    v.wait_ge(yg_in[par], 32 * h + 32)
                    v.scalar_tensor_tensor(out=xv, in0=yg[:, par, 0, :], scalar=prb[:, 0, bass.ds(b, 1)], in1=xv,
                                           op0=ALU.mult, op1=ALU.add).then_inc(S["rec_done"], 1)
                    v.wait_ge(S["rec_done"], 4 * NB + 2 * b + 1)
                    v.scalar_tensor_tensor(out=xv, in0=yg[:, par, 1, :], scalar=prb[:, 1, bass.ds(b, 1)], in1=xv,
                                           op0=ALU.mult, op1=ALU.add).then_inc(S["rec_done"], 1)
                    v.wait_ge(S["rec_done"], 4 * NB + 2 * b + 2)
                    v.wait_ge(ysh_in[par], 16 * h + 16)
                    if not first:
                        v.wait_ge(o_out[par], 16 * h)
                    v.scalar_tensor_tensor(out=ob[:, par, :], in0=yg[:, par, 2, :], scalar=tg[:, 1:2], in1=xv,
                                           op0=ALU.mult, op1=ALU.add).then_inc(S["cmb_done"], 1)
            combine(0, True)
            with v.Fori(1, NB // 2) as h:
                combine(h, False)

        @block.tensor
        def _(pe):
            pe.wait_ge(S["id_ready"], 4)
            pe.wait_ge(S["vone"], 6)

            def tr_k(half, par):
                b = 2 * half + par
                pe.wait_ge(S["k_split"], b + 1)
                need(pe, S["qT1_ready"], b)
                for kv in range(NKV):
                    ins = pe.transpose(Rb16[0][:, kv, :], kcat[:, par, kv, :, :, :].rearrange("p o r d -> p (o r d)"), id16[:, :])
                ins.then_inc(S["tk_done"], 1)

            def tr_q(half, par, part):
                b = 2 * half + par
                if part == 0:
                    pe.wait_ge(S["q_split"], b + 1)
                    need(pe, S["qT0_ready"], b)
                else:
                    pe.wait_ge(S["kT_ready"], b + 1)
                for j in range(BLK // 2):
                    blk = part * BLK // 2 + j
                    ins = pe.transpose(Rb16[1 - part][:, j, :], qcat[:, par, 2 * blk:2 * blk + 2, :, :].rearrange("p h r d -> p (h r d)"), id16[:, :])
                ins.then_inc(S["tq1_done"] if part else S["tq0_done"], 1)

            def scores_max(half, par, u):
                b = 2 * half + par
                if u == 0:
                    pe.wait_ge(S["kT_ready"], b + 1)
                    pe.wait_ge(S["qT0_ready"], b + 1)
                if u == 2:
                    pe.wait_ge(S["qT1_ready"], b + 1)
                need(pe, S["max_done"], UNITS * b + u)
                for j in range(HPU // 2):
                    for odd in range(2):
                        rows = slice(64 * odd, 64 * odd + 3 * D)
                        ins = pe.matmul(Mb[:, odd, j * P:(j + 1) * P], qT[rows, par, 4 * u + j, :], kT[rows, par, 2 * u + j // 2, :],
                                        start=True, stop=True)
                ins.then_inc(S["m_done"], 1)

            def scores_T(half, par, u):
                k = UNITS * (2 * half + par) + u
                pe.wait_ge(S["max_done"], k + 1)
                need(pe, S["exp_done"], k)
                for odd in range(2):
                    for j in range(HPU // 2):
                        m = negm[:, par, u, odd * 4 + j:odd * 4 + j + 1].to_broadcast([P, P])
                        pe.matmul(Tb[:, odd, j * P:(j + 1) * P], m, id16[:, :], start=(j == 0), stop=False, skip_group_check=True)
                for kv in range(2):
                    for odd in range(2):
                        rows = slice(64 * odd, 64 * odd + 3 * D)
                        ins = pe.matmul(Tb[:, odd, kv * 256:(kv + 1) * 256], kT[rows, par, 2 * u + kv, :],
                                        qT[rows, par, 4 * u + 2 * kv:4 * u + 2 * kv + 2, :].rearrange("p n c -> p (n c)"),
                                        start=False, stop=(kv == 1), skip_group_check=True)
                ins.then_inc(S["t_done"], 1)

            def outputs(half, par, u):
                b = 2 * half + par
                pe.wait_ge(S["exp_done"], UNITS * b + u + 1)
                if u == 0:
                    pe.wait_ge(S["v_ready"], b + 1)
                if u % 2 == 0:
                    need(pe, S["att_ready"], 2 * (b - 1) + u // 2 + 1)
                for j in range(HPU // 2):
                    for odd in range(2):
                        c = (u % 2) * HPU + 2 * j + odd
                        ins = pe.matmul(Ob[:, u // 2, c * (D + 1):(c + 1) * (D + 1)], Pt[:, u % 2, odd * 4 + j, :],
                                        vaug[:, par, 2 * u + j // 2, :], start=True, stop=True)
                ins.then_inc(S["pv_done"], 1)

            tr_k(0, 0)
            tr_q(0, 0, 0)
            tr_q(0, 0, 1)
            scores_max(0, 0, 0)

            def body(half, par, first, last):
                nx = (half, 1) if par == 0 else (half + 1, 0)
                pv = (half - 1, 1) if par == 0 else (half, 0)
                scores_max(half, par, 1)
                scores_T(half, par, 0)
                if not first:
                    outputs(*pv, 3)
                scores_max(half, par, 2)
                scores_T(half, par, 1)
                outputs(half, par, 0)
                if not last:
                    tr_k(*nx)
                    tr_q(*nx, 0)
                scores_max(half, par, 3)
                scores_T(half, par, 2)
                outputs(half, par, 1)
                if not last:
                    tr_q(*nx, 1)
                    scores_max(*nx, 0)
                scores_T(half, par, 3)
                outputs(half, par, 2)
            over_batches(pe, body)
            outputs(NB // 2 - 1, 1, 3)

            def gates(i, first):
                for par in range(2):
                    b = 2 * i + par
                    pe.wait_ge(S["x2l_ready"], b + 1)
                    if first:
                        pe.wait_ge(S["qT1_ready"], NB)
                        pe.wait_ge(S["qT0_ready"], NB)
                    else:
                        pe.wait_ge(S["x2T_ready"], b - 1)
                    for n in range(2 * KT):
                        ins = pe.transpose(Rb16[par][:, n, :], xhl[:, par, n // KT, (n % KT) * P:(n % KT + 1) * P], id16[:, :])
                    ins.then_inc(S["t2_done"], 1)
                for par in range(2):
                    b = 2 * i + par
                    pe.wait_ge(S["x2T_ready"], b + 1)
                    if first and par == 0:
                        pe.wait_ge(S["wrs_ready"], 2)
                        pe.wait_ge(S["max_done"], UNITS * NB)
                    terms = [(xh, wh, k) for xh, wh in ((0, 0), (0, 1), (1, 0)) for k in range(KT)]
                    for n, (xh, wh, k) in enumerate(terms):
                        ins = pe.matmul(PS[0][:, 0, bass.ds(b * 8, E_R)], xhT[:, par, xh * KT + k, :], wrs[:, wh, k, :],
                                        start=(n == 0), stop=(n == len(terms) - 1))
                    ins.then_inc(S["gate_done"], 1)
            gates(0, True)
            with pe.Fori(1, NB // 2) as i:
                gates(i, False)
            pe.wait_ge(S["rt_mask"], 1)
            pe.wait_ge(S["exp_done"], UNITS * NB)
            mv = msum[:, :, :].rearrange("p b e -> p (b e)")
            pe.matmul(PS[1][:, 0, 0:NB * 8], tri[:, :], mv, start=True, stop=True).then_inc(S["rt_cnt"], 1)
            pe.matmul(PS[1][:, 1, 0:NB * 8], one16[:, :], mv, start=True, stop=True).then_inc(S["rt_cnt"], 1)
            pe.wait_ge(S["id_load"], 16)
            pe.transpose(PS[0][:, 1, 0:R_COLS], idr[:, :], id32[0:R_COLS, 0:R_COLS]).then_inc(S["idT"], 1)
            pe.wait_ge(S["phaseC"], 1)

            def tr_x(i, par, half):
                pe.wait_ge(xs_in[par], 32 * (half + 1))
                for t in range(2):
                    need(pe, S["xTv_ready"] if t else S["xTa_ready"], i)
                    src = PS[3][:, t, :].bitcast(F16).rearrange("p (n c) -> p n c", c=P)
                    for n in range(2 * KT):
                        ins = pe.transpose(src[:, n, :], xs[:, par, t, n * P:(n + 1) * P], id16[:, :])
                    ins.then_inc(S["xt_done"], 1)

            TERMS = [(w, x, k) for w, x in ((0, 0), (0, 1), (1, 0)) for k in range(KT)]

            def feature_layer(l, bank, rhs, i, par, half, free, done):
                pe.wait_ge(wl_in[l][par], 16 * (half + 1))
                for hf in range(2):
                    need(pe, free, 2 * i - 1 + hf)
                    for m in range(2 * hf, 2 * hf + 2):
                        for n, (w, x, k) in enumerate(TERMS):
                            ins = pe.matmul(bank[:, hf, (m % 2) * TT:(m % 2 + 1) * TT], wb[:, par, l, k, w, m * P:(m + 1) * P],
                                            rhs(x, k), start=(n == 0), stop=(n == len(TERMS) - 1))
                    ins.then_inc(done, 1)

            def up(i, par, half):
                pe.wait_ge(S["xTa_ready"], i + 1)
                pe.wait_ge(S["xTv_ready"], i + 1)
                feature_layer(0, PS[0], lambda x, k: xT[:, par, x, k, :], i, par, half, S["u_ready"], S["l1_done"])

            def gate_l(i, par, half):
                pe.wait_ge(S["ul_ready"], 2 * i + 2)
                feature_layer(1, PS[1], lambda x, k: uhl[:, x, k, :], i, par, half, S["s_ready"], S["l2_done"])

            def down(i, par, half):
                pe.wait_ge(wl_in[2][par], 16 * (half + 1))
                pe.wait_ge(S["gl_ready"], 2 * i + 2)
                for t in range(2):
                    need(pe, S["y_ready"], 2 * i - 1 + t)
                    for n, (w, x, k) in enumerate(TERMS):
                        ins = pe.matmul(PS[2][:, t, :], ghl[:, x, k, t * P:(t + 1) * P], wb[:, par, 2, k, w, :],
                                        start=(n == 0), stop=(n == len(TERMS) - 1))
                    ins.then_inc(S["l3_done"], 1)

            tr_x(0, 0, 0)
            up(0, 0, 0)

            def tile(half, par, last):
                i = 2 * half + par
                if not last:
                    tr_x(i + 1, 1 - par, half + par)
                gate_l(i, par, half)
                if not last:
                    up(i + 1, 1 - par, half + par)
                down(i, par, half)
            tile(0, 0, False)
            tile(0, 1, False)
            with pe.Fori(1, N_TILES // 2 - 1) as h:
                tile(h, 0, False)
                tile(h, 1, False)
            tile(N_TILES // 2 - 1, 0, False)
            tile(N_TILES // 2 - 1, 1, True)


def kernel(x, ctx_512, g_xattn, g_ffn, L0_ffn_Wr, L0_ffn_br, L0_ffn_gate_bias, L0_ffn_Wup, L0_ffn_bup, L0_ffn_Wgate,
           L0_ffn_bgate, L0_ffn_Wdown, L0_ffn_bdown, L0_ffn_Wsu, L0_ffn_bsu, L0_ffn_Wsg, L0_ffn_bsg, L0_ffn_Wsd, L0_ffn_bsd):
    import concourse.bacc as _bacc
    from concourse import mybir as _mybir
    from concourse.bass_utils import run_bass_kernel_spmd as _run

    def joined(routed, shared):
        return np.concatenate([np.asarray(routed), np.asarray(shared)[None]], axis=0)

    layers = [joined(L0_ffn_Wup, L0_ffn_Wsu), joined(L0_ffn_Wgate, L0_ffn_Wsg), joined(L0_ffn_Wdown, L0_ffn_Wsd)]
    wall = np.stack([w.reshape(E_ALL * KT, P, HID) for w in layers], axis=2)
    cols = np.stack([joined(L0_ffn_bup, L0_ffn_bsu), joined(L0_ffn_bgate, L0_ffn_bsg)], axis=1)
    bcol = cols.reshape(E_ALL, 2 * KT, P).transpose(0, 2, 1)
    given = {
        "x": x, "ctx": ctx_512, "g_xattn": g_xattn, "g_ffn": g_ffn, "wr": L0_ffn_Wr, "br": L0_ffn_br, "gbias": L0_ffn_gate_bias,
        "wall": wall, "bcol": bcol, "bdown": joined(L0_ffn_bdown, L0_ffn_bsd),
    }
    nc = _bacc.Bacc("TRN2", target_bir_lowering=False, num_devices=1)
    arrays, args = {}, {}
    for name, value in given.items():
        v = np.ascontiguousarray(value)
        arrays[f"in_{name}"] = v
        args[name] = nc.dram_tensor(f"in_{name}", v.shape, _mybir.dt.from_np(v.dtype), kind="ExternalInput").ap()
    out = nc.dram_tensor("out_0", (NB, P, HID), _mybir.dt.float32, kind="ExternalOutput").ap()
    program(nc, args, out)
    r = _run(nc, [arrays], core_ids=[0])
    return r.results[0]["out_0"]
```

```python
import concourse.bass as bass
from concourse import mybir
from contextlib import ExitStack
import numpy as np

F32 = mybir.dt.float32
F16 = mybir.dt.float16
I32 = mybir.dt.int32
ALU = mybir.AluOpType
ACT = mybir.ActivationFunctionType
AX = mybir.AxisListType

P = 128
NB = 32
HID = 512
KT = HID // P
CTX = 128
NH = 32
NKV = 8
D = HID // NH
UNITS = 4
HPU = NH // UNITS
BLK = NH // 2
E_R = 7
E_ALL = 8
TT = 256
EPS = 1e-5
WS = 64.0
BIG = 3.0e38

SLOT_TILES = NB * P * 2 // TT + E_R - 1
SH_TILES = NB * P // TT
SH_A = SH_TILES // 2
N_TILES = SLOT_TILES + SH_TILES
SH_B0 = SH_A + SLOT_TILES
R_COLS = SLOT_TILES * TT // P
EARLY = NB * SH_A // SH_TILES
SB = 4
XC = 8


ROOTS = (1, 0)


def need(eng, sem, value):
    if isinstance(value, int) and value <= 0:
        return
    eng.wait_ge(sem, value)


def program(nc, a, out):
    ctx = ExitStack()
    phase = ExitStack()
    with ctx:
        def sb(name, shape, dt, where=ctx):
            return where.enter_context(nc.sbuf_tensor(name, shape, dt))

        def sem(name):
            return ctx.enter_context(nc.semaphore(name))

        wsc = nc.dram_tensor("wsc", (E_ALL, 3, P, KT * 2 * HID), F16, kind="Internal").ap()
        xnd = nc.dram_tensor("xnd", (NB * P, 2 * HID), F16, kind="Internal").ap()
        idd = nc.dram_tensor("idd", (R_COLS * P, 1), F32, kind="Internal").ap()
        ysl = nc.dram_tensor("ysl", (SH_B0 * TT, HID), F32, kind="Internal").ap()

        X = sb("X", [P, NB, HID], F32)
        id16 = sb("id16", [P, P], F16)
        id32 = sb("id32", [P, P], F32)
        tri = sb("tri", [P, P], F16)
        one16 = sb("one16", [P, P], F16)
        gts = sb("gts", [P, 2], F32)
        tg = sb("tg", [P, 2], F32)
        st1 = sb("st1", [P, NB, 6], F32)
        mv1 = sb("mv1", [P, NB, 2], F32)
        ln = sb("ln", [P, 6, NB], F32)
        ln2 = sb("ln2", [P, 6, NB], F32)
        st2 = sb("st2", [P, NB, 6], F32)
        mv2 = sb("mv2", [P, NB, 2], F32)
        eps = sb("eps", [P, 1], F32)
        wr32 = sb("wr32", [P, KT, E_R], F32)
        wrs = sb("wrs", [P, 2, KT, E_R], F16)
        brb = sb("brb", [P, E_R], F32)
        gbb = sb("gbb", [P, E_R], F32)
        idx = sb("idx", [P, R_COLS], I32)
        pos = sb("pos", [P, NB, 2], I32)
        prb = sb("prb", [P, 2, NB], F32)
        etab = sb("etab", [P, N_TILES], I32)
        chg = sb("chg", [P, N_TILES], I32)
        tok = sb("tok", [P, NB], F32)
        idr = sb("idr", [R_COLS, P], F32)
        rpos = sb("rpos", [P, NB, 2], I32)
        sct = sb("sct", [P, 2, SB, 2], I32)
        stk = sb("stk", [P, 2, SB], F32)

        def sa(name, shape, dt):
            return sb(name, shape, dt, phase)

        C = sa("C", [P, NB, NKV * D], F32)
        xn32 = sa("xn32", [P, 2, HID], F32)
        qcat = sa("qcat", [P, 2, NH, 4, D], F16)
        kcat = sa("kcat", [P, 2, NKV, 2, 4, D], F16)
        qT = sa("qT", [P, 2, BLK, P], F16)
        kT = sa("kT", [P, 2, NKV, P], F16)
        negm = sa("negm", [P, 2, UNITS, HPU], F16)
        Pt = sa("Pt", [P, 2, HPU, P], F32)
        Ps = sa("Ps", [P, 2, 2, HPU, P], F16)
        rec = sa("rec", [P, 2, NH // 2], F32)
        att = sa("att", [P, 2, HID], F32)
        wst = sa("wst", [P, 2, 3, HID], F32)
        whl = sa("whl", [P, 2, 3, 2, HID], F16)
        x2n = sa("x2n", [P, 4, HID], F32)
        xhl = sa("xhl", [P, 4, 2, HID], F16)
        xhT = sa("xhT", [P, 2, 2 * KT, P], F16)
        gate = sa("gate", [P, NB, 8], F32)
        bia = sa("bia", [P, NB, 8], F32)
        oh = sa("oh", [P, 2, NB, 8], F32)
        r1 = sa("r1", [P, NB, 8], F32)
        r2 = sa("r2", [P, NB, 8], F32)
        r3 = sa("r3", [P, NB, 8], F32)
        msum = sa("msum", [P, NB, 8], F16)
        mx = sa("mx", [P, NB], F32)
        rev8 = sa("rev8", [P, 8], F32)
        sel = sa("sel", [P, 2, NB], F32)
        ex = sa("ex", [P, 2, NB], F32)
        e8 = sa("e8", [P, 6, 8], F32)
        i8 = sa("i8", [P, 2, 8], I32)
        it = sa("it", [P, SLOT_TILES], F32)
        ef = sa("ef", [P, 2, SLOT_TILES], F32)
        phase.close()
        wb = sb("wb", [P, 2, 3, KT, 2, HID], F16)
        bb = sb("bb", [P, 2, 2, KT], F32)
        bd = sb("bd", [P, 2, HID], F32)
        xs = sb("xs", [P, 2, 2, 2 * HID], F16)
        xT = sb("xT", [P, 2, 2, KT, TT], F16)
        u32 = sb("u32", [P, 2, KT, TT], F32)
        uhl = sb("uhl", [P, 2, KT, TT], F16)
        sl = sb("sl", [P, KT, TT], F32)
        g32 = sb("g32", [P, KT, TT], F32)
        ghl = sb("ghl", [P, 2, KT, TT], F16)
        ixr = sb("ixr", [P, 2, 2], I32)
        ixf = sb("ixf", [P, 4, 2], I32)
        yb = sb("yb", [P, 2, 2, HID], F32)
        yg = sb("yg", [P, 4, 2, HID], F32)
        ys = sb("ys", [P, 2, HID], F32)
        ob = sb("ob", [P, 4, HID], F32)

        PS = [ctx.enter_context(nc.psum_tensor(f"PS{i}", [P, 2, 512], F32)) for i in range(4)]

        S = {}
        for n in ("const_in wr_in id0 id_ready ones_ready vone tanh_done tg_free var1 std1 ln1_ready chain chainp "
                  "xn_ready kh_ready qh_ready k_split v_ready q_split tk_done tq0_done tq1_done kT_ready qT0_ready qT1_ready "
                  "plo_g plo_v m_done max_done t_done exp_done pv_done att_ready x1_ready rec_done st2_ready "
                  "w64_ready whi_ready wlo_ready "
                  "var2 std2 ln2_ready x2n_ready x2h_ready x2l_ready t2_done x2T_ready gate_done wrs_ready wrh_ready "
                  "rt_mask rt_cnt rt_sel rt_exp rt_pos rt_etab idz id_scat id_load idT idx_ready phaseC "
                  "xt_done xTa_ready xTv_ready l1_done l2_done l3_done u_ready uh_ready ul_ready s_ready g_ready gh_ready gl_ready y_ready "
                  "ix_ready sct_ready cx").split():
            S[n] = sem(n)
        x_in = [sem(f"x_in{c}") for c in range(XC)]
        c_in = [sem(f"c_in{c}") for c in range(2)]
        w_in = [sem(f"w_in{j}") for j in range(2)]
        w_out = [sem(f"w_out{j}") for j in range(2)]
        x2_out = [sem(f"x2_out{j}") for j in range(4)]
        wl_in = [[sem(f"wl_in{l}{j}") for j in range(2)] for l in range(3)]
        bi_in = [sem(f"bi_in{j}") for j in range(2)]
        xs_in = [sem(f"xs_in{j}") for j in range(2)]
        xg_in = [sem(f"xg_in{j}") for j in range(2)]
        y_out = [sem(f"y_out{j}") for j in range(2)]
        scat = [sem(f"scat{j}") for j in range(2)]
        yg_in = [sem(f"yg_in{j}") for j in range(4)]
        ys_in = [sem(f"ys_in{j}") for j in range(2)]
        cmb = [sem(f"cmb{j}") for j in range(4)]
        o_out = [sem(f"o_out{j}") for j in range(4)]
        block = ctx.enter_context(nc.Block())

        Mb, Tb = PS[0], PS[1]
        Rb = PS[2]
        Ob = PS[3]
        Rb16 = [Rb[:, j, :].bitcast(F16).rearrange("p (n c) -> p n c", c=P) for j in range(2)]
        Obv = [Ob[:, j, 0:(NH // 2) * (D + 1)].rearrange("p (h c) -> p h c", c=D + 1) for j in range(2)]
        LG = PS[0][:, 0, 0:NB * 8].rearrange("p (b e) -> p b e", e=8)

        def over_batches(eng, body):
            body(0, 0, True, False)
            body(0, 1, False, False)
            body(1, 0, False, False)
            with eng.Fori(1, NB // 2 - 1) as i:
                body(i, 1, False, False)
                body(i + 1, 0, False, False)
            body(NB // 2 - 1, 1, False, True)

        def loads(half):
            if isinstance(half, int):
                return min(max(1, half - SH_A // 2 + 2), SLOT_TILES // 2 + 2)
            return half - SH_A // 2 + 2

        def tokens(half, shared=None):
            if shared is None:
                shared = not SH_A // 2 <= half < SH_B0 // 2
            if not shared:
                return xg_in, 32 * (half - SH_A // 2 + 1)
            late = isinstance(half, int) and half < SH_A // 2 or shared == "early"
            return xs_in, 32 * (half + 1 if late else half - SLOT_TILES // 2 + 1)

        def over_tiles(tile):
            first, second = SH_A // 2, SH_B0 // 2
            peeled = [0], [first - 1], [second - 1, second], [N_TILES // 2 - 1]
            loops = [(lambda h: 1, lambda h: tokens(h, "early")), (loads, lambda h: tokens(h, False)),
                     (lambda h: loads(N_TILES), lambda h: tokens(h, "late"))]
            for n, halves in enumerate(peeled):
                for half in halves:
                    for par in range(2):
                        tile(half, par, loads, tokens)
                if n < 3:
                    yield halves[-1] + 1, peeled[n + 1][0], *loops[n]

        @block.sync
        def _(sp):
            def load_w(b, par):
                sp.dma_start(wst[:, par, :, :], a["wall"][b]).then_inc(w_in[par], 16)

            xv = a["x"].rearrange("b p d -> p b d")
            n = NB // XC
            for c in range(XC):
                sp.dma_start(X[:, c * n:(c + 1) * n, :], xv[:, c * n:(c + 1) * n, :]).then_inc(x_in[c], 16)
                if c < 2:
                    cs = slice(0, n) if c == 0 else slice(n, NB)
                    sp.dma_start(C[:, cs, :], a["ctx"].rearrange("b t d -> t b d")[:, cs, :]).then_inc(c_in[c], 16)
                if c == 0:
                    load_w(0, 0)
                    load_w(1, 1)
                    sp.dma_start(gts[:, 0:1], a["g_xattn"].unsqueeze(0).to_broadcast([P, 1])).then_inc(S["const_in"], 16)
                    sp.dma_start(gts[:, 1:2], a["g_ffn"].unsqueeze(0).to_broadcast([P, 1])).then_inc(S["const_in"], 16)
                    sp.dma_start(brb[:, :], a["br"].unsqueeze(0).to_broadcast([P, E_R])).then_inc(S["const_in"], 16)
                    sp.dma_start(gbb[:, :], a["gbias"].unsqueeze(0).to_broadcast([P, E_R])).then_inc(S["const_in"], 16)
                    sp.dma_start(wr32[:, :, :], a["wr"].rearrange("(k p) e -> p k e", p=P)).then_inc(S["wr_in"], 16)

            def store_w(half, par, last):
                b = 2 * half + par
                sp.wait_ge(S["wlo_ready"], b + 1)
                e, kt = (b // KT, b % KT)
                sp.dma_start(wsc[e].rearrange("l p (k r) -> p l k r", k=KT)[:, :, kt, :],
                             whl[:, par, :, :, :].rearrange("p l h c -> p l (h c)")).then_inc(w_out[par], 16)
                if not last:
                    load_w(b + 2, par)

            with sp.Fori(0, NB // KT - 1) as e:
                for j in range(KT):
                    sp.wait_ge(S["wlo_ready"], KT * e + j + 1)
                    sp.dma_start(wsc[e].rearrange("l p (k r) -> p l k r", k=KT)[:, :, j, :],
                                 whl[:, j % 2, :, :, :].rearrange("p l h c -> p l (h c)")).then_inc(w_out[j % 2], 16)
                    load_w(KT * e + j + 2, j % 2)
            for b in range(NB - KT, NB):
                store_w(b // 2, b % 2, b + 2 >= NB)

            with sp.Fori(0, NB // 4) as i:
                for r in range(4):
                    sp.wait_ge(S["x2l_ready"], 4 * i + r + 1)
                    sp.dma_start(xnd[bass.ds((4 * i + r) * P, P), :], xhl[:, r, :, :].rearrange("p h c -> p (h c)")).then_inc(x2_out[r], 16)
            for j in range(4):
                sp.wait_ge(x2_out[j], 16 * (NB // 4))
            sp.wait_ge(S["phaseC"], 1)
            for par in range(2):
                sp.wait_ge(w_out[par], 16 * (NB // 2))
            def expert(i):
                return sp.value_load(etab[0:1, bass.ds(i, 1)], min_val=0, max_val=E_ALL - 1)

            def other(i):
                return {"cond": sp.value_load(chg[0:1, bass.ds(i, 1)], min_val=0, max_val=1)}

            def load_layer(l, e, par, cond):
                sp.dma_start(wb[:, par, l, :, :, :].rearrange("p k h c -> p (k h c)"),
                             wsc[bass.ds(e, 1), l].rearrange("o p r -> (o p) r"), **cond).then_inc(wl_in[l][par], 16)

            def load_bias(e, par, cond):
                sp.dma_start(bb[:, par, :, :].rearrange("p l k -> p (l k)"),
                             a["bcol"][bass.ds(e, 1)].rearrange("o p r -> (o p) r"), **cond).then_inc(bi_in[par], 16)
                sp.dma_start(bd[:, par, :], a["bdown"][bass.ds(e, 1), :].to_broadcast([P, HID]), **cond).then_inc(bi_in[par], 16)

            def store_y(i, par):
                sp.wait_ge(S["y_ready"], 2 * i + 2)
                sp.dma_start(ysl[bass.ds(i * TT, TT), :].rearrange("(t p) c -> p t c", p=P), yb[:, par, :, :]).then_inc(y_out[par], 16)

            def load_x(i, par, b):
                need(sp, S["xt_done"], 2 * i - 2)
                for t in range(2):
                    sp.dma_start(xs[:, par, t, :], xnd[bass.ds((b + t) * P, P), :]).then_inc(xs_in[par], 16)

            always = {}
            for i in range(2):
                load_x(i, i, 2 * i)
                for l in range(3):
                    load_layer(l, E_R, i, always)
                    if l == 0:
                        load_bias(E_R, i, always)

            with sp.Fori(0, SH_A // 2 - 1) as h:
                for par in range(2):
                    load_x(2 * h + par + 2, par, 4 * h + 2 * par + 4)
                    store_y(2 * h + par, par)

            def turn(i, par, cond2, cond3, xb=None):
                e2 = expert(i + 2)
                k2 = cond2(i + 2)
                if cond3 is not None:
                    e3 = expert(i + 3)
                    k3 = cond3(i + 3)
                sp.wait_ge(S["l2_done"], 2 * i + 2)
                load_layer(1, e2, par, k2)
                if xb is not None:
                    load_x(i + 2, par, xb)
                if cond3 is not None:
                    sp.wait_ge(S["l1_done"], 2 * i + 4)
                    load_layer(0, e3, 1 - par, k3)
                sp.wait_ge(S["l3_done"], 2 * i + 2)
                load_layer(2, e2, par, k2)
                store_y(i, par)
                load_bias(e2, par, k2)

            def yes(i):
                return always

            e = expert(SH_A)
            sp.wait_ge(S["l1_done"], 2 * SH_A - 2)
            load_layer(0, e, 0, always)
            turn(SH_A - 2, 0, yes, yes)
            turn(SH_A - 1, 1, yes, other)
            with sp.Fori(SH_A // 2, SH_B0 // 2 - 1) as h:
                for par in range(2):
                    turn(2 * h + par, par, other, other)
            turn(SH_B0 - 2, 0, other, other, EARLY)
            turn(SH_B0 - 1, 1, other, None, EARLY + 2)

            def early_rows(n):
                for k in range(2):
                    need(sp, cmb[k], n)
                    sp.dma_start(ys[:, k, :], ysl[bass.ds((2 * n + k) * P, P), :]).then_inc(ys_in[k], 16)

            def puts(n):
                for slot in range(4):
                    sp.wait_ge(cmb[slot], n + 1)
                    b = 2 * n + slot % 2 + (EARLY if slot >= 2 else 0)
                    sp.dma_start(out[bass.ds(b, 1)].rearrange("o p c -> (o p) c"), ob[:, slot, :]).then_inc(o_out[slot], 16)

            n_late = SH_TILES - SH_A
            load_x(SH_B0 + 2, 0, EARLY + 4)
            early_rows(0)

            def late(j, par, more):
                if more:
                    load_x(SH_B0 + j + 2, par, EARLY + 2 * j + 4)
                puts(j - 1)
                early_rows(j)
            with sp.Fori(0, n_late // 2 - 2) as h:
                late(2 * h + 1, 1, True)
                late(2 * h + 2, 0, True)
            for j in range(n_late - 3, n_late):
                late(j, j % 2, j + 2 < n_late)
            puts(n_late - 1)
            for slot in range(4):
                sp.wait_ge(o_out[slot], 16 * n_late)

        @block.gpsimd
        def _(g):
            cp = [0]

            def link(ins):
                cp[0] += 1
                ins.then_inc(S["chainp"], 1)
                g.wait_ge(S["chainp"], cp[0])
            g.memset(eps[:, :], EPS).then_inc(S["id_ready"], 1)
            link(g.memset(id32[:, :], 0.0))
            link(g.memset(one16[:, :], 1.0))
            g.affine_select(out=id32[:, :], in_=id32[:, :], compare_op=ALU.not_equal, fill=1.0, base=0,
                            pattern=[[-1, P]], channel_multiplier=1).then_inc(S["id_ready"], 1)
            g.wait_ge(S["id_ready"], 2)
            g.tensor_copy(id16[:, :], id32[:, :]).then_inc(S["id_ready"], 1)
            g.affine_select(out=tri[:, :], in_=one16[:, :], compare_op=ALU.is_gt, fill=0.0, base=0,
                            pattern=[[1, P]], channel_multiplier=-1).then_inc(S["id_ready"], 1)
            for par in range(2):
                g.memset(qcat[:, par, :, 3, :], 0.0).then_inc(S["vone"], 1)
                g.memset(kcat[:, par, :, :, 3, :], 0.0).then_inc(S["vone"], 1)
            g.wait_ge(S["vone"], 4)
            for par in range(2):
                g.memset(kcat[:, par, :, :, 3, 0:1], 1.0).then_inc(S["vone"], 1)
            g.iota(tok[:, :], pattern=[[P, NB]], base=0, channel_multiplier=1, allow_small_or_imprecise_dtypes=True).then_inc(S["id_ready"], 1)
            g.iota(rev8[:, :], pattern=[[-1, 8]], base=8, channel_multiplier=0, allow_small_or_imprecise_dtypes=True).then_inc(S["id_ready"], 1)
            g.iota(it[:, :], pattern=[[1, SLOT_TILES]], base=0, channel_multiplier=0, allow_small_or_imprecise_dtypes=True).then_inc(S["id_ready"], 1)
            g.memset(etab[:, 0:SH_A], E_R).then_inc(S["idx_ready"], 1)
            g.memset(etab[:, SH_B0:N_TILES], E_R).then_inc(S["idx_ready"], 1)
            link(g.memset(idr[:, :], 0.0))
            g.dma_start(idd.rearrange("(c p) o -> c (p o)", p=P), idr[:, :]).then_inc(S["idz"], 16)

            def split_kq(half, par):
                b = 2 * half + par
                g.wait_ge(S["kh_ready"], b + 1)
                cv = C[:, bass.ds(b, 1), :].rearrange("p o (h d) -> p (o h) d", d=D)
                g.tensor_tensor(kcat[:, par, :, :, 1, :], cv.unsqueeze(2).to_broadcast([P, NKV, 2, D]),
                                kcat[:, par, :, :, 0, :], ALU.subtract).then_inc(S["k_split"], 1)
                g.wait_ge(S["qh_ready"], b + 1)
                g.wait_ge(S["xn_ready"], b + 1)
                g.tensor_tensor(qcat[:, par, :, 0, :], xn32[:, par, :].rearrange("p (h d) -> p h d", d=D),
                                qcat[:, par, :, 1, :], ALU.subtract).then_inc(S["q_split"], 1)

            def low_p(half, par, u):
                g.wait_ge(S["exp_done"], 2 * (UNITS * (2 * half + par) + u + 1))
                g.tensor_tensor(Ps[:, u % 2, 1, :, :], Pt[:, u % 2, :, :], Ps[:, u % 2, 0, :, :], ALU.subtract).then_inc(S["plo_g"], 1)

            def residual(half, par):
                b = 2 * half + par
                g.wait_ge(S["att_ready"], 2 * b + 2)
                xv = X[:, bass.ds(b, 1), :].rearrange("p o c -> p (o c)")
                g.tensor_tensor(xv, xv, att[:, par, :], ALU.add).then_inc(S["x1_ready"], 1)

            def weights_lo(half, par):
                b = 2 * half + par
                g.wait_ge(S["whi_ready"], b + 1)
                g.tensor_tensor(whl[:, par, :, 1, :], wst[:, par, :, :], whl[:, par, :, 0, :], ALU.subtract).then_inc(S["wlo_ready"], 1)

            g.wait_ge(c_in[0], 16)
            g.wait_ge(S["ln1_ready"], 1)
            split_kq(0, 0)

            def body(half, par, first, last):
                if not last:
                    split_kq(*((half, 1) if par == 0 else (half + 1, 0)))
                if not first:
                    residual(*((half - 1, 1) if par == 0 else (half, 0)))
                low_p(half, par, 1)
                weights_lo(half, par)
                low_p(half, par, 3)
            over_batches(g, body)
            residual(NB // 2 - 1, 1)

            def low2(i):
                for k in range(4):
                    g.wait_ge(S["x2n_ready"], 4 * i + k + 1)
                    g.wait_ge(S["x2h_ready"], 4 * i + k + 1)
                    g.tensor_tensor(xhl[:, k, 1, :], x2n[:, k, :], xhl[:, k, 0, :], ALU.subtract).then_inc(S["x2l_ready"], 1)
            with g.Fori(0, NB // 4) as i:
                low2(i)

            g.wait_ge(S["idz"], 16)
            g.wait_ge(S["rt_pos"], 1)
            g.wait_ge(S["id_ready"], 7)

            def scatter(h, first):
                for j in range(2):
                    if not first:
                        g.wait_ge(scat[j], 16 * 2 * SB * h)
                        g.nop(nofuse=True)
                    g.tensor_copy(sct[:, j, :, :], rpos[:, bass.ds((2 * h + j) * SB, SB), :]).then_inc(S["sct_ready"], 1)
                    g.tensor_copy(stk[:, j, :], tok[:, bass.ds((2 * h + j) * SB, SB)]).then_inc(S["sct_ready"], 1)
                    g.wait_ge(S["sct_ready"], 4 * h + 2 * j + 2)
                    g.nop(nofuse=True)
                    for b in range(SB):
                        for k in range(2):
                            g.indirect_dma_start(out=idd, out_offset=bass.IndirectOffsetOnAxis(ap=sct[:, j, b, k:k + 1], axis=0),
                                                 in_=stk[:, j, b:b + 1], in_offset=None).then_inc(scat[j], 16)
            scatter(0, True)
            with g.Fori(1, NB // SB // 2) as h:
                scatter(h, False)
            for j in range(2):
                g.wait_ge(scat[j], 16 * NB)
            g.dma_start(idr[:, :], idd.rearrange("(c p) o -> c (p o)", p=P)).then_inc(S["id_load"], 16)
            for j in range(4):
                g.wait_ge(x2_out[j], 16 * (NB // 4))
            g.wait_ge(S["phaseC"], 1)
            g.wait_ge(S["idx_ready"], 3)

            def gather(i, par):
                g.wait_ge(S["xt_done"], 2 * i - 2)
                g.nop(nofuse=True)
                g.tensor_copy(ixr[:, par, :], idx[:, bass.ds(2 * (i - SH_A), 2)]).then_inc(S["ix_ready"], 1)
                g.wait_ge(S["ix_ready"], i - SH_A + 1)
                g.nop(nofuse=True)
                for t in range(2):
                    g.indirect_dma_start(out=xs[:, par, t, :], out_offset=None, in_=xnd,
                                         in_offset=bass.IndirectOffsetOnAxis(ap=ixr[:, par, t:t + 1], axis=0)).then_inc(xg_in[par], 16)
            with g.Fori(SH_A // 2, SH_B0 // 2) as h:
                for par in range(2):
                    gather(2 * h + par, par)

            for par in range(2):
                g.wait_ge(y_out[par], 16 * (SH_B0 // 2))

            def fetch(n):
                for slot in range(4):
                    b = 2 * n + slot % 2 + (EARLY if slot >= 2 else 0)
                    if not isinstance(n, int):
                        g.wait_ge(cmb[slot], n)
                        g.nop(nofuse=True)
                    g.tensor_copy(ixf[:, slot, :].unsqueeze(1), pos[:, bass.ds(b, 1), :]).then_inc(S["ix_ready"], 1)
                    g.wait_ge(S["ix_ready"], SLOT_TILES + 4 * n + slot + 1)
                    g.nop(nofuse=True)
                    for k in range(2):
                        g.indirect_dma_start(out=yg[:, slot, k, :], out_offset=None, in_=ysl,
                                             in_offset=bass.IndirectOffsetOnAxis(ap=ixf[:, slot, k:k + 1], axis=0)).then_inc(yg_in[slot], 16)
            fetch(0)
            with g.Fori(1, SH_TILES - SH_A) as n:
                fetch(n)

        @block.scalar
        def _(act):
            act.wait_ge(S["const_in"], 64)
            act.activation(tg[:, :], gts[:, :], ACT.Tanh).then_inc(S["tanh_done"], 1)
            act.wait_ge(S["id_ready"], 1)

            def root1(n, bs):
                act.wait_ge(S["var1"], n)
                act.activation(ln[:, 2, bs], mv1[:, bs, 1], ACT.Sqrt, bias=eps[:, 0:1]).then_inc(S["std1"], 1)
            root1(1, slice(0, NB // XC))
            act.wait_ge(c_in[0], 16)
            act.wait_ge(S["ln1_ready"], 1)
            act.wait_ge(S["wrs_ready"], 1)
            act.activation(wrs[:, 0, :, :], wr32[:, :, :], ACT.Copy).then_inc(S["wrh_ready"], 1)

            def high(half, par):
                b = 2 * half + par
                need(act, S["pv_done"], UNITS * (b - 1))
                cv = C[:, bass.ds(b, 1), :].rearrange("p o (h d) -> p (o h) d", d=D)
                for dup in range(2):
                    ins = act.activation(kcat[:, par, :, dup, 0:3:2, :], cv.unsqueeze(2).to_broadcast([P, NKV, 2, D]), ACT.Copy)
                ins.then_inc(S["kh_ready"], 1)
                need(act, S["tq1_done"], b - 1)
                act.activation(qcat[:, par, :, 1:3, :], X[:, bass.ds(b, 1), :].rearrange("p o (h d) -> p (o h) d", d=D).unsqueeze(2).to_broadcast([P, NH, 2, D]),
                               ACT.Identity, bias=ln[:, 1, bass.ds(b, 1)], scale=ln[:, 0, bass.ds(b, 1)]).then_inc(S["qh_ready"], 1)

            def evac_q0(half, par):
                b = 2 * half + par
                act.wait_ge(S["tq0_done"], b + 1)
                act.activation(qT[:, par, 0:8, :], Rb16[1], ACT.Copy).then_inc(S["qT0_ready"], 1)

            def exps(half, par, u):
                n = UNITS * (2 * half + par) + u
                need(act, S["pv_done"], n - 1)
                for odd in range(2):
                    act.wait_ge(S["t_done"], 2 * n + odd + 1)
                    heads = slice(odd * 4, odd * 4 + 4)
                    act.activation(Ps[:, u % 2, 0, heads, :].rearrange("p h s -> p (h s)"), Tb[:, odd, :], ACT.Exp, scale=float(D) ** -0.5)
                    act.activation(Pt[:, u % 2, heads, :].rearrange("p h s -> p (h s)"), Tb[:, odd, :], ACT.Exp, scale=float(D) ** -0.5).then_inc(S["exp_done"], 1)

            def weights_hi(half, par):
                b = 2 * half + par
                act.wait_ge(S["w64_ready"], b + 1)
                if not (isinstance(b, int) and b < 2):
                    act.wait_ge(w_out[par], 16 * half)
                act.activation(whl[:, par, :, 0, :], wst[:, par, :, :], ACT.Copy).then_inc(S["whi_ready"], 1)

            high(0, 0)
            evac_q0(0, 0)

            def body(half, par, first, last):
                nx = (half, 1) if par == 0 else (half + 1, 0)
                exps(half, par, 0)
                if isinstance(half, int) and (half, par) == ROOTS:
                    root1(2, slice(NB // XC, NB))
                    act.wait_ge(S["ln1_ready"], 2)
                    act.wait_ge(c_in[1], 16)
                if not last:
                    high(*nx)
                exps(half, par, 1)
                weights_hi(half, par)
                exps(half, par, 2)
                if not last:
                    evac_q0(*nx)
                exps(half, par, 3)
            over_batches(act, body)

            act.wait_ge(S["var2"], 1)
            act.activation(ln2[:, 2, :], mv2[:, :, 1], ACT.Sqrt, bias=eps[:, 0:1]).then_inc(S["std2"], 1)
            act.wait_ge(S["ln2_ready"], 1)

            def norm2(i, first):
                for k in range(4):
                    b = 4 * i + k
                    if not first:
                        act.wait_ge(S["t2_done"], b - 3)
                        act.wait_ge(x2_out[k], 16 * i)
                    act.activation(xhl[:, k, 0, :], X[:, bass.ds(b, 1), :].rearrange("p o c -> p (o c)"),
                                   ACT.Identity, bias=ln2[:, 1, bass.ds(b, 1)], scale=ln2[:, 0, bass.ds(b, 1)]).then_inc(S["x2h_ready"], 1)
            norm2(0, True)
            with act.Fori(1, NB // 4) as i:
                norm2(i, False)
            act.wait_ge(S["rt_sel"], 1)
            act.activation(ex[:, :, :], sel[:, :, :], ACT.Exp).then_inc(S["rt_exp"], 1)
            act.wait_ge(S["phaseC"], 1)

            def evac_x(i, par):
                act.wait_ge(S["xt_done"], 2 * i + 1)
                need(act, S["l1_done"], 2 * i - 2)
                act.activation(xT[:, par, :, :, 0:P], PS[3][:, 0, :].bitcast(F16).rearrange("p (h k c) -> p h k c", h=2, k=KT),
                               ACT.Copy).then_inc(S["xTa_ready"], 1)

            def up_out(i, par, n_loads):
                for hf in range(2):
                    act.wait_ge(S["l1_done"], 2 * i + hf + 1)
                    if hf == 0:
                        act.wait_ge(bi_in[par], 32 * n_loads)
                        need(act, S["g_ready"], 2 * i - 2)
                    for m in range(2 * hf, 2 * hf + 2):
                        ins = act.activation(u32[:, par, m, :], PS[0][:, hf, bass.ds((m % 2) * TT, TT)], ACT.Identity,
                                             bias=bb[:, par, 0, m:m + 1], scale=1.0 / WS)
                    ins.then_inc(S["u_ready"], 2 // 2)

            def gate_out(i, par):
                for hf in range(2):
                    act.wait_ge(S["l2_done"], 2 * i + hf + 1)
                    need(act, S["g_ready"], 2 * i - 1 + hf)
                    for m in range(2 * hf, 2 * hf + 2):
                        ins = act.activation(sl[:, m, :], PS[1][:, hf, bass.ds((m % 2) * TT, TT)], ACT.Silu,
                                             bias=bb[:, par, 1, m:m + 1], scale=1.0 / WS)
                    ins.then_inc(S["s_ready"], 1)
            evac_x(0, 0)
            up_out(0, 0, 1)

            def tile(half, par, loads_of, tokens_of):
                i = 2 * half + par
                last = isinstance(i, int) and i == N_TILES - 1
                if not last:
                    evac_x(i + 1, 1 - par)
                gate_out(i, par)
                if not last:
                    up_out(i + 1, 1 - par, loads_of(half + par))
            for lo, hi, *of in over_tiles(tile):
                with act.Fori(lo, hi) as h:
                    tile(h, 0, *of)
                    tile(h, 1, *of)

        @block.vector
        def _(v):
            cv = [0]

            def link(ins):
                cv[0] += 1
                ins.then_inc(S["chain"], 1)
                v.wait_ge(S["chain"], cv[0])

            n = NB // XC
            v.wait_ge(S["wr_in"], 16)
            v.tensor_scalar(wr32[:, :, :], wr32[:, :, :], WS, None, ALU.mult).then_inc(S["wrs_ready"], 1)

            def stats1(c):
                v.wait_ge(x_in[c], 16)
                for b in range(c * n, (c + 1) * n):
                    ins = v.bn_stats(st1[:, b, :], X[:, b, :])
                link(ins)
                for b in range(c * n, (c + 1) * n):
                    ins = v.bn_aggr(mv1[:, b, :], st1[:, b, :])
                return ins

            def rstd(mv, t, bs):
                link(v.reciprocal(t[:, 3, bs], t[:, 2, bs]))
                link(v.tensor_scalar(t[:, 4, bs], mv[:, bs, 1], EPS, None, ALU.add))
                link(v.tensor_tensor(t[:, 4, bs], t[:, 4, bs], t[:, 3, bs], ALU.mult))
                link(v.tensor_tensor(t[:, 4, bs], t[:, 4, bs], t[:, 3, bs], ALU.mult))
                link(v.tensor_scalar(t[:, 4, bs], t[:, 4, bs], -0.5, 1.5, ALU.mult, ALU.add))
                link(v.tensor_tensor(t[:, 0, bs], t[:, 4, bs], t[:, 3, bs], ALU.mult))
                return v.scalar_tensor_tensor(out=t[:, 1, bs], in0=mv[:, bs, 0], scalar=-1.0, in1=t[:, 0, bs], op0=ALU.mult, op1=ALU.mult)
            stats1(0).then_inc(S["var1"], 1)
            v.wait_ge(S["var1"], 1)
            v.wait_ge(S["std1"], 1)
            rstd(mv1, ln, slice(0, n)).then_inc(S["ln1_ready"], 1)
            v.wait_ge(S["ln1_ready"], 1)
            v.wait_ge(S["tanh_done"], 1)

            def late_stats1(part):
                for c in ((1, 2), (3, 4), (5, 6, 7))[part]:
                    ins = stats1(c)
                    if c < XC - 1:
                        link(ins)
                if part == 2:
                    ins.then_inc(S["var1"], 1)
                    v.wait_ge(S["var1"], 2)
                    v.wait_ge(S["std1"], 2)
                    rstd(mv1, ln, slice(n, NB)).then_inc(S["ln1_ready"], 1)
                    v.wait_ge(S["ln1_ready"], 2)
                    v.wait_ge(S["wrh_ready"], 1)
                    v.tensor_tensor(wrs[:, 1, :, :], wr32[:, :, :], wrs[:, 0, :, :], ALU.subtract).then_inc(S["wrs_ready"], 1)

            def norm1(half, par):
                b = 2 * half + par
                need(v, S["q_split"], b - 1)
                v.tensor_scalar(xn32[:, par, :], X[:, bass.ds(b, 1), :].rearrange("p o c -> p (o c)"), ln[:, 0, bass.ds(b, 1)],
                                ln[:, 1, bass.ds(b, 1)], ALU.mult, ALU.add).then_inc(S["xn_ready"], 1)

            def evac_k(half, par):
                b = 2 * half + par
                v.wait_ge(S["tk_done"], b + 1)
                v.tensor_copy(kT[:, par, :, :], Rb16[0]).then_inc(S["kT_ready"], 1)

            def evac_q1(half, par):
                b = 2 * half + par
                v.wait_ge(S["tq1_done"], b + 1)
                v.tensor_copy(qT[:, par, 8:16, :], Rb16[0]).then_inc(S["qT1_ready"], 1)

            def maxes(half, par, u):
                k = 2 * (UNITS * (2 * half + par) + u)
                for odd in range(2):
                    v.wait_ge(S["m_done"], k + odd + 1)
                    v.tensor_reduce(negm[:, par, u, odd * 4:odd * 4 + 4], Mb[:, odd, :].rearrange("p (j t) -> p j t", t=CTX),
                                    AX.X, ALU.max, negate=True).then_inc(S["max_done"], 1)

            def low_p(half, par, u):
                v.wait_ge(S["exp_done"], 2 * (UNITS * (2 * half + par) + u + 1))
                v.tensor_tensor(Ps[:, u % 2, 1, :, :], Pt[:, u % 2, :, :], Ps[:, u % 2, 0, :, :], ALU.subtract).then_inc(S["plo_v"], 1)

            def normalise(half, par, hf):
                b = 2 * half + par
                v.wait_ge(S["pv_done"], UNITS * b + 2 * hf + 2)
                v.reciprocal(rec[:, hf, :], Obv[hf][:, :, D]).then_inc(S["rec_done"], 1)
                v.wait_ge(S["rec_done"], 4 * b + 2 * hf + 1)
                v.tensor_scalar(rec[:, hf, :], rec[:, hf, :], tg[:, 0:1], None, ALU.mult).then_inc(S["rec_done"], 1)
                v.wait_ge(S["rec_done"], 4 * b + 2 * hf + 2)
                need(v, S["x1_ready"], b - 1)
                v.tensor_tensor(att[:, par, hf * 256:(hf + 1) * 256].rearrange("p (h d) -> p h d", d=D), Obv[hf][:, :, 0:D],
                                rec[:, hf, :].unsqueeze(2).to_broadcast([P, NH // 2, D]), ALU.mult).then_inc(S["att_ready"], 1)

            def stats2(half, par):
                b = 2 * half + par
                v.wait_ge(S["x1_ready"], b + 1)
                v.bn_stats(st2[:, bass.ds(b, 1), :].rearrange("p o c -> p (o c)"),
                           X[:, bass.ds(b, 1), :].rearrange("p o c -> p (o c)")).then_inc(S["st2_ready"], 1)

            def weights64(half, par):
                b = 2 * half + par
                v.wait_ge(w_in[par], 16 * (half + 1))
                v.tensor_scalar(wst[:, par, :, :], wst[:, par, :, :], WS, None, ALU.mult).then_inc(S["w64_ready"], 1)

            norm1(0, 0)
            evac_k(0, 0)
            evac_q1(0, 0)
            maxes(0, 0, 0)

            def body(half, par, first, last):
                nx = (half, 1) if par == 0 else (half + 1, 0)
                pv = (half - 1, 1) if par == 0 else (half, 0)
                maxes(half, par, 1)
                if isinstance(half, int) and 2 * half + par < 3:
                    late_stats1(2 * half + par)
                if not last:
                    norm1(*nx)
                weights64(half, par)
                low_p(half, par, 0)
                if not first:
                    normalise(*pv, 1)
                maxes(half, par, 2)
                if not last:
                    evac_k(*nx)
                if not first:
                    stats2(*pv)
                maxes(half, par, 3)
                low_p(half, par, 2)
                normalise(half, par, 0)
                if not last:
                    evac_q1(*nx)
                    maxes(*nx, 0)
            over_batches(v, body)
            normalise(NB // 2 - 1, 1, 1)
            stats2(NB // 2 - 1, 1)
            v.wait_ge(S["st2_ready"], NB)
            for b in range(NB):
                ins = v.bn_aggr(mv2[:, b, :], st2[:, b, :])
            ins.then_inc(S["var2"], 1)
            v.wait_ge(S["std2"], 1)
            v.wait_ge(S["var2"], 1)
            rstd(mv2, ln2, slice(0, NB)).then_inc(S["ln2_ready"], 1)
            v.wait_ge(S["ln2_ready"], 1)

            def norm2(b, k):
                need(v, S["x2l_ready"], b - 3)
                v.tensor_scalar(x2n[:, k, :], X[:, bass.ds(b, 1), :].rearrange("p o c -> p (o c)"), ln2[:, 0, bass.ds(b, 1)],
                                ln2[:, 1, bass.ds(b, 1)], ALU.mult, ALU.add).then_inc(S["x2n_ready"], 1)

            def evac_x2(b, k):
                v.wait_ge(S["t2_done"], b + 1)
                need(v, S["gate_done"], b - 1)
                v.tensor_copy(xhT[:, k % 2, :, :], Rb16[k % 2]).then_inc(S["x2T_ready"], 1)
            for b in range(3):
                norm2(b, b)

            def four(i, last):
                for k in range(4):
                    if not (last and k > 0):
                        norm2(4 * i + k + 3, (k + 3) % 4)
                    evac_x2(4 * i + k, k)
            four(0, False)
            with v.Fori(1, NB // 4 - 1) as i:
                four(i, False)
            four(NB // 4 - 1, True)

            def over_b(ap):
                return ap.unsqueeze(1).to_broadcast([P, NB, ap.shape[-1]])

            def over_e(ap):
                return ap.unsqueeze(2).to_broadcast([P, NB, 8])

            v.wait_ge(S["gate_done"], NB)
            link(v.memset(gate[:, :, :], 0.0))
            link(v.memset(bia[:, :, :], -BIG))
            link(v.scalar_tensor_tensor(out=gate[:, :, 0:E_R], in0=LG[:, :, 0:E_R], scalar=1.0 / WS, in1=over_b(brb[:, :]),
                                        op0=ALU.mult, op1=ALU.add))
            link(v.tensor_tensor(bia[:, :, 0:E_R], gate[:, :, 0:E_R], over_b(gbb[:, :]), ALU.add))
            v.wait_ge(S["id_ready"], 7)
            for k in range(2):
                link(v.tensor_reduce(mx[:, :], bia[:, :, :], AX.X, ALU.max))
                link(v.tensor_tensor(r1[:, :, :], bia[:, :, :], over_e(mx[:, :]), ALU.is_equal))
                link(v.tensor_tensor(r1[:, :, :], r1[:, :, :], over_b(rev8[:, :]), ALU.mult))
                link(v.tensor_reduce(mx[:, :], r1[:, :, :], AX.X, ALU.max))
                link(v.tensor_tensor(oh[:, k, :, :], over_b(rev8[:, :]), over_e(mx[:, :]), ALU.is_equal))
                if k == 0:
                    link(v.scalar_tensor_tensor(out=bia[:, :, :], in0=oh[:, 0, :, :], scalar=-BIG, in1=bia[:, :, :], op0=ALU.mult, op1=ALU.add))
                link(v.tensor_tensor(r2[:, :, :], oh[:, k, :, :], gate[:, :, :], ALU.mult))
                link(v.tensor_reduce(sel[:, k, :], r2[:, :, :], AX.X, ALU.add))
            v.tensor_tensor(msum[:, :, :], oh[:, 0, :, :], oh[:, 1, :, :], ALU.add).then_inc(S["rt_mask"], 1)
            link(v.tensor_tensor(mx[:, :], sel[:, 0, :], sel[:, 1, :], ALU.max))
            v.tensor_tensor(sel[:, :, :], sel[:, :, :], mx[:, :].unsqueeze(1).to_broadcast([P, 2, NB]), ALU.subtract).then_inc(S["rt_sel"], 1)
            v.wait_ge(S["rt_exp"], 1)
            link(v.tensor_tensor(mx[:, :], ex[:, 0, :], ex[:, 1, :], ALU.add))
            link(v.reciprocal(mx[:, :], mx[:, :]))
            link(v.tensor_scalar(mx[:, :], mx[:, :], tg[:, 1:2], None, ALU.mult))
            link(v.tensor_tensor(prb[:, :, :], ex[:, :, :], mx[:, :].unsqueeze(1).to_broadcast([P, 2, NB]), ALU.mult))
            v.wait_ge(S["rt_cnt"], 2)
            CNT = PS[1][:, 1, 0:NB * 8].rearrange("p (b e) -> p b e", e=8)
            RNK = PS[1][:, 0, 0:NB * 8].rearrange("p (b e) -> p b e", e=8)
            link(v.tensor_copy(r1[:, :, :], CNT))
            src, dst, s = r1, r2, 1
            while s < NB:
                link(v.tensor_copy(dst[:, 0:s, :], src[:, 0:s, :]))
                link(v.tensor_tensor(dst[:, s:NB, :], src[:, s:NB, :], src[:, 0:NB - s, :], ALU.add))
                src, dst, s = dst, (r3 if dst is r2 else r2), 2 * s
            link(v.tensor_scalar(e8[:, 0, :], src[:, NB - 1, :], float(TT - 1), None, ALU.add))
            link(v.tensor_copy(i8[:, 0, :], e8[:, 0, :]))
            link(v.tensor_scalar(i8[:, 1, :], i8[:, 0, :], TT.bit_length() - 1, None, ALU.logical_shift_right))
            link(v.tensor_copy(e8[:, 1, :], i8[:, 1, :]))
            ends, nxt, s = 1, 2, 1
            while s < 8:
                link(v.tensor_copy(e8[:, nxt, 0:s], e8[:, ends, 0:s]))
                link(v.tensor_tensor(e8[:, nxt, s:8], e8[:, ends, s:8], e8[:, ends, 0:8 - s], ALU.add))
                ends, nxt, s = nxt, nxt + 1, 2 * s
            link(v.tensor_tensor(e8[:, 5, :], e8[:, ends, :], e8[:, 1, :], ALU.subtract))
            link(v.tensor_scalar(e8[:, 5, :], e8[:, 5, :], float(TT), None, ALU.mult))
            tot = dst
            link(v.tensor_tensor(tot[:, :, :], src[:, :, :], r1[:, :, :], ALU.subtract))
            link(v.tensor_tensor(tot[:, :, :], tot[:, :, :], over_b(e8[:, 5, :]), ALU.add))
            link(v.tensor_tensor(tot[:, :, :], tot[:, :, :], RNK, ALU.add))
            for k in range(2):
                link(v.tensor_tensor(r1[:, :, :], tot[:, :, :], oh[:, k, :, :], ALU.mult))
                link(v.tensor_reduce(sel[:, k, :], r1[:, :, :], AX.X, ALU.add))
            v.tensor_copy(rpos[:, :, :].rearrange("p b k -> p k b"), sel[:, :, :]).then_inc(S["rt_pos"], 1)
            link(v.tensor_scalar(sel[:, :, :], sel[:, :, :], float(SH_A * TT), None, ALU.add))
            link(v.tensor_copy(pos[:, :, :].rearrange("p b k -> p k b"), sel[:, :, :]))
            link(v.memset(ef[:, 0, :], 0.0))
            for e in range(E_R):
                link(v.scalar_tensor_tensor(out=ef[:, (e + 1) % 2, :], in0=it[:, :], scalar=e8[:, ends, e:e + 1],
                                            in1=ef[:, e % 2, :], op0=ALU.is_ge, op1=ALU.add))
            link(v.tensor_scalar(ef[:, 0, :], ef[:, E_R % 2, :], float(E_R - 1), None, ALU.min))
            link(v.tensor_copy(etab[:, SH_A:SH_B0], ef[:, 0, :]))
            v.wait_ge(S["idx_ready"], 2)
            link(v.tensor_tensor(chg[:, 2:N_TILES], etab[:, 2:N_TILES], etab[:, 0:N_TILES - 2], ALU.not_equal))
            v.memset(mx[:, :], 0.0).then_inc(S["phaseC"], 1)

            def evac_x(i, par):
                v.wait_ge(S["xt_done"], 2 * i + 2)
                need(v, S["l1_done"], 2 * i - 2)
                v.tensor_copy(xT[:, par, :, :, P:TT], PS[3][:, 1, :].bitcast(F16).rearrange("p (h k c) -> p h k c", h=2, k=KT)).then_inc(S["xTv_ready"], 1)

            def split_u(i, par):
                for hf in range(2):
                    ms = slice(2 * hf, 2 * hf + 2)
                    v.wait_ge(S["u_ready"], 2 * i + hf + 1)
                    need(v, S["l2_done"], 2 * i)
                    v.tensor_copy(uhl[:, 0, ms, :], u32[:, par, ms, :]).then_inc(S["uh_ready"], 1)
                    v.wait_ge(S["uh_ready"], 2 * i + hf + 1)
                    v.tensor_tensor(uhl[:, 1, ms, :], u32[:, par, ms, :], uhl[:, 0, ms, :], ALU.subtract).then_inc(S["ul_ready"], 1)

            def gating(i, par):
                for hf in range(2):
                    ms = slice(2 * hf, 2 * hf + 2)
                    v.wait_ge(S["s_ready"], 2 * i + hf + 1)
                    v.tensor_tensor(g32[:, ms, :], sl[:, ms, :], u32[:, par, ms, :], ALU.mult).then_inc(S["g_ready"], 1)
                    v.wait_ge(S["g_ready"], 2 * i + hf + 1)
                    need(v, S["l3_done"], 2 * i)
                    v.tensor_copy(ghl[:, 0, ms, :], g32[:, ms, :]).then_inc(S["gh_ready"], 1)
                    v.wait_ge(S["gh_ready"], 2 * i + hf + 1)
                    v.tensor_tensor(ghl[:, 1, ms, :], g32[:, ms, :], ghl[:, 0, ms, :], ALU.subtract).then_inc(S["gl_ready"], 1)

            def down_out(i, par, stored):
                for t in range(2):
                    v.wait_ge(S["l3_done"], 2 * i + t + 1)
                    if t == 0:
                        need(v, y_out[par], 16 * stored)
                    v.scalar_tensor_tensor(out=yb[:, par, t, :], in0=PS[2][:, t, :], scalar=1.0 / WS, in1=bd[:, par, :],
                                           op0=ALU.mult, op1=ALU.add).then_inc(S["y_ready"], 1)

            def step_of(n, k):
                for slot in range(4):
                    b = 2 * n + slot % 2 + (EARLY if slot >= 2 else 0)
                    xv = X[:, bass.ds(b, 1), :].rearrange("p o c -> p (o c)")
                    if k < 2:
                        if k == 0:
                            v.wait_ge(yg_in[slot], 32 * n + 32)
                        else:
                            v.wait_ge(S["cx"], 8 * n + slot + 1)
                        v.scalar_tensor_tensor(out=xv, in0=yg[:, slot, k, :], scalar=prb[:, k, bass.ds(b, 1)], in1=xv,
                                               op0=ALU.mult, op1=ALU.add).then_inc(S["cx"], 1)
                        continue
                    v.wait_ge(S["cx"], 8 * n + 4 + slot + 1)
                    if slot < 2:
                        v.wait_ge(ys_in[slot], 16 * n + 16)
                    else:
                        v.wait_ge(S["y_ready"], 2 * (SH_B0 + n) + 2)
                    need(v, o_out[slot], 16 * n)
                    shared = ys[:, slot, :] if slot < 2 else yb[:, yb_par[0], slot - 2, :]
                    v.scalar_tensor_tensor(out=ob[:, slot, :], in0=shared, scalar=tg[:, 1:2], in1=xv,
                                           op0=ALU.mult, op1=ALU.add).then_inc(cmb[slot], 1)
            yb_par = [0]
            evac_x(0, 0)
            split_u(0, 0)

            def tile(half, par, stored, beside=None):
                i = 2 * half + par
                last = isinstance(i, int) and i == N_TILES - 1
                if not last:
                    evac_x(i + 1, 1 - par)
                gating(i, par)
                if beside is not None:
                    step_of(beside, 0)
                if not last:
                    split_u(i + 1, 1 - par)
                if beside is not None:
                    yb_par[0] = 1 - par
                    step_of(beside, 1)
                    step_of(beside, 2)
                down_out(i, par, stored)
            for par in range(2):
                tile(0, par, 0)
            with v.Fori(1, SH_A // 2 - 1) as h:
                for par in range(2):
                    tile(h, par, h)
            v.wait_ge(S["idT"], 1)
            v.tensor_copy(idx[:, :], PS[2][:, 0, 0:R_COLS]).then_inc(S["idx_ready"], 1)
            with v.Fori(SH_A // 2 - 1, SH_B0 // 2) as h:
                for par in range(2):
                    tile(h, par, h)
            tile(SH_B0 // 2, 0, SH_B0 // 2)
            tile(SH_B0 // 2, 1, SH_B0 // 2, 0)
            with v.Fori(SH_B0 // 2 + 1, N_TILES // 2 - 1) as h:
                for par in range(2):
                    tile(h, par, SH_B0 // 2, 2 * h + par - SH_B0 - 1)
            for par in range(2):
                tile(N_TILES // 2 - 1, par, SH_B0 // 2, N_TILES - 2 + par - SH_B0 - 1)
            yb_par[0] = (N_TILES - 1) % 2
            for k in range(3):
                step_of(SH_TILES - SH_A - 1, k)

        @block.tensor
        def _(pe):
            pe.wait_ge(S["id_ready"], 4)
            pe.wait_ge(S["vone"], 6)

            def tr_k(half, par):
                b = 2 * half + par
                pe.wait_ge(S["k_split"], b + 1)
                need(pe, S["qT1_ready"], b)
                for kv in range(NKV):
                    ins = pe.transpose(Rb16[0][:, kv, :], kcat[:, par, kv, :, :, :].rearrange("p o r d -> p (o r d)"), id16[:, :])
                ins.then_inc(S["tk_done"], 1)

            def tr_q(half, par, part):
                b = 2 * half + par
                if part == 0:
                    pe.wait_ge(S["q_split"], b + 1)
                    need(pe, S["qT0_ready"], b)
                else:
                    pe.wait_ge(S["kT_ready"], b + 1)
                for j in range(BLK // 2):
                    blk = part * BLK // 2 + j
                    ins = pe.transpose(Rb16[1 - part][:, j, :], qcat[:, par, 2 * blk:2 * blk + 2, :, :].rearrange("p h r d -> p (h r d)"), id16[:, :])
                ins.then_inc(S["tq1_done"] if part else S["tq0_done"], 1)

            def scores_max(half, par, u, odd):
                b = 2 * half + par
                if u == 0:
                    pe.wait_ge(S["kT_ready"], b + 1)
                    pe.wait_ge(S["qT0_ready"], b + 1)
                if u == 2:
                    pe.wait_ge(S["qT1_ready"], b + 1)
                need(pe, S["max_done"], 2 * (UNITS * b + u) + odd - 1)
                rows = slice(64 * odd, 64 * odd + 3 * D)
                for j in range(HPU // 2):
                    ins = pe.matmul(Mb[:, odd, j * P:(j + 1) * P], qT[rows, par, 4 * u + j, :], kT[rows, par, 2 * u + j // 2, :],
                                    start=True, stop=True)
                ins.then_inc(S["m_done"], 1)

            def scores_T(half, par, u, odd):
                k = 2 * (UNITS * (2 * half + par) + u) + odd
                pe.wait_ge(S["max_done"], k + 1)
                need(pe, S["exp_done"], k - 1)
                for j in range(HPU // 2):
                    m = negm[:, par, u, odd * 4 + j:odd * 4 + j + 1].to_broadcast([P, P])
                    pe.matmul(Tb[:, odd, j * P:(j + 1) * P], m, id16[:, :], start=(j == 0), stop=False, skip_group_check=True)
                rows = slice(64 * odd, 64 * odd + 3 * D)
                for kv in range(2):
                    ins = pe.matmul(Tb[:, odd, kv * 256:(kv + 1) * 256], kT[rows, par, 2 * u + kv, :],
                                    qT[rows, par, 4 * u + 2 * kv:4 * u + 2 * kv + 2, :].rearrange("p n c -> p (n c)"),
                                    start=False, stop=(kv == 1), skip_group_check=True)
                ins.then_inc(S["t_done"], 1)

            def step(half, par, u, nxt):
                for odd in range(2):
                    if nxt is not None:
                        scores_max(*nxt, odd)
                    scores_T(half, par, u, odd)

            def outputs(half, par, u):
                b = 2 * half + par
                pe.wait_ge(S["plo_g"] if u % 2 else S["plo_v"], 2 * b + u // 2 + 1)
                if u % 2 == 0:
                    need(pe, S["att_ready"], 2 * (b - 1) + u // 2 + 1)
                for j in range(HPU // 2):
                    for odd in range(2):
                        c = (u % 2) * HPU + 2 * j + odd
                        head = odd * 4 + j
                        kv = kcat[:, par, 2 * u + j // 2, 0, :, :].rearrange("p r d -> p (r d)")
                        o = Ob[:, u // 2, c * (D + 1):(c + 1) * (D + 1)]
                        pe.matmul(o, Ps[:, u % 2, 0, head, :], kv[:, 2 * D:3 * D + 1], start=True, stop=False)
                        pe.matmul(o[:, 0:D], Ps[:, u % 2, 0, head, :], kv[:, D:2 * D], start=False, stop=False)
                        ins = pe.matmul(o, Ps[:, u % 2, 1, head, :], kv[:, 2 * D:3 * D + 1], start=False, stop=True)
                ins.then_inc(S["pv_done"], 1)

            tr_k(0, 0)
            tr_q(0, 0, 0)
            tr_q(0, 0, 1)
            scores_max(0, 0, 0, 0)
            scores_max(0, 0, 0, 1)

            def body(half, par, first, last):
                nx = (half, 1) if par == 0 else (half + 1, 0)
                pv = (half - 1, 1) if par == 0 else (half, 0)
                step(half, par, 0, (half, par, 1))
                if not first:
                    outputs(*pv, 3)
                step(half, par, 1, (half, par, 2))
                outputs(half, par, 0)
                if not last:
                    tr_k(*nx)
                    tr_q(*nx, 0)
                step(half, par, 2, (half, par, 3))
                outputs(half, par, 1)
                if not last:
                    tr_q(*nx, 1)
                step(half, par, 3, None if last else (*nx, 0))
                outputs(half, par, 2)
            over_batches(pe, body)
            outputs(NB // 2 - 1, 1, 3)

            def tr_x2(b, k):
                pe.wait_ge(S["x2l_ready"], b + 1)
                need(pe, S["x2T_ready"], b - 1)
                for n in range(2 * KT):
                    ins = pe.transpose(Rb16[k % 2][:, n, :], xhl[:, k, n // KT, (n % KT) * P:(n % KT + 1) * P], id16[:, :])
                ins.then_inc(S["t2_done"], 1)

            def gates(b, k):
                pe.wait_ge(S["x2T_ready"], b + 1)
                terms = [(xh, wh, kt) for xh, wh in ((0, 0), (0, 1), (1, 0)) for kt in range(KT)]
                for n, (xh, wh, kt) in enumerate(terms):
                    ins = pe.matmul(PS[0][:, 0, bass.ds(b * 8, E_R)], xhT[:, k % 2, xh * KT + kt, :], wrs[:, wh, kt, :],
                                    start=(n == 0), stop=(n == len(terms) - 1))
                ins.then_inc(S["gate_done"], 1)
            pe.wait_ge(S["qT1_ready"], NB)
            pe.wait_ge(S["qT0_ready"], NB)
            pe.wait_ge(S["wrs_ready"], 2)
            pe.wait_ge(S["max_done"], 2 * UNITS * NB)
            tr_x2(0, 0)

            def four(i, last):
                for k in range(4):
                    if not (last and k == 3):
                        tr_x2(4 * i + k + 1, (k + 1) % 4)
                    gates(4 * i + k, k)
            four(0, False)
            with pe.Fori(1, NB // 4 - 1) as i:
                four(i, False)
            four(NB // 4 - 1, True)
            pe.wait_ge(S["rt_mask"], 1)
            pe.wait_ge(S["exp_done"], 2 * UNITS * NB)
            mv = msum[:, :, :].rearrange("p b e -> p (b e)")
            pe.matmul(PS[1][:, 0, 0:NB * 8], tri[:, :], mv, start=True, stop=True).then_inc(S["rt_cnt"], 1)
            pe.matmul(PS[1][:, 1, 0:NB * 8], one16[:, :], mv, start=True, stop=True).then_inc(S["rt_cnt"], 1)
            pe.wait_ge(S["phaseC"], 1)

            def tr_x(i, par, come):
                pe.wait_ge(come[0][par], come[1])
                for t in range(2):
                    need(pe, S["xTv_ready"] if t else S["xTa_ready"], i)
                    src = PS[3][:, t, :].bitcast(F16).rearrange("p (n c) -> p n c", c=P)
                    for n in range(2 * KT):
                        ins = pe.transpose(src[:, n, :], xs[:, par, t, n * P:(n + 1) * P], id16[:, :])
                    ins.then_inc(S["xt_done"], 1)

            TERMS = [(w, x, k) for w, x in ((0, 0), (0, 1), (1, 0)) for k in range(KT)]

            def feature_layer(l, bank, rhs, i, par, n_loads, free, done):
                pe.wait_ge(wl_in[l][par], 16 * n_loads)
                for hf in range(2):
                    need(pe, free, 2 * i - 1 + hf)
                    for m in range(2 * hf, 2 * hf + 2):
                        for n, (w, x, k) in enumerate(TERMS):
                            ins = pe.matmul(bank[:, hf, (m % 2) * TT:(m % 2 + 1) * TT], wb[:, par, l, k, w, m * P:(m + 1) * P],
                                            rhs(x, k), start=(n == 0), stop=(n == len(TERMS) - 1))
                    ins.then_inc(done, 1)

            def up(i, par, n_loads):
                pe.wait_ge(S["xTa_ready"], i + 1)
                pe.wait_ge(S["xTv_ready"], i + 1)
                feature_layer(0, PS[0], lambda x, k: xT[:, par, x, k, :], i, par, n_loads, S["u_ready"], S["l1_done"])

            def gate_l(i, par, n_loads):
                pe.wait_ge(S["ul_ready"], 2 * i + 2)
                feature_layer(1, PS[1], lambda x, k: uhl[:, x, k, :], i, par, n_loads, S["s_ready"], S["l2_done"])

            def down(i, par, n_loads):
                pe.wait_ge(wl_in[2][par], 16 * n_loads)
                pe.wait_ge(S["gl_ready"], 2 * i + 2)
                for t in range(2):
                    need(pe, S["y_ready"], 2 * i - 1 + t)
                    for n, (w, x, k) in enumerate(TERMS):
                        ins = pe.matmul(PS[2][:, t, :], ghl[:, x, k, t * P:(t + 1) * P], wb[:, par, 2, k, w, :],
                                        start=(n == 0), stop=(n == len(TERMS) - 1))
                    ins.then_inc(S["l3_done"], 1)

            tr_x(0, 0, tokens(0))
            up(0, 0, 1)

            def tile(half, par, loads_of, tokens_of):
                i = 2 * half + par
                last = isinstance(i, int) and i == N_TILES - 1
                if isinstance(i, int) and i == SH_A - 2:
                    pe.wait_ge(S["id_load"], 16)
                    pe.wait_ge(S["y_ready"], 2 * i)
                    pe.transpose(PS[2][:, 0, 0:R_COLS], idr[:, :], id32[0:R_COLS, 0:R_COLS]).then_inc(S["idT"], 1)
                if not last:
                    tr_x(i + 1, 1 - par, tokens_of(half + par))
                gate_l(i, par, loads_of(half))
                if not last:
                    up(i + 1, 1 - par, loads_of(half + par))
                if isinstance(i, int) and i == SH_A - 2:
                    pe.wait_ge(S["idx_ready"], 3)
                down(i, par, loads_of(half))
            for lo, hi, *of in over_tiles(tile):
                with pe.Fori(lo, hi) as h:
                    tile(h, 0, *of)
                    tile(h, 1, *of)


def kernel(x, ctx_512, g_xattn, g_ffn, L0_ffn_Wr, L0_ffn_br, L0_ffn_gate_bias, L0_ffn_Wup, L0_ffn_bup, L0_ffn_Wgate,
           L0_ffn_bgate, L0_ffn_Wdown, L0_ffn_bdown, L0_ffn_Wsu, L0_ffn_bsu, L0_ffn_Wsg, L0_ffn_bsg, L0_ffn_Wsd, L0_ffn_bsd):
    import concourse.bacc as _bacc
    from concourse import mybir as _mybir
    from concourse.bass_utils import run_bass_kernel_spmd as _run

    def joined(routed, shared):
        return np.concatenate([np.asarray(routed), np.asarray(shared)[None]], axis=0)

    layers = [joined(L0_ffn_Wup, L0_ffn_Wsu), joined(L0_ffn_Wgate, L0_ffn_Wsg), joined(L0_ffn_Wdown, L0_ffn_Wsd)]
    wall = np.stack([w.reshape(E_ALL * KT, P, HID) for w in layers], axis=2)
    cols = np.stack([joined(L0_ffn_bup, L0_ffn_bsu), joined(L0_ffn_bgate, L0_ffn_bsg)], axis=1)
    bcol = cols.reshape(E_ALL, 2 * KT, P).transpose(0, 2, 1)
    given = {
        "x": x, "ctx": ctx_512, "g_xattn": g_xattn, "g_ffn": g_ffn, "wr": L0_ffn_Wr, "br": L0_ffn_br, "gbias": L0_ffn_gate_bias,
        "wall": wall, "bcol": bcol, "bdown": joined(L0_ffn_bdown, L0_ffn_bsd),
    }
    nc = _bacc.Bacc("TRN2", target_bir_lowering=False, num_devices=1)
    arrays, args = {}, {}
    for name, value in given.items():
        v = np.ascontiguousarray(value)
        arrays[f"in_{name}"] = v
        args[name] = nc.dram_tensor(f"in_{name}", v.shape, _mybir.dt.from_np(v.dtype), kind="ExternalInput").ap()
    out = nc.dram_tensor("out_0", (NB, P, HID), _mybir.dt.float32, kind="ExternalOutput").ap()
    program(nc, args, out)
    r = _run(nc, [arrays], core_ids=[0])
    return r.results[0]["out_0"]
```

```python
import concourse.bass as bass
from concourse import mybir
from contextlib import ExitStack
import numpy as np

F32 = mybir.dt.float32
F16 = mybir.dt.float16
I32 = mybir.dt.int32
ALU = mybir.AluOpType
ACT = mybir.ActivationFunctionType
AX = mybir.AxisListType

P = 128
NB = 32
HID = 512
KT = HID // P
CTX = 128
NH = 32
NKV = 8
D = HID // NH
UNITS = 4
HPU = NH // UNITS
BLK = NH // 2
E_R = 7
E_ALL = 8
TT = 256
EPS = 1e-5
WS = 64.0
BIG = 3.0e38

SLOT_TILES = NB * P * 2 // TT + E_R - 1
SH_TILES = NB * P // TT
SH_A = SH_TILES // 2
N_TILES = SLOT_TILES + SH_TILES
SH_B0 = SH_A + SLOT_TILES
R_COLS = SLOT_TILES * TT // P
EARLY = NB * SH_A // SH_TILES
SB = 4
XC = 8


ROOTS = (0, 1)


def need(eng, sem, value):
    if isinstance(value, int) and value <= 0:
        return
    eng.wait_ge(sem, value)


def program(nc, a, out):
    ctx = ExitStack()
    phase = ExitStack()
    with ctx:
        def sb(name, shape, dt, where=ctx):
            return where.enter_context(nc.sbuf_tensor(name, shape, dt))

        def sem(name):
            return ctx.enter_context(nc.semaphore(name))

        wsc = nc.dram_tensor("wsc", (E_ALL * KT, 3, P, 2 * HID), F16, kind="Internal").ap()
        xnd = nc.dram_tensor("xnd", (NB * P, 2 * HID), F16, kind="Internal").ap()
        idd = nc.dram_tensor("idd", (R_COLS * P, 1), F32, kind="Internal").ap()
        ysl = nc.dram_tensor("ysl", (SH_B0 * TT, HID), F32, kind="Internal").ap()

        X = sb("X", [P, NB, HID], F32)
        id16 = sb("id16", [P, P], F16)
        id32 = sb("id32", [P, P], F32)
        tri = sb("tri", [P, P], F16)
        one16 = sb("one16", [P, P], F16)
        gts = sb("gts", [P, 2], F32)
        tg = sb("tg", [P, 2], F32)
        st1 = sb("st1", [P, NB, 6], F32)
        mv1 = sb("mv1", [P, NB, 2], F32)
        ln = sb("ln", [P, 6, NB], F32)
        ln2 = sb("ln2", [P, 6, NB], F32)
        st2 = sb("st2", [P, NB, 6], F32)
        mv2 = sb("mv2", [P, NB, 2], F32)
        eps = sb("eps", [P, 1], F32)
        wr32 = sb("wr32", [P, KT, E_R], F32)
        wrs = sb("wrs", [P, 2, KT, E_R], F16)
        brb = sb("brb", [P, E_R], F32)
        gbb = sb("gbb", [P, E_R], F32)
        idx = sb("idx", [P, R_COLS], I32)
        pos = sb("pos", [P, NB, 2], I32)
        prb = sb("prb", [P, 2, NB], F32)
        etab = sb("etab", [P, N_TILES], I32)
        chg = sb("chg", [P, N_TILES], I32)
        tok = sb("tok", [P, NB], F32)
        idr = sb("idr", [R_COLS, P], F32)
        rpos = sb("rpos", [P, NB, 2], I32)
        sct = sb("sct", [P, 2, SB, 2], I32)
        stk = sb("stk", [P, 2, SB], F32)

        ixr = sb("ixr", [P, 2, 2], I32)
        ixf = sb("ixf", [P, 4, 2], I32)
        msum = sb("msum", [P, NB, 8], F16)
        mx = sb("mx", [P, NB], F32)
        rev8 = sb("rev8", [P, 8], F32)
        sel = sb("sel", [P, 2, NB], F32)
        ex = sb("ex", [P, 2, NB], F32)
        e8 = sb("e8", [P, 6, 8], F32)
        i8 = sb("i8", [P, 2, 8], I32)
        it = sb("it", [P, SLOT_TILES], F32)
        ef = sb("ef", [P, 2, SLOT_TILES], F32)

        with ExitStack() as second:
            def sm(name, shape, dt):
                return sb(name, shape, dt, second)
            x2n = sm("x2n", [P, 4, HID], F32)
            xhl = sm("xhl", [P, 4, 2, HID], F16)
            xhT = sm("xhT", [P, 2, 2 * KT, P], F16)
            gate = sm("gate", [P, NB, 8], F32)
            bia = sm("bia", [P, NB, 8], F32)
            oh = sm("oh", [P, 2, NB, 8], F32)
            r1 = sm("r1", [P, NB, 8], F32)
            r2 = sm("r2", [P, NB, 8], F32)
            r3 = sm("r3", [P, NB, 8], F32)
            rnk = sm("rnk", [P, NB, 8], F32)
        yg = sb("yg", [P, 4, 2, HID], F32)
        ys = sb("ys", [P, 2, HID], F32)
        ob = sb("ob", [P, 4, HID], F32)

        def sa(name, shape, dt):
            return sb(name, shape, dt, phase)

        C = sa("C", [P, NB, NKV * D], F32)
        xn32 = sa("xn32", [P, 2, HID], F32)
        qcat = sa("qcat", [P, 2, NH, 4, D], F16)
        kcat = sa("kcat", [P, 4, NKV, 2, 4, D], F16)
        qT = sa("qT", [P, 2, BLK, P], F16)
        kT = sa("kT", [P, 2, NKV, P], F16)
        negm = sa("negm", [P, 2, 2, BLK // 2], F16)
        negT = sa("negT", [BLK, 2, P], F16)
        Pt = sa("Pt", [P, 2, HPU, P], F32)
        Ps = sa("Ps", [P, UNITS, 2, HPU, P], F16)
        rec = sa("rec", [P, 2, NH // 2], F32)
        att = sa("att", [P, 2, HID], F32)
        wst = sa("wst", [P, 2, 3, HID], F32)
        whl = sa("whl", [P, 2, 3, 2, HID], F16)
        phase.close()
        wb = sb("wb", [P, 2, 3, KT, 2, HID], F16)
        bb = sb("bb", [P, 2, 2, KT], F32)
        bd = sb("bd", [P, 2, HID], F32)
        xs = sb("xs", [P, 2, 2, 2 * HID], F16)
        xT = sb("xT", [P, 2, 2, KT, TT], F16)
        u32 = sb("u32", [P, 2, KT, TT], F32)
        uhl = sb("uhl", [P, 2, KT, TT], F16)
        sl = sb("sl", [P, KT, TT], F32)
        g32 = sb("g32", [P, KT, TT], F32)
        ghl = sb("ghl", [P, 2, KT, TT], F16)
        yb = sb("yb", [P, 2, 2, HID], F32)

        PS = [ctx.enter_context(nc.psum_tensor(f"PS{i}", [P, 2, 512], F32)) for i in range(4)]

        S = {}
        for n in ("const_in wr_in id_ready vone tanh_done var1 std1 ln1_ready chain chainp "
                  "xn_ready kh_ready qh_ready k_split q_split tk_done tq0_done tq1_done kT_ready qT0_ready qT1_ready "
                  "plo_g plo_v m_done max_done negx_done negT_ready t_done exp_done pv_done att_ready x1_ready rec_done st2_ready "
                  "w64_ready whi_ready wlo_ready "
                  "var2 std2 ln2_ready x2n_ready x2h_ready x2l_ready t2_done x2T_ready gate_done wrs_ready wrh_ready "
                  "rt_mask rt_cnt rt_sel rt_exp lg_read rnk_read rt_pos idz id_load idT idx_ready phaseC "
                  "xt_done xTa_ready xTv_ready l1_done l2_done l3_done u_ready uh_ready ul_ready s_ready g_ready gh_ready gl_ready y_ready "
                  "ix_ready sct_ready cx shared_in").split():
            S[n] = sem(n)
        neg_in = [sem(f"neg_in{j}") for j in range(2)]
        x_in = [sem(f"x_in{c}") for c in range(XC)]
        c_in = [sem(f"c_in{c}") for c in range(2)]
        w_in = [sem(f"w_in{j}") for j in range(2)]
        w_out = [sem(f"w_out{j}") for j in range(2)]
        x2_out = [sem(f"x2_out{j}") for j in range(4)]
        wl_in = [[sem(f"wl_in{l}{j}") for j in range(2)] for l in range(3)]
        bi_in = [sem(f"bi_in{j}") for j in range(2)]
        xs_in = [sem(f"xs_in{j}") for j in range(2)]
        xg_in = [sem(f"xg_in{j}") for j in range(2)]
        y_out = [sem(f"y_out{j}") for j in range(2)]
        scat = [sem(f"scat{j}") for j in range(2)]
        yg_in = [sem(f"yg_in{j}") for j in range(2)]
        ys_in = [sem(f"ys_in{j}") for j in range(2)]
        added = [sem(f"added{j}") for j in range(2)]
        o_out = [sem(f"o_out{j}") for j in range(2)]
        block = ctx.enter_context(nc.Block())

        Mb, Tb = PS[0], PS[1]
        Rb = PS[2]
        Ob = PS[3]
        Rb16 = [Rb[:, j, :].bitcast(F16).rearrange("p (n c) -> p n c", c=P) for j in range(2)]
        Obv = [Ob[:, j, 0:(NH // 2) * (D + 1)].rearrange("p (h c) -> p h c", c=D + 1) for j in range(2)]
        NT = [Ob[0:BLK, 1 - j, 384:384 + P // 2].bitcast(F16) for j in range(2)]
        LG = PS[0][:, 0, 0:NB * 8].rearrange("p (b e) -> p b e", e=8)

        def over_batches(eng, body):
            body(0, 0, 0)
            body(0, 1, 1)
            with eng.Fori(0, (NB - 4) // 4) as i:
                for k in range(4):
                    body(2 * i + 1 + k // 2, k % 2, (k + 2) % 4)
            body(NB // 2 - 1, 0, NB % 4 + 2)
            body(NB // 2 - 1, 1, NB % 4 + 3)

        def follow(half, par, quad, n):
            b = par + n
            if isinstance(half, int) and 2 * half + b >= NB:
                return None
            return half + b // 2, b % 2, (quad + n) % 4

        def number(half, par):
            return 2 * half + par

        def loads(half):
            if isinstance(half, int):
                return min(max(1, half - SH_A // 2 + 2), SLOT_TILES // 2 + 2)
            return half - SH_A // 2 + 2

        def tokens(half, shared=None):
            if shared is None:
                shared = not SH_A // 2 <= half < SH_B0 // 2
            if not shared:
                return xg_in, 32 * (half - SH_A // 2 + 1)
            late = isinstance(half, int) and half < SH_A // 2 or shared == "early"
            return xs_in, 32 * (half + 1 if late else half - SLOT_TILES // 2 + 1)

        def over_tiles(tile):
            first, second = SH_A // 2, SH_B0 // 2
            peeled = [0], [first - 1], [second - 1, second], [N_TILES // 2 - 1]
            loops = [(lambda h: 1, lambda h: tokens(h, "early")), (loads, lambda h: tokens(h, False)),
                     (lambda h: loads(N_TILES), lambda h: tokens(h, "late"))]
            for n, halves in enumerate(peeled):
                for half in halves:
                    for par in range(2):
                        tile(half, par, loads, tokens)
                if n < 3:
                    yield halves[-1] + 1, peeled[n + 1][0], *loops[n]

        @block.sync
        def _(sp):
            def load_w(b, par):
                sp.dma_start(wst[:, par, :, :], a["wall"][b]).then_inc(w_in[par], 16)

            xv = a["x"].rearrange("b p d -> p b d")
            n = NB // XC
            ctxv = a["ctx"].rearrange("b t d -> t b d")

            def load_rows(cs):
                for c in cs:
                    sp.dma_start(X[:, c * n:(c + 1) * n, :], xv[:, c * n:(c + 1) * n, :]).then_inc(x_in[c], 16)
            load_rows([0])
            sp.dma_start(C[:, 0:n, :], ctxv[:, 0:n, :]).then_inc(c_in[0], 16)
            load_w(0, 0)
            load_w(1, 1)
            sp.dma_start(gts[:, 0:1], a["g_xattn"].unsqueeze(0).to_broadcast([P, 1])).then_inc(S["const_in"], 16)
            sp.dma_start(gts[:, 1:2], a["g_ffn"].unsqueeze(0).to_broadcast([P, 1])).then_inc(S["const_in"], 16)
            sp.dma_start(brb[:, :], a["br"].unsqueeze(0).to_broadcast([P, E_R])).then_inc(S["const_in"], 16)
            sp.dma_start(gbb[:, :], a["gbias"].unsqueeze(0).to_broadcast([P, E_R])).then_inc(S["const_in"], 16)
            sp.dma_start(wr32[:, :, :], a["wr"].rearrange("(k p) e -> p k e", p=P)).then_inc(S["wr_in"], 16)
            load_rows([1, 2, 3])

            def neg_rows(half, par, pair):
                sp.wait_ge(S["negT_ready"], 2 * number(half, par) + pair + 1)
                sp.dma_start(qT[3 * D::64, par, BLK // 2 * pair:BLK // 2 * (pair + 1), :],
                             negT[:, pair, :]).then_inc(neg_in[pair], 16)

            def store_w(half, par, last):
                b = number(half, par)
                sp.wait_ge(S["wlo_ready"], b + 1)
                sp.dma_start(wsc[bass.ds(b, 1)].rearrange("o l p r -> (o p) l r"),
                             whl[:, par, :, :, :].rearrange("p l h c -> p l (h c)")).then_inc(w_out[par], 16)
                if not last:
                    load_w(b + 2, par)

            neg_rows(0, 0, 0)
            load_rows([4, 5])
            sp.dma_start(C[:, n:NB, :], ctxv[:, n:NB, :]).then_inc(c_in[1], 16)

            def body(half, par, quad):
                nx = follow(half, par, quad, 1)
                neg_rows(half, par, 1)
                if isinstance(half, int) and number(half, par) == 0:
                    load_rows([6, 7])
                if not (isinstance(half, int) and number(half, par) == 0):
                    pv = (half - 1, 1) if par == 0 else (half, 0)
                    store_w(*pv, nx is None)
                if nx is not None:
                    neg_rows(*nx[:2], 0)
            over_batches(sp, body)
            def expert(i):
                return sp.value_load(etab[0:1, bass.ds(i, 1)], min_val=0, max_val=E_ALL - 1)

            def other(i):
                return {"cond": sp.value_load(chg[0:1, bass.ds(i, 1)], min_val=0, max_val=1)}

            def load_layer(l, e, par, cond):
                sp.dma_start(wb[:, par, l, :, :, :].rearrange("p k h c -> p k (h c)"),
                             wsc.rearrange("(e k) l p r -> e l p k r", k=KT)[bass.ds(e, 1), l].rearrange("o p k r -> (o p) k r"), **cond).then_inc(wl_in[l][par], 16)

            def load_bias(e, par, cond):
                sp.dma_start(bb[:, par, :, :].rearrange("p l k -> p (l k)"),
                             a["bcol"][bass.ds(e, 1)].rearrange("o p r -> (o p) r"), **cond).then_inc(bi_in[par], 16)
                sp.dma_start(bd[:, par, :], a["bdown"][bass.ds(e, 1), :].to_broadcast([P, HID]), **cond).then_inc(bi_in[par], 16)

            def store_y(i, par):
                sp.wait_ge(S["y_ready"], 2 * i + 2)
                sp.dma_start(ysl[bass.ds(i * TT, TT), :].rearrange("(t p) c -> p t c", p=P), yb[:, par, :, :]).then_inc(y_out[par], 16)

            def load_x(i, par, b):
                need(sp, S["xt_done"], 2 * i - 2)
                for t in range(2):
                    sp.dma_start(xs[:, par, t, :], xnd[bass.ds((b + t) * P, P), :]).then_inc(xs_in[par], 16)

            always = {}

            def first_layer(l, par):
                load_layer(l, E_R, par, always)
                if l == 0:
                    load_bias(E_R, par, always)

            def store_x2(i):
                for r in range(4):
                    sp.wait_ge(S["x2l_ready"], 4 * i + r + 1)
                    sp.dma_start(xnd[bass.ds((4 * i + r) * P, P), :], xhl[:, r, :, :].rearrange("p h c -> p (h c)")).then_inc(x2_out[r], 16)
            store_x2(0)
            store_w(NB // 2 - 1, 1, True)
            store_x2(1)
            sp.wait_ge(S["x1_ready"], NB)
            for par in range(2):
                sp.wait_ge(w_out[par], 16 * (NB // 2))
            for l in range(3):
                first_layer(l, 0)
                store_x2(l + 2)
            with sp.Fori(5, NB // 4 - 1) as i:
                store_x2(i)
            for r in range(4):
                sp.wait_ge(x2_out[r], 16)
            for i in range(2):
                load_x(i, i, 2 * i)
            store_x2(NB // 4 - 1)
            for l in range(3):
                first_layer(l, 1)
            for j in range(4):
                sp.wait_ge(x2_out[j], 16 * (NB // 4))

            with sp.Fori(0, SH_A // 2 - 1) as h:
                for par in range(2):
                    load_x(2 * h + par + 2, par, 4 * h + 2 * par + 4)
                    store_y(2 * h + par, par)

            def turn(i, par, cond2, cond3, xb=None):
                e2 = expert(i + 2)
                k2 = cond2(i + 2)
                if cond3 is not None:
                    e3 = expert(i + 3)
                    k3 = cond3(i + 3)
                sp.wait_ge(S["l2_done"], 2 * i + 2)
                load_layer(1, e2, par, k2)
                if xb is not None:
                    load_x(i + 2, par, xb)
                if cond3 is not None:
                    sp.wait_ge(S["l1_done"], 2 * i + 4)
                    load_layer(0, e3, 1 - par, k3)
                sp.wait_ge(S["l3_done"], 2 * i + 2)
                load_layer(2, e2, par, k2)
                store_y(i, par)
                load_bias(e2, par, k2)

            def yes(i):
                return always

            sp.wait_ge(S["phaseC"], 1)
            e = expert(SH_A)
            sp.wait_ge(S["l1_done"], 2 * SH_A - 2)
            load_layer(0, e, 0, always)
            turn(SH_A - 2, 0, yes, yes)
            turn(SH_A - 1, 1, yes, other)
            for par in range(2):
                sp.wait_ge(y_out[par], 16 * (SH_A // 2))

            def early_row(n, par):
                need(sp, S["shared_in"], 2 * n + par - 1)
                sp.dma_start(ys[:, par, :], ysl[bass.ds((2 * n + par) * P, P), :]).then_inc(ys_in[par], 16)
            for par in range(2):
                early_row(0, par)
            first = SH_A // 2
            with sp.Fori(first, first + EARLY // 2 - 1) as h:
                for par in range(2):
                    turn(2 * h + par, par, other, other)
                    early_row(h - first + 1, par)
            with sp.Fori(first + EARLY // 2 - 1, SH_B0 // 2 - 1) as h:
                for par in range(2):
                    turn(2 * h + par, par, other, other)
            turn(SH_B0 - 2, 0, other, other, EARLY)
            turn(SH_B0 - 1, 1, other, None, EARLY + 2)

            def put(n, par):
                sp.wait_ge(added[par], 2 * n + 2)
                sp.dma_start(out[bass.ds(4 * n + 2 * par, 2)].rearrange("b p c -> p b c"), ob[:, 2 * par:2 * par + 2, :]).then_inc(o_out[par], 16)

            load_x(SH_B0 + 2, 0, EARLY + 4)
            load_x(SH_B0 + 3, 1, EARLY + 6)
            put(0, 0)
            with sp.Fori(0, (N_TILES - SH_B0) // 2 - 2) as h:
                for par in range(2):
                    load_x(SH_B0 + 2 * h + par + 4, par, EARLY + 4 * h + 2 * par + 8)
                    put(2 * h + par, 1)
                    put(2 * h + par + 1, 0)
            for n in range(N_TILES - SH_B0 - 4, NB // 4 - 1):
                put(n, 1)
                put(n + 1, 0)
            put(NB // 4 - 1, 1)
            for par in range(2):
                sp.wait_ge(o_out[par], 16 * (NB // 4))

        @block.gpsimd
        def _(g):
            cp = [0]

            def link(ins):
                cp[0] += 1
                ins.then_inc(S["chainp"], 1)
                g.wait_ge(S["chainp"], cp[0])
            g.memset(eps[:, :], EPS).then_inc(S["id_ready"], 1)
            link(g.memset(id32[:, :], 0.0))
            link(g.memset(one16[:, :], 1.0))
            g.affine_select(out=id32[:, :], in_=id32[:, :], compare_op=ALU.not_equal, fill=1.0, base=0,
                            pattern=[[-1, P]], channel_multiplier=1).then_inc(S["id_ready"], 1)
            g.wait_ge(S["id_ready"], 2)
            g.tensor_copy(id16[:, :], id32[:, :]).then_inc(S["id_ready"], 1)
            g.affine_select(out=tri[:, :], in_=one16[:, :], compare_op=ALU.is_gt, fill=0.0, base=0,
                            pattern=[[1, P]], channel_multiplier=-1).then_inc(S["id_ready"], 1)
            for par in range(2):
                g.memset(qcat[:, par, :, 3, :], 0.0).then_inc(S["vone"], 1)
            for quad in range(4):
                g.memset(kcat[:, quad, :, :, 3, :], 0.0).then_inc(S["vone"], 1)
            g.wait_ge(S["vone"], 6)
            for quad in range(4):
                g.memset(kcat[:, quad, :, :, 3, 0:1], 1.0).then_inc(S["vone"], 1)
            g.iota(tok[:, :], pattern=[[P, NB]], base=0, channel_multiplier=1, allow_small_or_imprecise_dtypes=True).then_inc(S["id_ready"], 1)
            g.iota(rev8[:, :], pattern=[[-1, 8]], base=8, channel_multiplier=0, allow_small_or_imprecise_dtypes=True).then_inc(S["id_ready"], 1)
            g.iota(it[:, :], pattern=[[1, SLOT_TILES]], base=0, channel_multiplier=0, allow_small_or_imprecise_dtypes=True).then_inc(S["id_ready"], 1)
            g.memset(etab[:, 0:SH_A], E_R).then_inc(S["idx_ready"], 1)
            g.memset(etab[:, SH_B0:N_TILES], E_R).then_inc(S["idx_ready"], 1)
            link(g.memset(idr[:, :], 0.0))
            g.dma_start(idd.rearrange("(c p) o -> c (p o)", p=P), idr[:, :]).then_inc(S["idz"], 16)

            def split_kq(half, par, quad):
                b = 2 * half + par
                g.wait_ge(S["kh_ready"], b + 1)
                cv = C[:, bass.ds(b, 1), :].rearrange("p o (h d) -> p (o h) d", d=D)
                g.tensor_tensor(kcat[:, quad, :, :, 1, :], cv.unsqueeze(2).to_broadcast([P, NKV, 2, D]),
                                kcat[:, quad, :, :, 0, :], ALU.subtract).then_inc(S["k_split"], 1)
                g.wait_ge(S["qh_ready"], b + 1)
                g.wait_ge(S["xn_ready"], b + 1)
                g.tensor_tensor(qcat[:, par, :, 0, :], xn32[:, par, :].rearrange("p (h d) -> p h d", d=D),
                                qcat[:, par, :, 1, :], ALU.subtract).then_inc(S["q_split"], 1)

            def low_p(half, par, u):
                g.wait_ge(S["exp_done"], 2 * (UNITS * (2 * half + par) + u + 1))
                g.tensor_tensor(Ps[:, u, 1, :, :], Pt[:, u % 2, :, :], Ps[:, u, 0, :, :], ALU.subtract).then_inc(S["plo_g"], 1)

            def residual(half, par):
                b = 2 * half + par
                g.wait_ge(S["att_ready"], 2 * b + 2)
                xv = X[:, bass.ds(b, 1), :].rearrange("p o c -> p (o c)")
                g.tensor_tensor(xv, xv, att[:, par, :], ALU.add).then_inc(S["x1_ready"], 1)

            def weights_lo(half, par):
                b = 2 * half + par
                g.wait_ge(S["whi_ready"], b + 1)
                g.tensor_tensor(whl[:, par, :, 1, :], wst[:, par, :, :], whl[:, par, :, 0, :], ALU.subtract).then_inc(S["wlo_ready"], 1)

            g.wait_ge(c_in[0], 16)
            g.wait_ge(S["ln1_ready"], 1)
            split_kq(0, 0, 0)
            split_kq(0, 1, 1)

            def body(half, par, quad):
                low_p(half, par, 1)
                if not (isinstance(half, int) and number(half, par) == 0):
                    residual(*((half - 1, 1) if par == 0 else (half, 0)))
                after = follow(half, par, quad, 2)
                if after is not None:
                    split_kq(*after)
                low_p(half, par, 3)
                if not (isinstance(half, int) and number(half, par) == NB - 1):
                    weights_lo(half, par)
            over_batches(g, body)
            residual(NB // 2 - 1, 1)

            def low2(i):
                for k in range(4):
                    g.wait_ge(S["x2n_ready"], 4 * i + k + 1)
                    g.wait_ge(S["x2h_ready"], 4 * i + k + 1)
                    g.tensor_tensor(xhl[:, k, 1, :], x2n[:, k, :], xhl[:, k, 0, :], ALU.subtract).then_inc(S["x2l_ready"], 1)
            with g.Fori(0, NB // 4) as i:
                low2(i)

            g.wait_ge(S["idz"], 16)
            g.wait_ge(S["rt_pos"], 1)
            g.wait_ge(S["id_ready"], 7)

            def scatter(h, first):
                for j in range(2):
                    if not first:
                        g.wait_ge(scat[j], 16 * 2 * SB * h)
                        g.nop(nofuse=True)
                    g.tensor_copy(sct[:, j, :, :], rpos[:, bass.ds((2 * h + j) * SB, SB), :]).then_inc(S["sct_ready"], 1)
                    g.tensor_copy(stk[:, j, :], tok[:, bass.ds((2 * h + j) * SB, SB)]).then_inc(S["sct_ready"], 1)
                    g.wait_ge(S["sct_ready"], 4 * h + 2 * j + 2)
                    g.nop(nofuse=True)
                    for b in range(SB):
                        for k in range(2):
                            g.indirect_dma_start(out=idd, out_offset=bass.IndirectOffsetOnAxis(ap=sct[:, j, b, k:k + 1], axis=0),
                                                 in_=stk[:, j, b:b + 1], in_offset=None).then_inc(scat[j], 16)
            scatter(0, True)
            with g.Fori(1, NB // SB // 2) as h:
                scatter(h, False)
            for j in range(2):
                g.wait_ge(scat[j], 16 * NB)
            g.dma_start(idr[:, :], idd.rearrange("(c p) o -> c (p o)", p=P)).then_inc(S["id_load"], 16)
            for j in range(4):
                g.wait_ge(x2_out[j], 16 * (NB // 4))
            g.wait_ge(S["phaseC"], 1)
            g.wait_ge(S["idx_ready"], 3)

            def gather(i, par):
                g.wait_ge(S["xt_done"], 2 * i - 2)
                g.nop(nofuse=True)
                g.tensor_copy(ixr[:, par, :], idx[:, bass.ds(2 * (i - SH_A), 2)]).then_inc(S["ix_ready"], 1)
                g.wait_ge(S["ix_ready"], i - SH_A + 1)
                g.nop(nofuse=True)
                for t in range(2):
                    g.indirect_dma_start(out=xs[:, par, t, :], out_offset=None, in_=xnd,
                                         in_offset=bass.IndirectOffsetOnAxis(ap=ixr[:, par, t:t + 1], axis=0)).then_inc(xg_in[par], 16)
            with g.Fori(SH_A // 2, SH_B0 // 2) as h:
                for par in range(2):
                    gather(2 * h + par, par)

            for par in range(2):
                g.wait_ge(y_out[par], 16 * (SH_B0 // 2))

            def fetch(n):
                for par in range(2):
                    if not isinstance(n, int):
                        g.wait_ge(added[par], 2 * n)
                        g.nop(nofuse=True)
                    g.tensor_copy(ixf[:, 2 * par:2 * par + 2, :], pos[:, bass.ds(4 * n + 2 * par, 2), :]).then_inc(S["ix_ready"], 1)
                    g.wait_ge(S["ix_ready"], SLOT_TILES + 2 * n + par + 1)
                    g.nop(nofuse=True)
                    for k in range(2):
                        for t in range(2):
                            slot = 2 * par + t
                            g.indirect_dma_start(out=yg[:, slot, k, :], out_offset=None, in_=ysl,
                                                 in_offset=bass.IndirectOffsetOnAxis(ap=ixf[:, slot, k:k + 1], axis=0)).then_inc(yg_in[par], 16)
            fetch(0)
            with g.Fori(1, NB // 4) as n:
                fetch(n)

        @block.scalar
        def _(act):
            act.wait_ge(S["const_in"], 64)
            act.activation(tg[:, :], gts[:, :], ACT.Tanh).then_inc(S["tanh_done"], 1)
            act.wait_ge(S["id_ready"], 1)

            def root1(n, bs):
                act.wait_ge(S["var1"], n)
                act.activation(ln[:, 2, bs], mv1[:, bs, 1], ACT.Sqrt, bias=eps[:, 0:1]).then_inc(S["std1"], 1)
            root1(1, slice(0, NB // XC))
            act.wait_ge(c_in[0], 16)
            act.wait_ge(S["ln1_ready"], 1)

            def high(half, par, quad):
                b = 2 * half + par
                need(act, S["pv_done"], UNITS * (b - 3))
                cv = C[:, bass.ds(b, 1), :].rearrange("p o (h d) -> p (o h) d", d=D)
                for dup in range(2):
                    ins = act.activation(kcat[:, quad, :, dup, 0:3:2, :], cv.unsqueeze(2).to_broadcast([P, NKV, 2, D]), ACT.Copy)
                ins.then_inc(S["kh_ready"], 1)
                need(act, S["tq1_done"], b - 1)
                act.activation(qcat[:, par, :, 1:3, :], X[:, bass.ds(b, 1), :].rearrange("p o (h d) -> p (o h) d", d=D).unsqueeze(2).to_broadcast([P, NH, 2, D]),
                               ACT.Identity, bias=ln[:, 1, bass.ds(b, 1)], scale=ln[:, 0, bass.ds(b, 1)]).then_inc(S["qh_ready"], 1)

            def evac_q0(half, par):
                b = 2 * half + par
                act.wait_ge(S["tq0_done"], b + 1)
                act.activation(qT[:, par, 0:8, :], Rb16[1], ACT.Copy).then_inc(S["qT0_ready"], 1)

            def exps(half, par, u):
                n = UNITS * (2 * half + par) + u
                need(act, S["pv_done"], n - 3)
                need(act, S["plo_g"] if u % 2 else S["plo_v"], 2 * number(half, par) + u // 2)
                for odd in range(2):
                    act.wait_ge(S["t_done"], 2 * n + odd + 1)
                    heads = slice(odd * 4, odd * 4 + 4)
                    act.activation(Ps[:, u, 0, heads, :].rearrange("p h s -> p (h s)"), Tb[:, odd, :], ACT.Exp, scale=float(D) ** -0.5)
                    act.activation(Pt[:, u % 2, heads, :].rearrange("p h s -> p (h s)"), Tb[:, odd, :], ACT.Exp, scale=float(D) ** -0.5).then_inc(S["exp_done"], 1)

            def weights_hi(half, par):
                b = 2 * half + par
                act.wait_ge(S["w64_ready"], b + 1)
                if not (isinstance(b, int) and b < 2):
                    act.wait_ge(w_out[par], 16 * half)
                act.activation(whl[:, par, :, 0, :], wst[:, par, :, :], ACT.Copy).then_inc(S["whi_ready"], 1)

            high(0, 0, 0)
            evac_q0(0, 0)
            high(0, 1, 1)
            act.wait_ge(S["wrs_ready"], 1)
            act.activation(wrs[:, 0, :, :], wr32[:, :, :], ACT.Copy).then_inc(S["wrh_ready"], 1)

            def body(half, par, quad):
                nx = follow(half, par, quad, 1)
                after = follow(half, par, quad, 2)
                if nx is not None:
                    evac_q0(*nx[:2])
                exps(half, par, 0)
                exps(half, par, 1)
                if isinstance(half, int) and (half, par) == ROOTS:
                    root1(2, slice(NB // XC, NB))
                    act.wait_ge(S["ln1_ready"], 2)
                    act.wait_ge(c_in[1], 16)
                if after is not None:
                    high(*after)
                exps(half, par, 2)
                weights_hi(half, par)
                exps(half, par, 3)
            over_batches(act, body)

            def root2(n, bs):
                act.wait_ge(S["var2"], n)
                act.activation(ln2[:, 2, bs], mv2[:, bs, 1], ACT.Sqrt, bias=eps[:, 0:1]).then_inc(S["std2"], 1)
            root2(1, slice(0, NB - 1))
            act.wait_ge(S["ln2_ready"], 1)

            def norm2(i, first):
                for k in range(4):
                    b = 4 * i + k
                    if not first:
                        act.wait_ge(S["t2_done"], b - 3)
                        act.wait_ge(x2_out[k], 16 * i)
                    act.activation(xhl[:, k, 0, :], X[:, bass.ds(b, 1), :].rearrange("p o c -> p (o c)"),
                                   ACT.Identity, bias=ln2[:, 1, bass.ds(b, 1)], scale=ln2[:, 0, bass.ds(b, 1)]).then_inc(S["x2h_ready"], 1)
            norm2(0, True)
            root2(2, slice(NB - 1, NB))
            act.wait_ge(S["ln2_ready"], 2)
            with act.Fori(1, NB // 4) as i:
                norm2(i, False)

            def evac_x(i, par):
                act.wait_ge(S["xt_done"], 2 * i + 1)
                need(act, S["l1_done"], 2 * i - 2)
                act.activation(xT[:, par, :, :, 0:P], PS[3][:, 0, :].bitcast(F16).rearrange("p (h k c) -> p h k c", h=2, k=KT),
                               ACT.Copy).then_inc(S["xTa_ready"], 1)

            def up_out(i, par, n_loads):
                for hf in range(2):
                    act.wait_ge(S["l1_done"], 2 * i + hf + 1)
                    if hf == 0:
                        act.wait_ge(bi_in[par], 32 * n_loads)
                        need(act, S["g_ready"], 2 * i - 2)
                    for m in range(2 * hf, 2 * hf + 2):
                        ins = act.activation(u32[:, par, m, :], PS[0][:, hf, bass.ds((m % 2) * TT, TT)], ACT.Identity,
                                             bias=bb[:, par, 0, m:m + 1], scale=1.0 / WS)
                    ins.then_inc(S["u_ready"], 1)

            def gate_out(i, par):
                for hf in range(2):
                    act.wait_ge(S["l2_done"], 2 * i + hf + 1)
                    need(act, S["g_ready"], 2 * i - 1 + hf)
                    for m in range(2 * hf, 2 * hf + 2):
                        ins = act.activation(sl[:, m, :], PS[1][:, hf, bass.ds((m % 2) * TT, TT)], ACT.Silu,
                                             bias=bb[:, par, 1, m:m + 1], scale=1.0 / WS)
                    ins.then_inc(S["s_ready"], 1)
            evac_x(0, 0)
            up_out(0, 0, 1)
            act.wait_ge(S["rt_sel"], 1)
            act.activation(ex[:, :, :], sel[:, :, :], ACT.Exp).then_inc(S["rt_exp"], 1)

            def tile(half, par, loads_of, tokens_of):
                i = 2 * half + par
                last = isinstance(i, int) and i == N_TILES - 1
                if not last:
                    evac_x(i + 1, 1 - par)
                gate_out(i, par)
                if not last:
                    up_out(i + 1, 1 - par, loads_of(half + par))
            for lo, hi, *of in over_tiles(tile):
                with act.Fori(lo, hi) as h:
                    tile(h, 0, *of)
                    tile(h, 1, *of)

        @block.vector
        def _(v):
            cv = [0]

            def link(ins):
                cv[0] += 1
                ins.then_inc(S["chain"], 1)
                v.wait_ge(S["chain"], cv[0])

            n = NB // XC

            def stats1(c):
                v.wait_ge(x_in[c], 16)
                for b in range(c * n, (c + 1) * n):
                    ins = v.bn_stats(st1[:, b, :], X[:, b, :])
                link(ins)
                for b in range(c * n, (c + 1) * n):
                    ins = v.bn_aggr(mv1[:, b, :], st1[:, b, :])
                return ins

            def rstd(mv, t, bs):
                link(v.reciprocal(t[:, 3, bs], t[:, 2, bs]))
                link(v.tensor_scalar(t[:, 4, bs], mv[:, bs, 1], EPS, None, ALU.add))
                link(v.tensor_tensor(t[:, 4, bs], t[:, 4, bs], t[:, 3, bs], ALU.mult))
                link(v.tensor_tensor(t[:, 4, bs], t[:, 4, bs], t[:, 3, bs], ALU.mult))
                link(v.tensor_scalar(t[:, 4, bs], t[:, 4, bs], -0.5, 1.5, ALU.mult, ALU.add))
                link(v.tensor_tensor(t[:, 0, bs], t[:, 4, bs], t[:, 3, bs], ALU.mult))
                return v.scalar_tensor_tensor(out=t[:, 1, bs], in0=mv[:, bs, 0], scalar=-1.0, in1=t[:, 0, bs], op0=ALU.mult, op1=ALU.mult)
            stats1(0).then_inc(S["var1"], 1)
            v.wait_ge(S["var1"], 1)
            v.wait_ge(S["std1"], 1)
            rstd(mv1, ln, slice(0, n)).then_inc(S["ln1_ready"], 1)
            v.wait_ge(S["ln1_ready"], 1)
            v.wait_ge(S["tanh_done"], 1)

            def late_stats1(part):
                for c in ((1, 2, 3), (4, 5, 6, 7))[part]:
                    ins = stats1(c)
                    if c < XC - 1:
                        link(ins)
                if part == 1:
                    ins.then_inc(S["var1"], 1)
                    v.wait_ge(S["var1"], 2)
                    v.wait_ge(S["std1"], 2)
                    rstd(mv1, ln, slice(n, NB)).then_inc(S["ln1_ready"], 1)
                    v.wait_ge(S["ln1_ready"], 2)
                    v.wait_ge(S["wrh_ready"], 1)
                    v.tensor_tensor(wrs[:, 1, :, :], wr32[:, :, :], wrs[:, 0, :, :], ALU.subtract).then_inc(S["wrs_ready"], 1)

            def norm1(half, par):
                b = 2 * half + par
                need(v, S["q_split"], b - 1)
                v.tensor_scalar(xn32[:, par, :], X[:, bass.ds(b, 1), :].rearrange("p o c -> p (o c)"), ln[:, 0, bass.ds(b, 1)],
                                ln[:, 1, bass.ds(b, 1)], ALU.mult, ALU.add).then_inc(S["xn_ready"], 1)

            def evac_k(half, par):
                b = 2 * half + par
                v.wait_ge(S["tk_done"], b + 1)
                v.tensor_copy(kT[:, par, :, :], Rb16[0]).then_inc(S["kT_ready"], 1)

            def evac_q1(half, par):
                b = 2 * half + par
                v.wait_ge(S["tq1_done"], b + 1)
                v.tensor_copy(qT[:, par, 8:16, :], Rb16[0]).then_inc(S["qT1_ready"], 1)

            def maxes(half, par, u):
                b = number(half, par)
                if u % 2 == 0:
                    need(v, S["negx_done"], 2 * b - 1 + u // 2)
                for odd in range(2):
                    v.wait_ge(S["m_done"], 2 * (UNITS * b + u) + odd + 1)
                    v.tensor_reduce(negm[:, u // 2, odd, u % 2 * 4:u % 2 * 4 + 4], Mb[:, odd, :].rearrange("p (j t) -> p j t", t=CTX),
                                    AX.X, ALU.max, negate=True).then_inc(S["max_done"], 1)

            def evac_neg(half, par, pair):
                b = number(half, par)
                v.wait_ge(S["negx_done"], 2 * b + pair + 1)
                need(v, neg_in[pair], 16 * b)
                v.tensor_copy(negT[:, pair, :], NT[pair]).then_inc(S["negT_ready"], 1)

            def low_p(half, par, u):
                v.wait_ge(S["exp_done"], 2 * (UNITS * (2 * half + par) + u + 1))
                v.tensor_tensor(Ps[:, u, 1, :, :], Pt[:, u % 2, :, :], Ps[:, u, 0, :, :], ALU.subtract).then_inc(S["plo_v"], 1)

            def normalise(half, par, hf):
                b = 2 * half + par
                v.wait_ge(S["pv_done"], UNITS * b + 2 * hf + 2)
                v.reciprocal(rec[:, hf, :], Obv[hf][:, :, D]).then_inc(S["rec_done"], 1)
                v.wait_ge(S["rec_done"], 4 * b + 2 * hf + 1)
                v.tensor_scalar(rec[:, hf, :], rec[:, hf, :], tg[:, 0:1], None, ALU.mult).then_inc(S["rec_done"], 1)
                v.wait_ge(S["rec_done"], 4 * b + 2 * hf + 2)
                need(v, S["x1_ready"], b - 1)
                v.tensor_tensor(att[:, par, hf * 256:(hf + 1) * 256].rearrange("p (h d) -> p h d", d=D), Obv[hf][:, :, 0:D],
                                rec[:, hf, :].unsqueeze(2).to_broadcast([P, NH // 2, D]), ALU.mult).then_inc(S["att_ready"], 1)

            def stats2(half, par):
                b = 2 * half + par
                v.wait_ge(S["x1_ready"], b + 1)
                v.bn_stats(st2[:, bass.ds(b, 1), :].rearrange("p o c -> p (o c)"),
                           X[:, bass.ds(b, 1), :].rearrange("p o c -> p (o c)")).then_inc(S["st2_ready"], 1)

            def weights64(half, par):
                b = 2 * half + par
                v.wait_ge(w_in[par], 16 * (half + 1))
                v.tensor_scalar(wst[:, par, :, :], wst[:, par, :, :], WS, None, ALU.mult).then_inc(S["w64_ready"], 1)

            norm1(0, 0)
            norm1(0, 1)
            v.wait_ge(S["wr_in"], 16)
            v.tensor_scalar(wr32[:, :, :], wr32[:, :, :], WS, None, ALU.mult).then_inc(S["wrs_ready"], 1)
            evac_k(0, 0)
            evac_q1(0, 0)
            maxes(0, 0, 0)
            maxes(0, 0, 1)
            evac_neg(0, 0, 0)
            maxes(0, 0, 2)

            def body(half, par, quad):
                nx = follow(half, par, quad, 1)
                after = follow(half, par, quad, 2)
                pv = (half - 1, 1) if par == 0 else (half, 0)
                start = isinstance(half, int) and number(half, par) == 0
                if not start:
                    normalise(*pv, 0)
                if nx is not None:
                    evac_k(*nx[:2])
                maxes(half, par, 3)
                if isinstance(half, int) and number(half, par) < 2:
                    late_stats1(number(half, par))
                if after is not None:
                    norm1(*after[:2])
                evac_neg(half, par, 1)
                weights64(half, par)
                low_p(half, par, 0)
                if nx is not None:
                    maxes(*nx[:2], 0)
                    evac_q1(*nx[:2])
                if not start:
                    normalise(*pv, 1)
                if nx is not None:
                    maxes(*nx[:2], 1)
                if nx is not None:
                    evac_neg(*nx[:2], 0)
                low_p(half, par, 2)
                if not start:
                    stats2(*pv)
                if nx is not None:
                    maxes(*nx[:2], 2)
            over_batches(v, body)
            def stats_to(n, bs):
                v.wait_ge(S["st2_ready"], bs.stop)
                for b in range(bs.start, bs.stop):
                    ins = v.bn_aggr(mv2[:, b, :], st2[:, b, :])
                ins.then_inc(S["var2"], 1)
                v.wait_ge(S["std2"], n)
                v.wait_ge(S["var2"], n)
                rstd(mv2, ln2, bs).then_inc(S["ln2_ready"], 1)
                v.wait_ge(S["ln2_ready"], n)
            normalise(NB // 2 - 1, 1, 0)
            stats_to(1, slice(0, NB - 1))

            def norm2(b, k):
                need(v, S["x2l_ready"], b - 3)
                v.tensor_scalar(x2n[:, k, :], X[:, bass.ds(b, 1), :].rearrange("p o c -> p (o c)"), ln2[:, 0, bass.ds(b, 1)],
                                ln2[:, 1, bass.ds(b, 1)], ALU.mult, ALU.add).then_inc(S["x2n_ready"], 1)

            def evac_x2(b, k):
                v.wait_ge(S["t2_done"], b + 1)
                need(v, S["gate_done"], b - 1)
                v.tensor_copy(xhT[:, k % 2, :, :], Rb16[k % 2]).then_inc(S["x2T_ready"], 1)
            for b in range(3):
                norm2(b, b)
            normalise(NB // 2 - 1, 1, 1)
            stats2(NB // 2 - 1, 1)
            stats_to(2, slice(NB - 1, NB))
            v.wait_ge(S["whi_ready"], NB)
            v.wait_ge(S["wlo_ready"], NB - 1)
            v.tensor_tensor(whl[:, 1, :, 1, :], wst[:, 1, :, :], whl[:, 1, :, 0, :], ALU.subtract).then_inc(S["wlo_ready"], 1)

            def four(i, last):
                for k in range(4):
                    if not (last and k > 0):
                        norm2(4 * i + k + 3, (k + 3) % 4)
                    evac_x2(4 * i + k, k)
            four(0, False)
            with v.Fori(1, NB // 4 - 1) as i:
                four(i, False)
            four(NB // 4 - 1, True)

            def over_b(ap):
                return ap.unsqueeze(1).to_broadcast([P, NB, ap.shape[-1]])

            def over_e(ap):
                return ap.unsqueeze(2).to_broadcast([P, NB, 8])

            def logits():
                link(v.memset(gate[:, :, :], 0.0))
                link(v.memset(bia[:, :, :], -BIG))
                v.wait_ge(S["gate_done"], NB)
                v.scalar_tensor_tensor(out=gate[:, :, 0:E_R], in0=LG[:, :, 0:E_R], scalar=1.0 / WS, in1=over_b(brb[:, :]),
                                            op0=ALU.mult, op1=ALU.add).then_inc(S["lg_read"], 1)
                v.wait_ge(S["lg_read"], 1)
                link(v.tensor_tensor(bia[:, :, 0:E_R], gate[:, :, 0:E_R], over_b(gbb[:, :]), ALU.add))

            def choose():
                v.wait_ge(S["id_ready"], 7)
                for k in range(2):
                    link(v.tensor_reduce(mx[:, :], bia[:, :, :], AX.X, ALU.max))
                    link(v.tensor_tensor(r1[:, :, :], bia[:, :, :], over_e(mx[:, :]), ALU.is_equal))
                    link(v.tensor_tensor(r1[:, :, :], r1[:, :, :], over_b(rev8[:, :]), ALU.mult))
                    link(v.tensor_reduce(mx[:, :], r1[:, :, :], AX.X, ALU.max))
                    link(v.tensor_tensor(oh[:, k, :, :], over_b(rev8[:, :]), over_e(mx[:, :]), ALU.is_equal))
                    if k == 0:
                        link(v.scalar_tensor_tensor(out=bia[:, :, :], in0=oh[:, 0, :, :], scalar=-BIG, in1=bia[:, :, :], op0=ALU.mult, op1=ALU.add))
                    link(v.tensor_tensor(r2[:, :, :], oh[:, k, :, :], gate[:, :, :], ALU.mult))
                    link(v.tensor_reduce(sel[:, k, :], r2[:, :, :], AX.X, ALU.add))
                v.tensor_tensor(msum[:, :, :], oh[:, 0, :, :], oh[:, 1, :, :], ALU.add).then_inc(S["rt_mask"], 1)
                link(v.tensor_tensor(mx[:, :], sel[:, 0, :], sel[:, 1, :], ALU.max))
                v.tensor_tensor(sel[:, :, :], sel[:, :, :], mx[:, :].unsqueeze(1).to_broadcast([P, 2, NB]), ALU.subtract).then_inc(S["rt_sel"], 1)

            def place():
                v.wait_ge(S["rt_exp"], 1)
                v.wait_ge(S["rt_cnt"], 2)
                CNT = PS[2][:, 1, 0:NB * 8].rearrange("p (b e) -> p b e", e=8)
                RNK = PS[2][:, 0, 0:NB * 8].rearrange("p (b e) -> p b e", e=8)
                link(v.tensor_copy(r1[:, :, :], CNT))
                v.tensor_copy(rnk[:, :, :], RNK).then_inc(S["rnk_read"], 1)
                v.wait_ge(S["rnk_read"], 1)
                src, dst, s = r1, r2, 1
                while s < NB:
                    link(v.tensor_copy(dst[:, 0:s, :], src[:, 0:s, :]))
                    link(v.tensor_tensor(dst[:, s:NB, :], src[:, s:NB, :], src[:, 0:NB - s, :], ALU.add))
                    src, dst, s = dst, (r3 if dst is r2 else r2), 2 * s
                link(v.tensor_scalar(e8[:, 0, :], src[:, NB - 1, :], float(TT - 1), None, ALU.add))
                link(v.tensor_copy(i8[:, 0, :], e8[:, 0, :]))
                link(v.tensor_scalar(i8[:, 1, :], i8[:, 0, :], TT.bit_length() - 1, None, ALU.logical_shift_right))
                link(v.tensor_copy(e8[:, 1, :], i8[:, 1, :]))
                ends, nxt, s = 1, 2, 1
                while s < 8:
                    link(v.tensor_copy(e8[:, nxt, 0:s], e8[:, ends, 0:s]))
                    link(v.tensor_tensor(e8[:, nxt, s:8], e8[:, ends, s:8], e8[:, ends, 0:8 - s], ALU.add))
                    ends, nxt, s = nxt, nxt + 1, 2 * s
                link(v.tensor_tensor(e8[:, 5, :], e8[:, ends, :], e8[:, 1, :], ALU.subtract))
                link(v.tensor_scalar(e8[:, 5, :], e8[:, 5, :], float(TT), None, ALU.mult))
                tot = dst
                link(v.tensor_tensor(tot[:, :, :], src[:, :, :], r1[:, :, :], ALU.subtract))
                link(v.tensor_tensor(tot[:, :, :], tot[:, :, :], over_b(e8[:, 5, :]), ALU.add))
                link(v.tensor_tensor(tot[:, :, :], tot[:, :, :], rnk[:, :, :], ALU.add))
                for k in range(2):
                    link(v.tensor_tensor(r1[:, :, :], tot[:, :, :], oh[:, k, :, :], ALU.mult))
                    link(v.tensor_reduce(sel[:, k, :], r1[:, :, :], AX.X, ALU.add))
                v.tensor_copy(rpos[:, :, :].rearrange("p b k -> p k b"), sel[:, :, :]).then_inc(S["rt_pos"], 1)
                return ends

            def tables(ends):
                v.wait_ge(S["rt_exp"], 1)
                link(v.tensor_tensor(mx[:, :], ex[:, 0, :], ex[:, 1, :], ALU.add))
                link(v.reciprocal(mx[:, :], mx[:, :]))
                link(v.tensor_scalar(mx[:, :], mx[:, :], tg[:, 1:2], None, ALU.mult))
                link(v.tensor_tensor(prb[:, :, :], ex[:, :, :], mx[:, :].unsqueeze(1).to_broadcast([P, 2, NB]), ALU.mult))
                link(v.tensor_scalar(sel[:, :, :], sel[:, :, :], float(SH_A * TT), None, ALU.add))
                link(v.tensor_copy(pos[:, :, :].rearrange("p b k -> p k b"), sel[:, :, :]))
                link(v.memset(ef[:, 0, :], 0.0))
                for e in range(E_R):
                    link(v.scalar_tensor_tensor(out=ef[:, (e + 1) % 2, :], in0=it[:, :], scalar=e8[:, ends, e:e + 1],
                                                in1=ef[:, e % 2, :], op0=ALU.is_ge, op1=ALU.add))
                link(v.tensor_scalar(ef[:, 0, :], ef[:, E_R % 2, :], float(E_R - 1), None, ALU.min))
                link(v.tensor_copy(etab[:, SH_A:SH_B0], ef[:, 0, :]))
                v.wait_ge(S["idx_ready"], 2)
                link(v.tensor_tensor(chg[:, 2:N_TILES], etab[:, 2:N_TILES], etab[:, 0:N_TILES - 2], ALU.not_equal))
                v.memset(mx[:, :], 0.0).then_inc(S["phaseC"], 1)

            def evac_x(i, par):
                v.wait_ge(S["xt_done"], 2 * i + 2)
                need(v, S["l1_done"], 2 * i - 2)
                v.tensor_copy(xT[:, par, :, :, P:TT], PS[3][:, 1, :].bitcast(F16).rearrange("p (h k c) -> p h k c", h=2, k=KT)).then_inc(S["xTv_ready"], 1)

            def split_u(i, par):
                for hf in range(2):
                    ms = slice(2 * hf, 2 * hf + 2)
                    v.wait_ge(S["u_ready"], 2 * i + hf + 1)
                    need(v, S["l2_done"], 2 * i)
                    v.tensor_copy(uhl[:, 0, ms, :], u32[:, par, ms, :]).then_inc(S["uh_ready"], 1)
                    v.wait_ge(S["uh_ready"], 2 * i + hf + 1)
                    v.tensor_tensor(uhl[:, 1, ms, :], u32[:, par, ms, :], uhl[:, 0, ms, :], ALU.subtract).then_inc(S["ul_ready"], 1)

            def gating(i, par):
                for hf in range(2):
                    ms = slice(2 * hf, 2 * hf + 2)
                    v.wait_ge(S["s_ready"], 2 * i + hf + 1)
                    v.tensor_tensor(g32[:, ms, :], sl[:, ms, :], u32[:, par, ms, :], ALU.mult).then_inc(S["g_ready"], 1)
                    v.wait_ge(S["g_ready"], 2 * i + hf + 1)
                    need(v, S["l3_done"], 2 * i)
                    v.tensor_copy(ghl[:, 0, ms, :], g32[:, ms, :]).then_inc(S["gh_ready"], 1)
                    v.wait_ge(S["gh_ready"], 2 * i + hf + 1)
                    v.tensor_tensor(ghl[:, 1, ms, :], g32[:, ms, :], ghl[:, 0, ms, :], ALU.subtract).then_inc(S["gl_ready"], 1)

            def down_out(i, par, stored):
                for t in range(2):
                    v.wait_ge(S["l3_done"], 2 * i + t + 1)
                    if t == 0:
                        need(v, y_out[par], 16 * stored)
                    v.scalar_tensor_tensor(out=yb[:, par, t, :], in0=PS[2][:, t, :], scalar=1.0 / WS, in1=bd[:, par, :],
                                           op0=ALU.mult, op1=ALU.add).then_inc(S["y_ready"], 1)

            def add_shared(b, y):
                xv = X[:, bass.ds(b, 1), :].rearrange("p o c -> p (o c)")
                v.scalar_tensor_tensor(out=xv, in0=y, scalar=tg[:, 1:2], in1=xv, op0=ALU.mult, op1=ALU.add).then_inc(S["shared_in"], 1)

            def add_routed(n, par):
                for k in range(2):
                    for t in range(2):
                        b = 4 * n + 2 * par + t
                        slot = 2 * par + t
                        xv = X[:, bass.ds(b, 1), :].rearrange("p o c -> p (o c)")
                        if k == 0:
                            if t == 0:
                                v.wait_ge(yg_in[par], 64 * (n + 1))
                                v.wait_ge(S["shared_in"], 4 * n + 2 * par + 2)
                            res, done = xv, S["cx"]
                        else:
                            v.wait_ge(S["cx"], 4 * n + 2 * par + t + 1)
                            if t == 0:
                                need(v, o_out[par], 16 * n)
                            res, done = ob[:, slot, :], added[par]
                        v.scalar_tensor_tensor(out=res, in0=yg[:, slot, k, :], scalar=prb[:, k, bass.ds(b, 1)], in1=xv,
                                               op0=ALU.mult, op1=ALU.add).then_inc(done, 1)
            logits()
            evac_x(0, 0)
            choose()
            split_u(0, 0)

            def tile(half, par, stored, early=None, late=None):
                i = 2 * half + par
                last = isinstance(i, int) and i == N_TILES - 1
                first = isinstance(i, int) and i == 0
                if not last:
                    evac_x(i + 1, 1 - par)
                if first:
                    ends = place()
                gating(i, par)
                if late is not None and not (isinstance(late, int) and late == 0):
                    add_routed(late - 1, 1)
                if not last:
                    split_u(i + 1, 1 - par)
                if early is not None:
                    v.wait_ge(ys_in[par], 16 * (half - SH_A // 2 + 1))
                    add_shared(early, ys[:, par, :])
                down_out(i, par, stored)
                if first:
                    tables(ends)
                if late is not None:
                    for t in range(2):
                        v.wait_ge(S["y_ready"], 2 * i + t + 1)
                        add_shared(EARLY + 2 * late + t, yb[:, par, t, :])
                    add_routed(late, 0)
            for par in range(2):
                tile(0, par, 0)
            with v.Fori(1, SH_A // 2 - 1) as h:
                for par in range(2):
                    tile(h, par, h)
            v.wait_ge(S["idT"], 1)
            v.tensor_copy(idx[:, :], PS[2][:, 0, 0:R_COLS]).then_inc(S["idx_ready"], 1)
            for par in range(2):
                tile(SH_A // 2 - 1, par, SH_A // 2 - 1)
            with v.Fori(SH_A // 2, (SH_A + EARLY) // 2) as h:
                for par in range(2):
                    tile(h, par, h, early=2 * h + par - SH_A)
            with v.Fori((SH_A + EARLY) // 2, SH_B0 // 2) as h:
                for par in range(2):
                    tile(h, par, h)
            for par in range(2):
                tile(SH_B0 // 2, par, SH_B0 // 2, late=par)
            with v.Fori(SH_B0 // 2 + 1, N_TILES // 2 - 1) as h:
                for par in range(2):
                    tile(h, par, SH_B0 // 2, late=2 * h + par - SH_B0)
            for par in range(2):
                tile(N_TILES // 2 - 1, par, SH_B0 // 2, late=N_TILES - 2 + par - SH_B0)
            add_routed(NB // 4 - 1, 1)

        @block.tensor
        def _(pe):
            pe.wait_ge(S["id_ready"], 4)
            pe.wait_ge(S["vone"], 10)

            def tr_k(half, par, quad):
                b = 2 * half + par
                pe.wait_ge(S["k_split"], b + 1)
                need(pe, S["qT1_ready"], b)
                for kv in range(NKV):
                    ins = pe.transpose(Rb16[0][:, kv, :], kcat[:, quad, kv, :, :, :].rearrange("p o r d -> p (o r d)"), id16[:, :])
                ins.then_inc(S["tk_done"], 1)

            def tr_q(half, par, part):
                b = 2 * half + par
                if part == 0:
                    pe.wait_ge(S["q_split"], b + 1)
                    need(pe, S["qT0_ready"], b)
                else:
                    pe.wait_ge(S["kT_ready"], b + 1)
                for j in range(BLK // 2):
                    blk = part * BLK // 2 + j
                    ins = pe.transpose(Rb16[1 - part][:, j, :], qcat[:, par, 2 * blk:2 * blk + 2, :, :].rearrange("p h r d -> p (h r d)"), id16[:, :])
                ins.then_inc(S["tq1_done"] if part else S["tq0_done"], 1)

            def scores_max(half, par, u, odd):
                b = 2 * half + par
                if u == 0:
                    pe.wait_ge(S["kT_ready"], b + 1)
                    pe.wait_ge(S["qT0_ready"], b + 1)
                if u == 2:
                    pe.wait_ge(S["qT1_ready"], b + 1)
                need(pe, S["max_done"], 2 * (UNITS * b + u) + odd - 1)
                rows = slice(64 * odd, 64 * odd + 3 * D)
                for j in range(HPU // 2):
                    ins = pe.matmul(Mb[:, odd, j * P:(j + 1) * P], qT[rows, par, 4 * u + j, :], kT[rows, par, 2 * u + j // 2, :],
                                    start=True, stop=True)
                ins.then_inc(S["m_done"], 1)

            def scores_T(half, par, u, odd):
                b = number(half, par)
                pe.wait_ge(neg_in[u // 2], 16 * (b + 1))
                need(pe, S["exp_done"], 2 * (UNITS * b + u) + odd - 1)
                rows = slice(64 * odd, 64 * odd + 3 * D + 1)
                for kv in range(2):
                    ins = pe.matmul(Tb[:, odd, kv * 256:(kv + 1) * 256], kT[rows, par, 2 * u + kv, :],
                                    qT[rows, par, 4 * u + 2 * kv:4 * u + 2 * kv + 2, :].rearrange("p n c -> p (n c)"),
                                    start=True, stop=True)
                ins.then_inc(S["t_done"], 1)

            def step(half, par, u, nxt):
                for odd in range(2):
                    if nxt is not None:
                        scores_max(*nxt, odd)
                    scores_T(half, par, u, odd)

            def outputs(half, par, quad, u):
                b = 2 * half + par
                pe.wait_ge(S["plo_g"] if u % 2 else S["plo_v"], 2 * b + u // 2 + 1)
                if u % 2 == 0:
                    need(pe, S["att_ready"], 2 * (b - 1) + u // 2 + 1)
                    if u == 0 or not (isinstance(half, int) and b == NB - 1):
                        pe.wait_ge(S["negT_ready"], 2 * b + 2 + u // 2)
                for j in range(HPU // 2):
                    for odd in range(2):
                        c = (u % 2) * HPU + 2 * j + odd
                        head = odd * 4 + j
                        kv = kcat[:, quad, 2 * u + j // 2, 0, :, :].rearrange("p r d -> p (r d)")
                        o = Ob[:, u // 2, c * (D + 1):(c + 1) * (D + 1)]
                        pe.matmul(o, Ps[:, u, 0, head, :], kv[:, 2 * D:3 * D + 1], start=True, stop=False)
                        pe.matmul(o[:, 0:D], Ps[:, u, 0, head, :], kv[:, D:2 * D], start=False, stop=False)
                        ins = pe.matmul(o, Ps[:, u, 1, head, :], kv[:, 2 * D:3 * D + 1], start=False, stop=True)
                ins.then_inc(S["pv_done"], 1)

            def tr_neg(half, par, pair):
                b = number(half, par)
                pe.wait_ge(S["max_done"], 2 * (UNITS * b + 2 * pair + 2))
                need(pe, S["att_ready"], 2 * b - 2 + pair)
                pe.transpose(NT[pair], negm[:, pair, :, :].rearrange("p o j -> p (o j)"), id16[:, :]).then_inc(S["negx_done"], 1)

            tr_k(0, 0, 0)
            tr_q(0, 0, 0)
            tr_q(0, 0, 1)
            for u in range(3):
                for odd in range(2):
                    scores_max(0, 0, u, odd)
                if u == 1:
                    tr_neg(0, 0, 0)

            def body(half, par, quad):
                nx = follow(half, par, quad, 1)
                if nx is not None:
                    tr_k(*nx)
                    tr_q(*nx[:2], 0)
                start = isinstance(half, int) and number(half, par) == 0
                pv = (*((half - 1, 1) if par == 0 else (half, 0)), (quad - 1) % 4)
                step(half, par, 0, (half, par, 3))
                if not start:
                    outputs(*pv, 2)
                tr_neg(half, par, 1)
                step(half, par, 1, nx and (*nx[:2], 0))
                if not start:
                    outputs(*pv, 3)
                if nx is not None:
                    tr_q(*nx[:2], 1)
                step(half, par, 2, nx and (*nx[:2], 1))
                outputs(half, par, quad, 0)
                if nx is not None:
                    tr_neg(*nx[:2], 0)
                step(half, par, 3, nx and (*nx[:2], 2))
                outputs(half, par, quad, 1)
            over_batches(pe, body)
            for u in range(2, UNITS):
                outputs(NB // 2 - 1, 1, NB % 4 + 3, u)

            def tr_x2(b, k):
                pe.wait_ge(S["x2l_ready"], b + 1)
                need(pe, S["x2T_ready"], b - 1)
                for n in range(2 * KT):
                    ins = pe.transpose(Rb16[k % 2][:, n, :], xhl[:, k, n // KT, (n % KT) * P:(n % KT + 1) * P], id16[:, :])
                ins.then_inc(S["t2_done"], 1)

            def gates(b, k):
                pe.wait_ge(S["x2T_ready"], b + 1)
                terms = [(xh, wh, kt) for xh, wh in ((0, 0), (0, 1), (1, 0)) for kt in range(KT)]
                for n, (xh, wh, kt) in enumerate(terms):
                    ins = pe.matmul(PS[0][:, 0, bass.ds(b * 8, E_R)], xhT[:, k % 2, xh * KT + kt, :], wrs[:, wh, kt, :],
                                    start=(n == 0), stop=(n == len(terms) - 1))
                ins.then_inc(S["gate_done"], 1)
            pe.wait_ge(S["qT1_ready"], NB)
            pe.wait_ge(S["qT0_ready"], NB)
            pe.wait_ge(S["wrs_ready"], 2)
            pe.wait_ge(S["max_done"], 2 * UNITS * NB)
            tr_x2(0, 0)

            def four(i, last):
                for k in range(4):
                    if not (last and k == 3):
                        tr_x2(4 * i + k + 1, (k + 1) % 4)
                    gates(4 * i + k, k)
            four(0, False)
            with pe.Fori(1, NB // 4 - 1) as i:
                four(i, False)
            four(NB // 4 - 1, True)
            pe.wait_ge(S["exp_done"], 2 * UNITS * NB)
            pe.wait_ge(S["att_ready"], 2 * NB)

            def ranks():
                pe.wait_ge(S["rt_mask"], 1)
                pe.wait_ge(S["x2T_ready"], NB)
                mv = msum[:, :, :].rearrange("p b e -> p (b e)")
                pe.matmul(PS[2][:, 0, 0:NB * 8], tri[:, :], mv, start=True, stop=True).then_inc(S["rt_cnt"], 1)
                pe.matmul(PS[2][:, 1, 0:NB * 8], one16[:, :], mv, start=True, stop=True).then_inc(S["rt_cnt"], 1)

            def tr_x(i, par, come):
                pe.wait_ge(come[0][par], come[1])
                for t in range(2):
                    need(pe, S["xTv_ready"] if t else S["xTa_ready"], i)
                    src = PS[3][:, t, :].bitcast(F16).rearrange("p (n c) -> p n c", c=P)
                    for n in range(2 * KT):
                        ins = pe.transpose(src[:, n, :], xs[:, par, t, n * P:(n + 1) * P], id16[:, :])
                    ins.then_inc(S["xt_done"], 1)

            TERMS = [(w, x, k) for w, x in ((0, 0), (0, 1), (1, 0)) for k in range(KT)]

            def feature_layer(l, bank, rhs, i, par, n_loads, free, done):
                pe.wait_ge(wl_in[l][par], 16 * n_loads)
                for hf in range(2):
                    need(pe, free, 2 * i - 1 + hf)
                    for m in range(2 * hf, 2 * hf + 2):
                        for n, (w, x, k) in enumerate(TERMS):
                            ins = pe.matmul(bank[:, hf, (m % 2) * TT:(m % 2 + 1) * TT], wb[:, par, l, k, w, m * P:(m + 1) * P],
                                            rhs(x, k), start=(n == 0), stop=(n == len(TERMS) - 1))
                    ins.then_inc(done, 1)

            def up(i, par, n_loads):
                pe.wait_ge(S["xTa_ready"], i + 1)
                pe.wait_ge(S["xTv_ready"], i + 1)
                feature_layer(0, PS[0], lambda x, k: xT[:, par, x, k, :], i, par, n_loads, S["u_ready"], S["l1_done"])

            def gate_l(i, par, n_loads):
                pe.wait_ge(S["ul_ready"], 2 * i + 2)
                feature_layer(1, PS[1], lambda x, k: uhl[:, x, k, :], i, par, n_loads, S["s_ready"], S["l2_done"])

            def down(i, par, n_loads):
                pe.wait_ge(wl_in[2][par], 16 * n_loads)
                pe.wait_ge(S["gl_ready"], 2 * i + 2)
                for t in range(2):
                    need(pe, S["y_ready"], 2 * i - 1 + t)
                    for n, (w, x, k) in enumerate(TERMS):
                        ins = pe.matmul(PS[2][:, t, :], ghl[:, x, k, t * P:(t + 1) * P], wb[:, par, 2, k, w, :],
                                        start=(n == 0), stop=(n == len(TERMS) - 1))
                    ins.then_inc(S["l3_done"], 1)

            tr_x(0, 0, tokens(0))
            pe.wait_ge(S["lg_read"], 1)
            up(0, 0, 1)

            def tile(half, par, loads_of, tokens_of):
                i = 2 * half + par
                last = isinstance(i, int) and i == N_TILES - 1
                if isinstance(i, int) and i == SH_A - 2:
                    pe.wait_ge(S["id_load"], 16)
                    pe.wait_ge(S["y_ready"], 2 * i)
                    pe.transpose(PS[2][:, 0, 0:R_COLS], idr[:, :], id32[0:R_COLS, 0:R_COLS]).then_inc(S["idT"], 1)
                if not last:
                    tr_x(i + 1, 1 - par, tokens_of(half + par))
                if isinstance(i, int) and i == 0:
                    ranks()
                gate_l(i, par, loads_of(half))
                if not last:
                    up(i + 1, 1 - par, loads_of(half + par))
                if isinstance(i, int) and i == SH_A - 2:
                    pe.wait_ge(S["idx_ready"], 3)
                if isinstance(i, int) and i == 0:
                    pe.wait_ge(S["rnk_read"], 1)
                down(i, par, loads_of(half))
            for lo, hi, *of in over_tiles(tile):
                with pe.Fori(lo, hi) as h:
                    tile(h, 0, *of)
                    tile(h, 1, *of)


def kernel(x, ctx_512, g_xattn, g_ffn, L0_ffn_Wr, L0_ffn_br, L0_ffn_gate_bias, L0_ffn_Wup, L0_ffn_bup, L0_ffn_Wgate,
           L0_ffn_bgate, L0_ffn_Wdown, L0_ffn_bdown, L0_ffn_Wsu, L0_ffn_bsu, L0_ffn_Wsg, L0_ffn_bsg, L0_ffn_Wsd, L0_ffn_bsd):
    import concourse.bacc as _bacc
    from concourse import mybir as _mybir
    from concourse.bass_utils import run_bass_kernel_spmd as _run

    def joined(routed, shared):
        return np.concatenate([np.asarray(routed), np.asarray(shared)[None]], axis=0)

    layers = [joined(L0_ffn_Wup, L0_ffn_Wsu), joined(L0_ffn_Wgate, L0_ffn_Wsg), joined(L0_ffn_Wdown, L0_ffn_Wsd)]
    wall = np.stack([w.reshape(E_ALL * KT, P, HID) for w in layers], axis=2)
    cols = np.stack([joined(L0_ffn_bup, L0_ffn_bsu), joined(L0_ffn_bgate, L0_ffn_bsg)], axis=1)
    bcol = cols.reshape(E_ALL, 2 * KT, P).transpose(0, 2, 1)
    given = {
        "x": x, "ctx": ctx_512, "g_xattn": g_xattn, "g_ffn": g_ffn, "wr": L0_ffn_Wr, "br": L0_ffn_br, "gbias": L0_ffn_gate_bias,
        "wall": wall, "bcol": bcol, "bdown": joined(L0_ffn_bdown, L0_ffn_bsd),
    }
    nc = _bacc.Bacc("TRN2", target_bir_lowering=False, num_devices=1)
    arrays, args = {}, {}
    for name, value in given.items():
        v = np.ascontiguousarray(value)
        arrays[f"in_{name}"] = v
        args[name] = nc.dram_tensor(f"in_{name}", v.shape, _mybir.dt.from_np(v.dtype), kind="ExternalInput").ap()
    out = nc.dram_tensor("out_0", (NB, P, HID), _mybir.dt.float32, kind="ExternalOutput").ap()
    program(nc, args, out)
    r = _run(nc, [arrays], core_ids=[0])
    return r.results[0]["out_0"]
```
